# Optimizing a Trainium2 kernel written in Bass

```python
import numpy as np
import jax
import jax.numpy as jnp

def _softmax(x, axis=-1):
    return jax.nn.softmax(x, axis=axis)

def _gelu(x):
    return jax.nn.gelu(x, approximate=True)

def _silu(x):
    return jax.nn.silu(x)

def _sigmoid(x):
    return jax.nn.sigmoid(x)

def _layernorm(x, axis=-1, eps=1e-05):
    m = jnp.mean(x, axis=axis, keepdims=True)
    v = jnp.var(x, axis=axis, keepdims=True)
    return (x - m) / jnp.sqrt(v + eps)

def _scatter_add(tgt, idx, src, axis=0):
    return tgt.at[idx].add(src)

def _segment_sum(src, seg, n):
    return jax.ops.segment_sum(src, seg, n)
kernel_name = 'mk_prb_d4_jaxref_r8_b40d29'

def setup_inputs(seed: int=0):
    np.random.seed(seed)
    _w = jnp.asarray

    def _L0_attn_setup():
        import jax, jax.numpy as jnp
        import numpy as np
        B, S, D = (4, 512, 128)
        H = 16
        HD = D // H

        def feature_map(x):
            return jnp.exp(-jnp.square(x) * 0.5)
        key = jax.random.key(seed)
        ks = jax.random.split(key, 9)
        s = 1.0 / np.sqrt(D)
        return {'x': jax.random.normal(ks[0], (B, S, D), dtype=jnp.float32), 'Wq': jax.random.normal(ks[1], (D, D), dtype=jnp.float32) * s, 'bq': jax.random.normal(ks[2], (D,), dtype=jnp.float32) * s, 'Wk': jax.random.normal(ks[3], (D, D), dtype=jnp.float32) * s, 'bk': jax.random.normal(ks[4], (D,), dtype=jnp.float32) * s, 'Wv': jax.random.normal(ks[5], (D, D), dtype=jnp.float32) * s, 'bv': jax.random.normal(ks[6], (D,), dtype=jnp.float32) * s, 'Wo': jax.random.normal(ks[7], (D, D), dtype=jnp.float32) * s, 'bo': jax.random.normal(ks[8], (D,), dtype=jnp.float32) * s}
    _L0_attn_in = _L0_attn_setup()

    def _L0_ffn_setup():
        import jax, jax.numpy as jnp
        import numpy as np
        THRESH_FACTOR = 0.7

        def ternary_quantize(w):
            delta = THRESH_FACTOR * jnp.mean(jnp.abs(w))
            return jnp.where(w > delta, 1.0, jnp.where(w < -delta, -1.0, 0.0)).astype(w.dtype)
        key = jax.random.key(seed)
        k1, k2, k3 = jax.random.split(key, 3)
        B, S, D_IN, D_OUT = (8, 512, 128, 128)
        inp = {'input': jax.random.normal(k1, (B, S, D_IN), dtype=jnp.float32), 'weight': jax.random.normal(k2, (D_OUT, D_IN), dtype=jnp.float32) * (1.0 / np.sqrt(D_IN)), 'alpha': jnp.ones((1,), dtype=jnp.float32), 'bias': jax.random.normal(k3, (D_OUT,), dtype=jnp.float32) * (1.0 / np.sqrt(D_IN))}
        return inp
    _L0_ffn_in = _L0_ffn_setup()

    def _L1_attn_setup():
        import jax, jax.numpy as jnp
        import numpy as np
        EPS = 1e-06

        def _rmsnorm(x, scale):
            var = jnp.mean(jnp.square(x), axis=-1, keepdims=True)
            return x * jax.lax.rsqrt(var + EPS) * scale
        key = jax.random.key(seed)
        ks = jax.random.split(key, 6)
        B, S, D, H, Dh = (2, 256, 128, 16, 64)
        x = jax.random.normal(ks[0], (B, S, D), dtype=jnp.float32)
        norm_scale = jnp.ones((D,), dtype=jnp.float32)
        wq = jax.random.normal(ks[1], (D, H, Dh), dtype=jnp.float32) / np.sqrt(D)
        wk = jax.random.normal(ks[2], (D, H, Dh), dtype=jnp.float32) / np.sqrt(D)
        wv = jax.random.normal(ks[3], (D, H, Dh), dtype=jnp.float32) / np.sqrt(D)
        w_out = jax.random.normal(ks[4], (H, Dh, D), dtype=jnp.float32) / np.sqrt(H * Dh)
        b_out = jnp.zeros((D,), dtype=jnp.float32)
        return {'x': x, 'norm_scale': norm_scale, 'wq': wq, 'wk': wk, 'wv': wv, 'w_out': w_out, 'b_out': b_out}
    _L1_attn_in = _L1_attn_setup()

    def _L1_ffn_setup():
        import jax, jax.numpy as jnp
        import numpy as np
        HIDDEN = 128
        FFN = 512
        NUM_EXPERTS = 8
        TOP_K = 2
        BATCH, SEQ = (2, 256)
        key = jax.random.key(seed)
        ks = jax.random.split(key, 6)
        s_h = 1.0 / np.sqrt(HIDDEN)
        s_f = 1.0 / np.sqrt(FFN)
        return {'hidden_states': jax.random.normal(ks[0], (BATCH, SEQ, HIDDEN), jnp.float32), 'gate_w': jax.random.uniform(ks[1], (HIDDEN, NUM_EXPERTS), jnp.float32, -s_h, s_h), 'gate_b': jax.random.uniform(ks[2], (NUM_EXPERTS,), jnp.float32, -s_h, s_h), 'w1': jax.random.uniform(ks[3], (NUM_EXPERTS, HIDDEN, FFN), jnp.float32, -s_h, s_h), 'w3': jax.random.uniform(ks[4], (NUM_EXPERTS, HIDDEN, FFN), jnp.float32, -s_h, s_h), 'w2': jax.random.uniform(ks[5], (NUM_EXPERTS, FFN, HIDDEN), jnp.float32, -s_f, s_f)}
    _L1_ffn_in = _L1_ffn_setup()

    def _L2_attn_setup():
        import jax, jax.numpy as jnp
        import numpy as np
        import math
        D_MODEL = 128
        NUM_HEADS = 16
        HEAD_DIM = D_MODEL // NUM_HEADS
        key = jax.random.key(seed)
        k_x, k_qkv, k_o = jax.random.split(key, 3)
        B, S = (2, 256)
        x = jax.random.normal(k_x, (B, S, D_MODEL), dtype=jnp.float32)
        sigma_qkv = math.sqrt(2.0 / (D_MODEL + 3 * D_MODEL))
        w_qkv = jax.random.truncated_normal(k_qkv, -3.0, 3.0, (3 * D_MODEL, D_MODEL), dtype=jnp.float32) * sigma_qkv
        sigma_o = math.sqrt(2.0 / (D_MODEL + D_MODEL))
        w_out = jax.random.truncated_normal(k_o, -3.0, 3.0, (D_MODEL, D_MODEL), dtype=jnp.float32) * sigma_o
        return {'x': x, 'w_qkv': w_qkv, 'w_out': w_out}
    _L2_attn_in = _L2_attn_setup()

    def _L2_ffn_setup():
        import jax, jax.numpy as jnp
        import numpy as np
        B, S, D, F, E = (4, 256, 128, 512, 8)
        LN_EPS = 1e-05
        key = jax.random.key(seed)
        ks = jax.random.split(key, 6)
        sc = 0.02
        return {'x': jax.random.normal(ks[0], (B, S, D), dtype=jnp.float32), 'Wr': jax.random.normal(ks[1], (D, E), dtype=jnp.float32) * sc, 'br': jnp.zeros((E,), jnp.float32), 'ln_g': jnp.ones((D,), jnp.float32), 'ln_b': jnp.zeros((D,), jnp.float32), 'W1': jax.random.normal(ks[2], (E, D, F), dtype=jnp.float32) * sc, 'b1': jnp.zeros((E, F), jnp.float32), 'W2': jax.random.normal(ks[3], (E, F, D), dtype=jnp.float32) * sc, 'b2': jnp.zeros((E, D), jnp.float32)}
    _L2_ffn_in = _L2_ffn_setup()

    def _L3_attn_setup():
        import jax, jax.numpy as jnp
        import numpy as np
        import math
        D_MODEL, D_C, D_R, NH = (128, 128, 32, 16)
        HD = D_MODEL // NH
        B, T = (2, 256)

        def _rope_tables(T, d_R):
            inv_freq = 1.0 / 10000.0 ** (jnp.arange(0, d_R, 2, dtype=jnp.float32) / d_R)
            t = jnp.arange(T, dtype=jnp.float32)
            freqs = jnp.outer(t, inv_freq)
            return (jnp.cos(freqs), jnp.sin(freqs))

        def _rotary_apply(x, cos, sin):
            d = x.shape[-1]
            x1, x2 = (x[..., :d // 2], x[..., d // 2:])
            return jnp.concatenate([x1 * cos - x2 * sin, x2 * cos + x1 * sin], axis=-1)
        key = jax.random.key(seed)
        ks = jax.random.split(key, 8)
        s = lambda fan_in: 1.0 / math.sqrt(fan_in)
        return {'x': jax.random.normal(ks[0], (B, T, D_MODEL), jnp.float32), 'W_kv_down': jax.random.normal(ks[1], (D_MODEL, D_C), jnp.float32) * s(D_MODEL), 'W_k_up': jax.random.normal(ks[2], (D_C, D_MODEL), jnp.float32) * s(D_C), 'W_v_up': jax.random.normal(ks[3], (D_C, D_MODEL), jnp.float32) * s(D_C), 'W_q': jax.random.normal(ks[4], (D_MODEL, D_MODEL), jnp.float32) * s(D_MODEL), 'W_q_rope': jax.random.normal(ks[5], (D_MODEL, D_R), jnp.float32) * s(D_MODEL), 'W_k_rope': jax.random.normal(ks[6], (D_C, D_R), jnp.float32) * s(D_C), 'W_o': jax.random.normal(ks[7], (D_MODEL, D_MODEL), jnp.float32) * s(D_MODEL)}
    _L3_attn_in = _L3_attn_setup()

    def _L3_ffn_setup():
        import jax, jax.numpy as jnp
        import numpy as np
        B, S, DIM = (4, 256, 128)
        E, K, HID = (8, 2, 512)
        key = jax.random.key(seed)
        ks = jax.random.split(key, 8)
        init = lambda k, sh: jax.random.normal(k, sh, jnp.float32) * 0.02
        return {'x': jax.random.normal(ks[0], (B, S, DIM), jnp.float32), 'gate_w': init(ks[1], (DIM, E)), 'gate_b': jnp.zeros((E,), jnp.float32), 'w1': init(ks[2], (E, DIM, HID)), 'b1': jnp.zeros((E, HID), jnp.float32), 'w2': init(ks[3], (E, HID, DIM)), 'b2': jnp.zeros((E, DIM), jnp.float32), 'ws1': init(ks[4], (DIM, HID)), 'bs1': jnp.zeros((HID,), jnp.float32), 'ws2': init(ks[5], (HID, DIM)), 'bs2': jnp.zeros((DIM,), jnp.float32)}
    _L3_ffn_in = _L3_ffn_setup()
    _d = {'L0_attn_x': _L0_attn_in['x'], 'L0_attn_Wq': _L0_attn_in['Wq'], 'L0_attn_bq': _L0_attn_in['bq'], 'L0_attn_Wk': _L0_attn_in['Wk'], 'L0_attn_bk': _L0_attn_in['bk'], 'L0_attn_Wv': _L0_attn_in['Wv'], 'L0_attn_bv': _L0_attn_in['bv'], 'L0_attn_Wo': _L0_attn_in['Wo'], 'L0_attn_bo': _L0_attn_in['bo'], 'L0_ffn_weight': _L0_ffn_in['weight'], 'L0_ffn_alpha': _L0_ffn_in['alpha'], 'L0_ffn_bias': _L0_ffn_in['bias'], 'L1_attn_norm_scale': _L1_attn_in['norm_scale'], 'L1_attn_wq': _L1_attn_in['wq'], 'L1_attn_wk': _L1_attn_in['wk'], 'L1_attn_wv': _L1_attn_in['wv'], 'L1_attn_w_out': _L1_attn_in['w_out'], 'L1_attn_b_out': _L1_attn_in['b_out'], 'L1_ffn_gate_w': _L1_ffn_in['gate_w'], 'L1_ffn_gate_b': _L1_ffn_in['gate_b'], 'L1_ffn_w1': _L1_ffn_in['w1'], 'L1_ffn_w3': _L1_ffn_in['w3'], 'L1_ffn_w2': _L1_ffn_in['w2'], 'L2_attn_w_qkv': _L2_attn_in['w_qkv'], 'L2_attn_w_out': _L2_attn_in['w_out'], 'L2_ffn_Wr': _L2_ffn_in['Wr'], 'L2_ffn_br': _L2_ffn_in['br'], 'L2_ffn_ln_g': _L2_ffn_in['ln_g'], 'L2_ffn_ln_b': _L2_ffn_in['ln_b'], 'L2_ffn_W1': _L2_ffn_in['W1'], 'L2_ffn_b1': _L2_ffn_in['b1'], 'L2_ffn_W2': _L2_ffn_in['W2'], 'L2_ffn_b2': _L2_ffn_in['b2'], 'L3_attn_W_kv_down': _L3_attn_in['W_kv_down'], 'L3_attn_W_k_up': _L3_attn_in['W_k_up'], 'L3_attn_W_v_up': _L3_attn_in['W_v_up'], 'L3_attn_W_q': _L3_attn_in['W_q'], 'L3_attn_W_q_rope': _L3_attn_in['W_q_rope'], 'L3_attn_W_k_rope': _L3_attn_in['W_k_rope'], 'L3_attn_W_o': _L3_attn_in['W_o'], 'L3_ffn_gate_w': _L3_ffn_in['gate_w'], 'L3_ffn_gate_b': _L3_ffn_in['gate_b'], 'L3_ffn_w1': _L3_ffn_in['w1'], 'L3_ffn_b1': _L3_ffn_in['b1'], 'L3_ffn_w2': _L3_ffn_in['w2'], 'L3_ffn_b2': _L3_ffn_in['b2'], 'L3_ffn_ws1': _L3_ffn_in['ws1'], 'L3_ffn_bs1': _L3_ffn_in['bs1'], 'L3_ffn_ws2': _L3_ffn_in['ws2'], 'L3_ffn_bs2': _L3_ffn_in['bs2']}
    _x0 = _d['L0_attn_x']
    _d['L0_attn_x'] = jax.random.normal(jax.random.fold_in(jax.random.key(seed), 1), (16, 256, 128), dtype=_x0.dtype)
    del _x0
    return _d

def reference(L0_attn_x, L0_attn_Wq, L0_attn_bq, L0_attn_Wk, L0_attn_bk, L0_attn_Wv, L0_attn_bv, L0_attn_Wo, L0_attn_bo, L0_ffn_weight, L0_ffn_alpha, L0_ffn_bias, L1_attn_norm_scale, L1_attn_wq, L1_attn_wk, L1_attn_wv, L1_attn_w_out, L1_attn_b_out, L1_ffn_gate_w, L1_ffn_gate_b, L1_ffn_w1, L1_ffn_w3, L1_ffn_w2, L2_attn_w_qkv, L2_attn_w_out, L2_ffn_Wr, L2_ffn_br, L2_ffn_ln_g, L2_ffn_ln_b, L2_ffn_W1, L2_ffn_b1, L2_ffn_W2, L2_ffn_b2, L3_attn_W_kv_down, L3_attn_W_k_up, L3_attn_W_v_up, L3_attn_W_q, L3_attn_W_q_rope, L3_attn_W_k_rope, L3_attn_W_o, L3_ffn_gate_w, L3_ffn_gate_b, L3_ffn_w1, L3_ffn_b1, L3_ffn_w2, L3_ffn_b2, L3_ffn_ws1, L3_ffn_bs1, L3_ffn_ws2, L3_ffn_bs2):

    def _L0_attn_ref(x, Wq, bq, Wk, bk, Wv, bv, Wo, bo):
        import jax, jax.numpy as jnp
        import numpy as np
        B, S, D = (4, 512, 128)
        H = 16
        HD = D // H

        def feature_map(x):
            return jnp.exp(-jnp.square(x) * 0.5)
        b, s, _ = x.shape
        q = feature_map((x @ Wq + bq).reshape(b, s, H, HD))
        k = feature_map((x @ Wk + bk).reshape(b, s, H, HD))
        v = (x @ Wv + bv).reshape(b, s, H, HD)
        coeff = jnp.sum(q * k, axis=-1, keepdims=True)
        qkv = coeff * v
        out = qkv.reshape(b, s, H * HD)
        return out @ Wo + bo

    def _L0_ffn_ref(input, weight, alpha, bias):
        import jax, jax.numpy as jnp
        import numpy as np
        THRESH_FACTOR = 0.7

        def ternary_quantize(w):
            delta = THRESH_FACTOR * jnp.mean(jnp.abs(w))
            return jnp.where(w > delta, 1.0, jnp.where(w < -delta, -1.0, 0.0)).astype(w.dtype)
        w_ternary = ternary_quantize(weight)
        w_eff = w_ternary * alpha
        out = jnp.einsum('bsd,od->bso', input, w_eff) + bias
        return out

    def _L1_attn_ref(x, norm_scale, wq, wk, wv, w_out, b_out):
        import jax, jax.numpy as jnp
        import numpy as np
        EPS = 1e-06

        def _rmsnorm(x, scale):
            var = jnp.mean(jnp.square(x), axis=-1, keepdims=True)
            return x * jax.lax.rsqrt(var + EPS) * scale
        dtype = x.dtype
        softmax_dtype = jnp.float32
        h = _rmsnorm(x, norm_scale)
        q = jnp.einsum('bsd,dhe->bshe', h, wq)
        k = jnp.einsum('bsd,dhe->bshe', h, wk)
        v = jnp.einsum('bsd,dhe->bshe', h, wv)
        head_dim = q.shape[-1]
        scale = head_dim ** (-0.5)
        q = (q * scale).astype(softmax_dtype)
        kf = k.astype(softmax_dtype)
        weights = jnp.einsum('bqhd,bkhd->bhqk', q, kf)
        weights = jax.nn.softmax(weights, axis=-1).astype(dtype)
        new_vals = jnp.einsum('bhqk,bkhd->bqhd', weights, v).astype(dtype)
        out = jnp.einsum('bqhe,hed->bqd', new_vals, w_out) + b_out
        return out

    def _L1_ffn_ref(hidden_states, gate_w, gate_b, w1, w3, w2):
        import jax, jax.numpy as jnp
        import numpy as np
        HIDDEN = 128
        FFN = 512
        NUM_EXPERTS = 8
        TOP_K = 2
        BATCH, SEQ = (2, 256)
        B, S, D = hidden_states.shape
        T = B * S
        x = hidden_states.reshape(T, D)
        logits = x @ gate_w + gate_b
        probs = jax.nn.softmax(logits.astype(jnp.float32), axis=-1)
        top_w, top_idx = jax.lax.top_k(probs, TOP_K)
        top_w = top_w / jnp.sum(top_w, axis=-1, keepdims=True)
        combine = jnp.zeros((T, NUM_EXPERTS), jnp.float32)
        combine = combine.at[jnp.arange(T)[:, None], top_idx].set(top_w)
        combine = combine.astype(x.dtype)
        h = jax.nn.silu(jnp.einsum('td,edf->tef', x, w1)) * jnp.einsum('td,edf->tef', x, w3)
        out_e = jnp.einsum('tef,efd->ted', h, w2)
        out = jnp.einsum('ted,te->td', out_e, combine)
        return out.reshape(B, S, D)

    def _L2_attn_ref(x, w_qkv, w_out):
        import jax, jax.numpy as jnp
        import numpy as np
        import math
        D_MODEL = 128
        NUM_HEADS = 16
        HEAD_DIM = D_MODEL // NUM_HEADS
        B, S, _ = x.shape
        qkv = jnp.einsum('bsi,oi->bso', x, w_qkv)
        q, k, v = jnp.split(qkv, 3, axis=-1)

        def to_heads(t):
            return t.reshape(B, S, NUM_HEADS, HEAD_DIM).transpose(0, 2, 1, 3)
        q, k, v = (to_heads(q), to_heads(k), to_heads(v))
        scale = 1.0 / math.sqrt(HEAD_DIM)
        logits = jnp.einsum('bhsd,bhtd->bhst', q, k) * scale
        mask = jnp.tril(jnp.ones((S, S), dtype=bool))
        neg_inf = jnp.finfo(jnp.float32).min
        logits = jnp.where(mask, logits, neg_inf)
        probs = jax.nn.softmax(logits, axis=-1)
        probs = probs * mask.astype(probs.dtype)
        out = jnp.einsum('bhst,bhtd->bhsd', probs, v)
        out = out.transpose(0, 2, 1, 3).reshape(B, S, D_MODEL)
        return jnp.einsum('bsi,oi->bso', out, w_out)

    def _L2_ffn_ref(x, Wr, br, ln_g, ln_b, W1, b1, W2, b2):
        import jax, jax.numpy as jnp
        import numpy as np
        B, S, D, F, E = (4, 256, 128, 512, 8)
        LN_EPS = 1e-05
        tokens_shape = x.shape[:-1]
        xt = x.reshape(-1, x.shape[-1])
        router_logits = xt @ Wr + br
        router_probs = jax.nn.softmax(router_logits, axis=-1)
        gates = jnp.max(router_probs, axis=-1, keepdims=True)
        idx = jnp.argmax(router_probs, axis=-1)
        onehot = jax.nn.one_hot(idx, E, dtype=xt.dtype)
        mu = jnp.mean(xt, axis=-1, keepdims=True)
        var = jnp.mean(jnp.square(xt - mu), axis=-1, keepdims=True)
        xn = (xt - mu) * jax.lax.rsqrt(var + LN_EPS) * ln_g + ln_b
        h = jnp.einsum('te,td,edf->tf', onehot, xn, W1) + b1[idx]
        h = jax.nn.relu(h)
        y = jnp.einsum('te,tf,efd->td', onehot, h, W2) + b2[idx]
        y = y * gates
        return y.reshape(tokens_shape + (y.shape[-1],))

    def _L3_attn_ref(x, W_kv_down, W_k_up, W_v_up, W_q, W_q_rope, W_k_rope, W_o):
        import jax, jax.numpy as jnp
        import numpy as np
        import math
        D_MODEL, D_C, D_R, NH = (128, 128, 32, 16)
        HD = D_MODEL // NH
        B, T = (2, 256)

        def _rope_tables(T, d_R):
            inv_freq = 1.0 / 10000.0 ** (jnp.arange(0, d_R, 2, dtype=jnp.float32) / d_R)
            t = jnp.arange(T, dtype=jnp.float32)
            freqs = jnp.outer(t, inv_freq)
            return (jnp.cos(freqs), jnp.sin(freqs))

        def _rotary_apply(x, cos, sin):
            d = x.shape[-1]
            x1, x2 = (x[..., :d // 2], x[..., d // 2:])
            return jnp.concatenate([x1 * cos - x2 * sin, x2 * cos + x1 * sin], axis=-1)
        Bb, Tt, _ = x.shape
        cos, sin = _rope_tables(Tt, D_R)
        cos = cos[None]
        sin = sin[None]
        c_kv = x @ W_kv_down
        k_rope = _rotary_apply(c_kv @ W_k_rope, cos, sin)
        k = (c_kv @ W_k_up).reshape(Bb, Tt, NH, HD)
        v = (c_kv @ W_v_up).reshape(Bb, Tt, NH, HD)
        q = (x @ W_q).reshape(Bb, Tt, NH, HD)
        q_rope = _rotary_apply(x @ W_q_rope, cos, sin)
        scale = math.sqrt(HD + D_R)
        scores = jnp.einsum('bqhd,bkhd->bhqk', q, k)
        scores = scores + jnp.einsum('bqr,bkr->bqk', q_rope, k_rope)[:, None]
        scores = scores / scale
        causal = jnp.triu(jnp.ones((Tt, Tt), dtype=bool), k=1)
        scores = jnp.where(causal[None, None], -jnp.inf, scores)
        w = jax.nn.softmax(scores, axis=-1)
        attn = jnp.einsum('bhqk,bkhd->bqhd', w, v).reshape(Bb, Tt, D_MODEL)
        return attn @ W_o

    def _L3_ffn_ref(x, gate_w, gate_b, w1, b1, w2, b2, ws1, bs1, ws2, bs2):
        import jax, jax.numpy as jnp
        import numpy as np
        B, S, DIM = (4, 256, 128)
        E, K, HID = (8, 2, 512)
        orig_shape = x.shape
        xf = x.reshape(-1, DIM)
        logits = xf @ gate_w + gate_b
        top_w, top_i = jax.lax.top_k(logits, K)
        gw = jax.nn.softmax(top_w, axis=-1).astype(xf.dtype)
        combine = (gw[:, :, None] * jax.nn.one_hot(top_i, E, dtype=xf.dtype)).sum(axis=1)
        out = jnp.zeros_like(xf)
        for e in range(E):
            h = jax.nn.gelu(xf @ w1[e] + b1[e], approximate=False)
            out = out + combine[:, e:e + 1] * (h @ w2[e] + b2[e])
        shared = jax.nn.gelu(xf @ ws1 + bs1, approximate=False) @ ws2 + bs2
        return (out + shared).reshape(orig_shape)
    x = L0_attn_x
    xn = _layernorm(x, axis=-1)
    x = x + _L0_attn_ref(xn, L0_attn_Wq, L0_attn_bq, L0_attn_Wk, L0_attn_bk, L0_attn_Wv, L0_attn_bv, L0_attn_Wo, L0_attn_bo) + _L0_ffn_ref(xn, L0_ffn_weight, L0_ffn_alpha, L0_ffn_bias)
    xn = _layernorm(x, axis=-1)
    x = x + _L1_attn_ref(xn, L1_attn_norm_scale, L1_attn_wq, L1_attn_wk, L1_attn_wv, L1_attn_w_out, L1_attn_b_out) + _L1_ffn_ref(xn, L1_ffn_gate_w, L1_ffn_gate_b, L1_ffn_w1, L1_ffn_w3, L1_ffn_w2)
    xn = _layernorm(x, axis=-1)
    x = x + _L2_attn_ref(xn, L2_attn_w_qkv, L2_attn_w_out) + _L2_ffn_ref(xn, L2_ffn_Wr, L2_ffn_br, L2_ffn_ln_g, L2_ffn_ln_b, L2_ffn_W1, L2_ffn_b1, L2_ffn_W2, L2_ffn_b2)
    xn = _layernorm(x, axis=-1)
    x = x + _L3_attn_ref(xn, L3_attn_W_kv_down, L3_attn_W_k_up, L3_attn_W_v_up, L3_attn_W_q, L3_attn_W_q_rope, L3_attn_W_k_rope, L3_attn_W_o) + _L3_ffn_ref(xn, L3_ffn_gate_w, L3_ffn_gate_b, L3_ffn_w1, L3_ffn_b1, L3_ffn_w2, L3_ffn_b2, L3_ffn_ws1, L3_ffn_bs1, L3_ffn_ws2, L3_ffn_bs2)
    return x

_drawn_inputs = setup_inputs


def setup_inputs(seed=0):
    import zlib

    import numpy as np

    out = dict(_drawn_inputs(seed))
    spreads = {'L1_attn_norm_scale': (1.0, 0.6),
     'L1_attn_b_out': (0.0, 2.0),
     'L2_ffn_br': (0.0, 0.8),
     'L2_ffn_ln_g': (1.0, 0.6),
     'L2_ffn_ln_b': (0.0, 0.8),
     'L2_ffn_b1': (0.0, 2.0),
     'L2_ffn_b2': (0.0, 2.0),
     'L3_ffn_gate_b': (0.0, 0.8),
     'L3_ffn_b1': (0.0, 2.0),
     'L3_ffn_b2': (0.0, 2.0),
     'L3_ffn_bs1': (0.0, 2.0),
     'L3_ffn_bs2': (0.0, 2.0)}
    factors = {'L0_attn_bq': 6.543,
     'L0_attn_bk': 6.485,
     'L0_attn_bo': 5.847,
     'L0_ffn_bias': 5.995,
     'L1_attn_wq': 2.894,
     'L1_attn_wk': 2.909,
     'L1_attn_wv': 2.676,
     'L1_attn_w_out': 2.682,
     'L1_ffn_gate_w': 8.0,
     'L1_ffn_gate_b': 8.0,
     'L1_ffn_w1': 7.33,
     'L1_ffn_w3': 7.138,
     'L1_ffn_w2': 7.129,
     'L2_attn_w_qkv': 4.321,
     'L2_attn_w_out': 4.406,
     'L2_ffn_Wr': 8.0,
     'L2_ffn_W1': 8.0,
     'L2_ffn_W2': 8.0,
     'L3_attn_W_k_up': 12.474,
     'L3_attn_W_q': 12.523,
     'L3_ffn_gate_w': 7.986,
     'L3_ffn_w1': 8.0,
     'L3_ffn_w2': 8.0,
     'L3_ffn_ws1': 8.0,
     'L3_ffn_ws2': 8.0,
     'L3_attn_W_kv_down': 4.164,
     'L3_attn_W_v_up': 3.966,
     'L3_attn_W_q_rope': 8.0,
     'L3_attn_W_k_rope': 8.0,
     'L3_attn_W_o': 3.945}
    for name, (base, spread) in spreads.items():
        noise = np.random.default_rng([zlib.crc32(name.encode()), seed]).standard_normal(out[name].shape)
        drawn = base * np.exp(spread * noise) if base else spread * noise
        out[name] = jnp.asarray(drawn.astype(out[name].dtype))
    for name, factor in factors.items():
        out[name] = (out[name] * factor).astype(out[name].dtype)
    return out
```

```python
from contextlib import ExitStack

import numpy as np

import concourse.bass as bass
from concourse import mybir

ALU = mybir.AluOpType
ACT = mybir.ActivationFunctionType
AX = mybir.AxisListType
F32 = mybir.dt.float32
BF16 = mybir.dt.bfloat16

P = 128
SEQ = 256
CHUNK = 512
TILES = CHUNK // P
TOKENS = 16 * SEQ
NCH = TOKENS // CHUNK
HEADS = 16
UNITS = 2 * HEADS
E = 8
FB = 4
PIECES = E * FB
HD1 = 64
ROPE = 32
GROUP = 32
LN_EPS = 1e-5
RMS_EPS = 1e-6
SCALE1 = HD1 ** -0.5
SCALE2 = 8 ** -0.5
SCALE3 = (8 + ROPE) ** -0.5
BIG = 3.0e38

ROW_B1_2, ROW_B1_3, ROW_BS1 = 0, PIECES, 2 * PIECES
VECTORS = ["L0_attn_bq", "L0_attn_bk", "L0_attn_bv", "L0_attn_bo", "L0_ffn_bias", "L1_attn_norm_scale",
           "L1_attn_b_out", "L2_ffn_ln_g", "L2_ffn_ln_b", "L3_ffn_bs2"]
COL = {name: 2 * PIECES + FB + n for n, name in enumerate(VECTORS)}
ROWS = 2 * PIECES + FB + len(VECTORS)


class Event:

    def __init__(self, sem, per):
        self.sem, self.per = sem, per

    def value(self, layer, i, k):
        before = sum(n * NCH for l, n in self.per.items() if l < layer)
        return i * self.per[layer] + (before + k + 1)

    def wait(self, eng, layer, i, k):
        assert 0 <= k < self.per[layer]
        eng.wait_ge(self.sem, self.value(layer, i, k))


class Chain:

    def __init__(self, eng, event, layer, i):
        self.eng, self.event, self.layer, self.i, self.k = eng, event, layer, i, 0

    def link(self, ins):
        ins.then_inc(self.event.sem, 1)
        self.event.wait(self.eng, self.layer, self.i, self.k)
        self.k += 1

    def last(self, ins):
        ins.then_inc(self.event.sem, 1)
        self.k += 1

    def settle(self):
        self.event.wait(self.eng, self.layer, self.i, self.k - 1)

    def close(self):
        assert self.k == self.event.per[self.layer], (self.layer, self.k)


def build_program(nc, A, out):
    ctx = ExitStack()
    with ctx:
        def sb(name, shape, dt=F32):
            return ctx.enter_context(nc.sbuf_tensor(name, shape, dt))

        def bank(name):
            return ctx.enter_context(nc.psum_tensor(name, [P, CHUNK], F32))

        def sem(name):
            return ctx.enter_context(nc.semaphore(name))

        def event(name, **per):
            return Event(sem(name), {int(k[1]): n for k, n in per.items()})

        x = sb("x", [P, TOKENS // P, P])
        ident = sb("ident", [P, P])
        ident16 = sb("ident16", [P, P], BF16)
        mask16 = sb("mask16", [P, P], BF16)
        mask32 = sb("mask32", [P, P])
        head_sum = sb("head_sum", [P, P])
        head_pick = sb("head_pick", [P, 2, 4])
        expert_pick = sb("expert_pick", [E, E, P])
        rank_w = sb("rank_w", [P, TILES, E])
        cos_t = sb("cos_t", [P, SEQ])
        sin_t = sb("sin_t", [P, SEQ])
        rows = sb("rows", [ROWS, P])
        cols = sb("cols", [P, ROWS])
        bias0 = sb("bias0", [P, 1])
        ones = sb("ones", [P, P])
        pow_half = sb("pow_half", [P, TILES])
        w0 = sb("w0", [P, 4, P])
        w0f = sb("w0f", [P, P])
        tern = sb("tern", [P, 3, P])
        tsum = sb("tsum", [P, 4])
        alpha = sb("alpha", [P, 1])
        w2t = sb("w2t", [P, 4, P])
        w2a = sb("w2a", [P, PIECES * P])
        w2b = sb("w2b", [P, PIECES, P])
        wr2 = sb("wr2", [P, E])
        b2_2 = sb("b2_2", [E, P])
        rb = sb("rb", [P, 3, TILES, E])
        wg1 = sb("wg1", [P, E])
        wg3 = sb("wg3", [P, E])
        b2_3 = sb("b2_3", [E, P])
        region = sb("region", [P, 16384])
        w1q = region[:, 0:1024]
        w1k = region[:, 1024:2048]
        w1v = region[:, 2048:3072]
        w1o = region[:, 3072:4096].rearrange("p (j d) -> p j d", j=8)
        w1a = region[:, 4096:8192]
        w1c = region[:, 8192:12288]
        w1b = region[:, 12288:16384].rearrange("p (n d) -> p n d", n=PIECES)
        w3d = region[:, 0:128]
        w3k = region[:, 128:256]
        w3v = region[:, 256:384]
        w3q = region[:, 384:512]
        w3o = region[:, 512:640]
        w3qr = region[:, 640:672]
        w3kr = region[:, 672:704]
        rope_w = sb("rope_w", [P, 4, 4, ROPE])
        w3a = region[:, 1024:1024 + 36 * P]
        w3b = region[:, 6144:6144 + 36 * P].rearrange("p (n d) -> p n d", n=36)
        stats = sb("stats", [P, TILES, 6])
        mv = sb("mv", [P, TILES, 2])
        rstd = sb("rstd", [P, 4, TILES])
        xn = sb("xn", [P, TILES, P])
        xs = sb("xs", [P, TILES, P])
        xnT = sb("xnT", [P, CHUNK])
        xsT = sb("xsT", [P, CHUNK])
        v1 = sb("v1", [P, TILES, HEADS * HD1])
        vpad = v1[:, :, 0:HEADS * GROUP].rearrange("p t (g j c) -> p t g j c", g=4, j=4)
        qT = sb("qT", [P, 4, CHUNK])
        kT = sb("kT", [P, 2, CHUNK])
        tmp = sb("tmp", [P, 2, CHUNK])
        prob = sb("prob", [P, 3, CHUNK])
        probT = sb("probT", [P, 2, CHUNK])
        nmax = sb("nmax", [P, 4, 2])
        psum_row = sb("psum_row", [P, 4, 2])
        rrow = sb("rrow", [P, 4, 2])
        oT = sb("oT", [P, 2, CHUNK])
        lg = sb("lg", [P, 8, TILES, E])
        sc = sb("sc", [P, 8, TILES])
        cw = sb("cw", [P, TILES, E])
        cT = sb("cT", [E, CHUNK])
        xc = sb("xc", [P, 2, CHUNK])
        act_t = sb("act_t", [P, 2, CHUNK])
        gate_h = sb("gate_h", [P, 2, CHUNK])
        hid = sb("hid", [P, 2, CHUNK])
        yT = tmp[:, 1, :]
        qr, kr, cT3 = xc[:, 0, :], xc[:, 1, :], kT[:, 1, :]
        w2raw = hid[:, 0, :].rearrange("p (n i) -> p n i", n=4)

        acc = bank("acc")
        mo = [bank("mo0"), bank("mo1")]
        sco = [bank("sco0"), bank("sco1")]
        pt = bank("pt")
        ob = bank("ob")
        misc = bank("misc")

        x_in = sem("x_in")
        const_in = sem("const_in")
        w_in = [sem(f"w{n}_in") for n in range(4)]
        y_out = sem("y_out")
        setup_pe = sem("setup_pe")
        setup_v = sem("setup_v")
        setup_a = sem("setup_a")
        setup_g = sem("setup_g")
        w3_prep = sem("w3_prep")
        passed_v = sem("passed_v")
        passed_g = sem("passed_g")
        L = [0, 1, 2, 3]
        ln_aggr = event("ln_aggr", l0=8, l1=8, l2=8, l3=8)
        ln_rstd = event("ln_rstd", l0=2, l1=7, l2=7, l3=2)
        xn_made = event("xn_made", l0=4, l1=8, l2=8, l3=4)
        xn_turned = event("xn_turned", l0=1, l1=2, l2=2, l3=1)
        xT_made = event("xT_made", l0=1, l1=2, l2=2, l3=1)
        proj_full = event("proj_full", l0=4, l1=8, l2=3, l3=7)
        proj_read_a = event("proj_read_a", l0=4, l1=4, l2=2, l3=3)
        proj_read_v = event("proj_read_v", l0=2, l1=4, l2=7, l3=17)
        lg_full = event("lg_full", l1=1, l2=1, l3=1)
        route = event("route", l1=18, l2=10, l3=18)
        route_exp = event("route_exp", l1=1, l2=1, l3=1)
        cw_turned = event("cw_turned", l1=1, l2=1, l3=1)
        cT_made = event("cT_made", l1=1, l2=1, l3=1)
        pick_full = event("pick_full", l1=8, l2=8, l3=8)
        xc_made = event("xc_made", l1=8)
        q_full = event("q_full", l1=8)
        q_made = event("q_made", l1=8)
        k_full = event("k_full", l1=8)
        k_made = event("k_made", l1=8)
        s_full = event("s_full", l1=32, l2=32, l3=32)
        nmax_made = event("nmax_made", l1=32, l2=32, l3=32)
        exp_made = event("exp_made", l1=32, l2=32, l3=32)
        rrow_made = event("rrow_made", l1=32, l2=32, l3=32)
        prob_made = event("prob_made", l1=32, l2=32, l3=32)
        prob_turned = event("prob_turned", l1=32, l2=32, l3=32)
        probT_made = event("probT_made", l1=32, l2=32, l3=32)
        av_full = event("av_full", l1=32, l2=32, l3=32)
        oT_made = event("oT_made", l1=8, l2=1, l3=1)
        up_full = event("up_full", l1=32, l2=32, l3=36)
        gate_full = event("gate_full", l1=32)
        act_made = event("act_made", l1=32, l2=32, l3=36)
        gated = event("gated", l1=32)
        hid_made = event("hid_made", l1=32, l2=32, l3=32)
        down_done = event("down_done", l1=32, l2=32, l3=36)
        out_done = event("out_done", l1=7)
        acc_full = event("acc_full", l0=1, l1=1, l2=1, l3=1)
        yT_made = event("yT_made", l0=1, l1=1, l2=1, l3=1)
        y_turned = event("y_turned", l0=1, l1=1, l2=1, l3=1)
        x_made = event("x_made", l0=1, l1=1, l2=1, l3=1)

        N_W = [8, 8, 5, 12]

        def unit1(u):
            return u // 4, (u // 2) % 2, u % 2

        def unit2(u):
            return u // 8, (u // 4) % 2, u % 4

        block = ctx.enter_context(nc.Block())

        @block.sync
        def _(sp):
            def load(dst, src, s):
                sp.dma_start(dst, src).then_inc(s, 16)

            x_src = A["L0_attn_x"].rearrange("b s d -> (b s) d").rearrange("(c t p) d -> c p t d", p=P, t=TILES)
            load(x[:, 0:TILES, :], x_src[0], x_in)
            for dst, name in ((ident[:, :], "ident"), (mask32[:, :], "causal"), (head_sum[:, :], "head_sum"),
                              (head_pick[:, :, :], "head_pick"), (expert_pick[:, :, :], "expert_pick"),
                              (rank_w[:, :, :], "rank_w"), (cos_t[:, :], "cos_t"), (sin_t[:, :], "sin_t")):
                load(dst, A[name], const_in)
            load(rows[ROW_B1_2:ROW_B1_2 + PIECES, :], A["L2_ffn_b1"].rearrange("e (b p) -> (e b) p", p=P), const_in)
            load(rows[ROW_B1_3:ROW_B1_3 + PIECES, :], A["L3_ffn_b1"].rearrange("e (b p) -> (e b) p", p=P), const_in)
            load(rows[ROW_BS1:ROW_BS1 + FB, :], A["L3_ffn_bs1"].rearrange("(b p) -> b p", p=P), const_in)
            for name in VECTORS:
                load(rows[COL[name]:COL[name] + 1, :], A[name].rearrange("(a p) -> a p", a=1), const_in)
            for n, name in enumerate(("L1_ffn_gate_b", "L2_ffn_br", "L3_ffn_gate_b")):
                for t in range(TILES):
                    load(rb[:, n, t, :], A[name].rearrange("(a p) -> a p", a=1).broadcast_to([P, E]), const_in)
            load(tern[:, 0, :], A["L0_ffn_weight"], w_in[0])
            load(alpha[:, :], A["L0_ffn_alpha"].rearrange("(a p) -> a p", a=1).broadcast_to([P, 1]), w_in[0])
            for n, name in enumerate(("Wq", "Wk", "Wv", "Wo")):
                load(w0[:, n, :], A["L0_attn_" + name], w_in[0])
            load(w2raw[:, 0:3, :], A["L2_attn_w_qkv"].rearrange("(n p) i -> p n i", p=P), w_in[0])
            load(w2raw[:, 3, :], A["L2_attn_w_out"], w_in[0])
            for c in range(1, NCH):
                load(x[:, TILES * c:TILES * (c + 1), :], x_src[c], x_in)
            load(w1q, A["L1_attn_wq"].rearrange("d h e -> d (h e)"), w_in[1])
            load(w1k, A["L1_attn_wk"].rearrange("d h e -> d (h e)"), w_in[1])
            load(w1v, A["L1_attn_wv"].rearrange("d h e -> d (h e)"), w_in[1])
            load(w1o, A["L1_attn_w_out"].rearrange("h e d -> (h e) d").rearrange("(j p) d -> p j d", p=P), w_in[1])
            load(wg1[:, :], A["L1_ffn_gate_w"], w_in[1])
            load(w1a.rearrange("p (e f) -> p e f", e=E), A["L1_ffn_w1"].rearrange("e d f -> d e f"), w_in[1])
            load(w1c.rearrange("p (e f) -> p e f", e=E), A["L1_ffn_w3"].rearrange("e d f -> d e f"), w_in[1])
            load(w1b, A["L1_ffn_w2"].rearrange("e f d -> (e f) d").rearrange("(n p) d -> p n d", p=P), w_in[1])
            load(w2a[:, :].rearrange("p (e f) -> p e f", e=E), A["L2_ffn_W1"].rearrange("e d f -> d e f"), w_in[2])
            load(w2b[:, :, :], A["L2_ffn_W2"].rearrange("e f d -> (e f) d").rearrange("(n p) d -> p n d", p=P), w_in[2])
            load(wr2[:, :], A["L2_ffn_Wr"], w_in[2])
            load(b2_2[:, :], A["L2_ffn_b2"], w_in[2])
            load(b2_3[:, :], A["L3_ffn_b2"], w_in[2])
            sp.wait_ge(x_made.sem, x_made.value(1, NCH - 1, 0))
            for dst, name in ((w3d, "W_kv_down"), (w3k, "W_k_up"), (w3v, "W_v_up"), (w3q, "W_q"), (w3o, "W_o"),
                              (w3qr, "W_q_rope"), (w3kr, "W_k_rope")):
                load(dst, A["L3_attn_" + name], w_in[3])
            load(wg3[:, :], A["L3_ffn_gate_w"], w_in[3])
            load(w3a[:, 0:PIECES * P].rearrange("p (e f) -> p e f", e=E),
                 A["L3_ffn_w1"].rearrange("e d f -> d e f"), w_in[3])
            load(w3a[:, PIECES * P:36 * P], A["L3_ffn_ws1"], w_in[3])
            load(w3b[:, 0:PIECES, :], A["L3_ffn_w2"].rearrange("e f d -> (e f) d").rearrange("(n p) d -> p n d", p=P),
                 w_in[3])
            load(w3b[:, PIECES:36, :], A["L3_ffn_ws2"].rearrange("(n p) d -> p n d", p=P), w_in[3])
            y_dst = out.rearrange("b s d -> (b s) d").rearrange("(c t p) d -> c p t d", p=P, t=TILES)
            for c in range(NCH):
                x_made.wait(sp, 3, c, 0)
                sp.dma_start(y_dst[c], x[:, TILES * c:TILES * (c + 1), :]).then_inc(y_out, 16)
            sp.wait_ge(y_out, 16 * NCH)

        N_CONST = 8 + 3 + len(VECTORS) + 3 * TILES

        @block.gpsimd
        def _(pool):
            pool.memset(pow_half[:, :], -0.5).then_inc(setup_g, 1)
            pool.wait_ge(setup_g, 1)

            def norms(layer, i):
                ch = Chain(pool, ln_rstd, layer, i)
                ln_aggr.wait(pool, layer, i, 7)
                pool.sem_inc(passed_g, 1)
                ch.link(pool.tensor_scalar(rstd[:, 0, :], mv[:, :, 1], LN_EPS, None, ALU.add))
                ch.link(pool.tensor_tensor(rstd[:, 1, :], rstd[:, 0, :], pow_half[:, :], ALU.pow))
                if layer in (1, 2):
                    ch.link(pool.tensor_tensor(rstd[:, 2, :], rstd[:, 1, :], rstd[:, 1, :], ALU.mult))
                    ch.link(pool.tensor_tensor(rstd[:, 0, :], rstd[:, 2, :], mv[:, :, 1], ALU.mult))
                    pool.sem_inc(passed_g, 1)
                    ch.link(pool.tensor_scalar(rstd[:, 2, :], rstd[:, 0, :], RMS_EPS if layer == 1 else LN_EPS,
                                               None, ALU.add))
                    ch.link(pool.tensor_tensor(rstd[:, 0, :], rstd[:, 2, :], pow_half[:, :], ALU.pow))
                    ch.link(pool.tensor_tensor(rstd[:, 3, :], rstd[:, 1, :], rstd[:, 0, :], ALU.mult))
                ch.close()

            def norm_prob(layer, i, u):
                rrow_made.wait(pool, layer, i, u)
                pool.sem_inc(passed_g, 1)
                full = layer == 1
                for qt in range(2):
                    lo, hi = (256 * qt, 256 * qt + 256) if full else (128 * qt, 128 + 256 * qt)
                    ins = pool.tensor_scalar(prob[:, u % 3, lo:hi], prob[:, u % 3, lo:hi],
                                             rrow[:, u % 4, qt:qt + 1], None, ALU.mult)
                ins.then_inc(prob_made.sem, 1)

            for layer in L:
                if layer == 3:
                    pool.wait_ge(w_in[3], 16 * N_W[3])
                    for n, w in ((0, w3qr), (2, w3kr)):
                        for r in range(4):
                            pool.tensor_copy(rope_w[:, n, r, :], w)
                            pool.tensor_copy(rope_w[:, n + 1, r, 0:16], w[:, 16:32])
                            last = pool.tensor_copy(rope_w[:, n + 1, r, 16:32], w[:, 0:16])
                    last.then_inc(w3_prep, 1)
                with pool.Fori(0, NCH) as i:
                    norms(layer, i)
                    if layer:
                        for u in range(UNITS):
                            norm_prob(layer, i, u)

        @block.scalar
        def _(act):
            def copy(dst, src):
                return act.activation(dst, src, ACT.Copy)

            act.wait_ge(w_in[0], 16 * N_W[0])
            act.activation(tern[:, 1, :], tern[:, 0, :], ACT.Abs, accum_out=tsum[:, 0:1]).then_inc(setup_a, 1)
            act.wait_ge(setup_pe, 1)
            copy(cols[:, :], misc[:, 0:ROWS]).then_inc(setup_a, 1)
            act.wait_ge(setup_pe, 2)
            copy(tsum[:, 1:2], misc[:, 0:1]).then_inc(setup_a, 1)
            act.wait_ge(setup_pe, 3)
            copy(w2t[:, :, :], mo[0][:, :].rearrange("p (n i) -> p n i", n=4)).then_inc(setup_a, 1)
            act.wait_ge(setup_pe, 4)
            copy(w0f[:, :], misc[:, 0:P]).then_inc(setup_a, 1)
            act.wait_ge(setup_a, 5)

            def turned(layer, i):
                xn_turned.wait(act, layer, i, 0)
                copy(xnT[:, :], misc[:, :]).then_inc(xT_made.sem, 1)
                if layer in (1, 2):
                    xn_turned.wait(act, layer, i, 1)
                    if layer == 1:
                        ins = act.activation(xsT[:, :], mo[0][:, :], ACT.Identity,
                                             scale=cols[:, COL["L1_attn_norm_scale"]:COL["L1_attn_norm_scale"] + 1])
                    else:
                        ins = act.activation(xsT[:, :], mo[0][:, :], ACT.Identity,
                                             scale=cols[:, COL["L2_ffn_ln_g"]:COL["L2_ffn_ln_g"] + 1],
                                             bias=cols[:, COL["L2_ffn_ln_b"]:COL["L2_ffn_ln_b"] + 1])
                    ins.then_inc(xT_made.sem, 1)

            def finish(layer, i):
                acc_full.wait(act, layer, i, 0)
                bias = {0: bias0[:, 0:1], 1: cols[:, COL["L1_attn_b_out"]:COL["L1_attn_b_out"] + 1],
                        3: cols[:, COL["L3_ffn_bs2"]:COL["L3_ffn_bs2"] + 1]}.get(layer)
                ins = copy(yT, acc[:, :]) if bias is None else \
                    act.activation(yT, acc[:, :], ACT.Identity, bias=bias)
                ins.then_inc(yT_made.sem, 1)

            def exps(layer, i, u):
                nmax_made.wait(act, layer, i, u)
                if u >= 3:
                    prob_turned.wait(act, layer, i, u - 3)
                for qt in range(2):
                    lo, hi = (256 * qt, 256 * qt + 256) if layer == 1 else (128 * qt, 128 + 256 * qt)
                    ins = act.activation(prob[:, u % 3, lo:hi], sco[u % 2][:, lo:hi], ACT.Exp,
                                         bias=nmax[:, u % 4, qt:qt + 1], accum_out=psum_row[:, u % 4, qt:qt + 1])
                ins.then_inc(exp_made.sem, 1)

            def turn_prob(layer, i, u):
                prob_turned.wait(act, layer, i, u)
                if u >= 2:
                    av_full.wait(act, layer, i, u - 2)
                w = 512 if layer == 1 else 384
                copy(probT[:, u % 2, 0:w], pt[:, 0:w]).then_inc(probT_made.sem, 1)

            with act.Fori(0, NCH) as i:
                turned(0, i)
                ch = Chain(act, proj_read_a, 0, i)
                for n, name in enumerate(("L0_attn_bq", "L0_attn_bk")):
                    proj_full.wait(act, 0, i, n)
                    ch.last(act.activation(tmp[:, n, :], sco[n][:, :], ACT.Square, bias=cols[:, COL[name]:COL[name] + 1]))
                proj_full.wait(act, 0, i, 2)
                ch.last(act.activation(kT[:, 0, :], pt[:, :], ACT.Identity,
                                       bias=cols[:, COL["L0_attn_bv"]:COL["L0_attn_bv"] + 1]))
                proj_read_v.wait(act, 0, i, 0)
                ch.last(act.activation(qT[:, 1, :], qT[:, 0, :], ACT.Exp, scale=-0.5))
                ch.close()
                finish(0, i)

            with act.Fori(0, NCH) as i:
                turned(1, i)
                ch = Chain(act, proj_read_a, 1, i)
                vb = [sco[0], sco[1], pt, ob]
                for n in range(0, 8, 2):
                    proj_full.wait(act, 1, i, n)
                    ch.last(copy(v1[:, n // 2, 0:512], vb[n % 4][:, :]))
                ch.close()

                def q_evac(j):
                    q_full.wait(act, 1, i, j)
                    act.activation(qT[:, j % 2, :], misc[:, :], ACT.Copy, scale=SCALE1).then_inc(q_made.sem, 1)

                route.wait(act, 1, i, 12)
                act.activation(sc[:, 3, :], sc[:, 2, :], ACT.Exp).then_inc(route_exp.sem, 1)
                q_evac(0)
                for s in range(UNITS + 1):
                    if s < UNITS:
                        if s % 4 == 0 and s // 4 + 1 < 8:
                            q_evac(s // 4 + 1)
                        up_full.wait(act, 1, i, s)
                        if s >= 2:
                            gated.wait(act, 1, i, s - 2)
                        act.activation(act_t[:, s % 2, :], mo[0][:, :], ACT.Tanh, scale=0.5).then_inc(act_made.sem, 1)
                        exps(1, i, s)
                    if s >= 1:
                        turn_prob(1, i, s - 1)
                finish(1, i)

            with act.Fori(0, NCH) as i:
                turned(2, i)
                ch = Chain(act, proj_read_a, 2, i)
                proj_full.wait(act, 2, i, 0)
                for j in (0, 2):
                    ch.last(act.activation(qT[:, j, :], sco[0][:, :], ACT.Copy, scale=head_pick[:, 0, j:j + 1]))
                ch.close()
                route.wait(act, 2, i, 6)
                act.activation(lg[:, 4, :, :], lg[:, 3, :, :], ACT.Exp).then_inc(route_exp.sem, 1)
                for s in range(UNITS + 1):
                    if s < UNITS:
                        up_full.wait(act, 2, i, s)
                        if s >= 2:
                            hid_made.wait(act, 2, i, s - 2)
                        act.activation(act_t[:, s % 2, :], mo[0][:, :], ACT.Relu,
                                       bias=cols[:, ROW_B1_2 + s:ROW_B1_2 + s + 1]).then_inc(act_made.sem, 1)
                        exps(2, i, s)
                    if s >= 1:
                        turn_prob(2, i, s - 1)
                finish(2, i)

            with act.Fori(0, NCH) as i:
                turned(3, i)
                ch = Chain(act, proj_read_a, 3, i)
                proj_full.wait(act, 3, i, 0)
                ch.last(copy(cT3, sco[0][:, :]))
                proj_full.wait(act, 3, i, 1)
                for j in (0, 2):
                    ch.last(act.activation(qT[:, j, :], sco[1][:, :], ACT.Copy, scale=head_pick[:, 1, j:j + 1]))
                ch.close()
                route.wait(act, 3, i, 12)
                act.activation(sc[:, 3, :], sc[:, 2, :], ACT.Exp).then_inc(route_exp.sem, 1)
                for s in range(UNITS + 1):
                    if s < UNITS:
                        exps(3, i, s)
                    if s >= 1:
                        turn_prob(3, i, s - 1)
                for s in range(36):
                    up_full.wait(act, 3, i, s)
                    if s >= 2:
                        if s - 2 < PIECES:
                            hid_made.wait(act, 3, i, s - 2)
                        else:
                            down_done.wait(act, 3, i, s - 2)
                    act.activation(act_t[:, s % 2, :], mo[0][:, :], ACT.Gelu,
                                   bias=cols[:, ROW_B1_3 + s:ROW_B1_3 + s + 1]).then_inc(act_made.sem, 1)
                finish(3, i)

        @block.tensor
        def _(pe):
            pe.wait_ge(const_in, 16 * N_CONST)
            pe.transpose(misc[:, 0:ROWS], rows[:, :], ident[0:ROWS, 0:ROWS]).then_inc(setup_pe, 1)
            pe.wait_ge(setup_a, 2)
            pe.wait_ge(setup_v, 1)
            pe.matmul(misc[:, 0:1], ones[:, :], tsum[:, 0:1], start=True, stop=True).then_inc(setup_pe, 1)
            pe.wait_ge(w_in[0], 16 * N_W[0])
            for n in range(4):
                ins = pe.transpose(mo[0][:, n * P:(n + 1) * P], w2raw[:, n, :], ident[:, :])
            ins.then_inc(setup_pe, 1)
            pe.wait_ge(setup_v, 6)
            pe.transpose(misc[:, 0:P], tern[:, 2, :], ident[:, :]).then_inc(setup_pe, 1)
            pe.wait_ge(setup_a, 5)

            def mm(dst, lhsT, rhs, start, stop):
                return pe.matmul(dst, lhsT, rhs, start=start, stop=stop)

            def turn_x(layer, i):
                for src, dst, k in ((xn, misc, 0), (xs, mo[0], 1))[:2 if layer in (1, 2) else 1]:
                    xn_made.wait(pe, layer, i, 4 * k + 3)
                    for t in range(TILES):
                        ins = pe.transpose(dst[:, t * P:(t + 1) * P], src[:, t, :], ident[:, :])
                    ins.then_inc(xn_turned.sem, 1)

            def finish(layer, i):
                yT_made.wait(pe, layer, i, 0)
                for t in range(TILES):
                    ins = pe.transpose(misc[:, t * P:(t + 1) * P], yT[:, t * P:(t + 1) * P], ident[:, :])
                ins.then_inc(y_turned.sem, 1)

            def router(layer, i, w, src):
                for t in range(TILES):
                    ins = mm(misc[:, t * E:(t + 1) * E], src[:, t * P:(t + 1) * P], w[:, :], True, True)
                ins.then_inc(lg_full.sem, 1)

            def turn_cw(layer, i):
                route.wait(pe, layer, i, route.per[layer] - 1)
                for t in range(TILES):
                    ins = pe.transpose(misc[0:E, t * P:(t + 1) * P], cw[:, t, :], ident[:, :])
                ins.then_inc(cw_turned.sem, 1)

            def turn_prob(layer, i, u):
                prob_made.wait(pe, layer, i, u)
                if u >= 1:
                    probT_made.wait(pe, layer, i, u - 1)
                for kt in range(2):
                    for qt in range(2):
                        if layer == 1:
                            dst, src = 256 * kt + 128 * qt, 256 * qt + 128 * kt
                        elif kt <= qt:
                            dst, src = 256 * kt + 128 * (qt - kt), 128 * qt + 128 * kt
                        else:
                            continue
                        ins = pe.transpose(pt[:, dst:dst + P], prob[:, u % 3, src:src + P], ident[:, :])
                ins.then_inc(prob_turned.sem, 1)

            def av2(layer, i, u):
                g, b, j = unit2(u)
                probT_made.wait(pe, layer, i, u)
                lhs = [vpad[:, 2 * b + kt, g, j, :] for kt in range(2)]
                rows_o = slice(GROUP * g, GROUP * (g + 1))
                mm(ob[rows_o, SEQ * b:SEQ * b + 256], lhs[0], probT[:, u % 2, 0:256], j == 0, False)
                mm(ob[rows_o, SEQ * b + 128:SEQ * b + 256], lhs[1], probT[:, u % 2, 256:384], False, j == 3)\
                    .then_inc(av_full.sem, 1)

            def scores2(layer, i, u):
                g, b, j = unit2(u)
                if u >= 2:
                    exp_made.wait(pe, layer, i, u - 2)
                r = slice(GROUP * g, GROUP * (g + 1))
                for qt in range(2):
                    dst = sco[u % 2][:, 128 * qt:128 + 256 * qt]
                    q0, w = SEQ * b + 128 * qt, 128 + 128 * qt
                    mm(dst, qT[r, j, q0:q0 + P], kT[r, 0, SEQ * b:SEQ * b + w], True, False)
                    if layer == 3:
                        mm(dst, qr[r, q0:q0 + P], kr[r, SEQ * b:SEQ * b + w], False, False)
                    ins = mm(sco[u % 2][:, 256 * qt:256 * qt + 128], ident16[:, :], mask16[:, :], False, True)
                ins.then_inc(s_full.sem, 1)

            with pe.Fori(0, NCH) as i:
                turn_x(0, i)
                xT_made.wait(pe, 0, i, 0)
                for n, dst in enumerate((sco[0], sco[1], pt)):
                    mm(dst[:, :], w0[:, n, :], xnT[:, :], True, True).then_inc(proj_full.sem, 1)
                mm(acc[:, :], w0f[:, :], xnT[:, :], True, False)
                proj_read_a.wait(pe, 0, i, 3)
                mm(ob[:, :], head_sum[:, :], qT[:, 1, :], True, True).then_inc(proj_full.sem, 1)
                proj_read_v.wait(pe, 0, i, 1)
                mm(acc[:, :], w0[:, 3, :], oT[:, 0, :], False, True).then_inc(acc_full.sem, 1)
                finish(0, i)

            pe.wait_ge(w_in[1], 16 * N_W[1])
            with pe.Fori(0, NCH) as i:
                turn_x(1, i)
                xT_made.wait(pe, 1, i, 0)
                router(1, i, wg1, xnT)
                xT_made.wait(pe, 1, i, 1)
                vb = [sco[0], sco[1], pt, ob]
                for n in range(8):
                    t, half = n // 2, n % 2
                    if n >= 4:
                        (proj_read_v if half else proj_read_a).wait(pe, 1, i, (n - 4) // 2)
                    mm(vb[n % 4][:, :], xsT[:, t * P:(t + 1) * P], w1v[:, 512 * half:512 * half + 512], True, True)\
                        .then_inc(proj_full.sem, 1)
                turn_cw(1, i)

                def q_proj(j):
                    mm(misc[:, :], w1q[:, j * P:(j + 1) * P], xsT[:, :], True, True).then_inc(q_full.sem, 1)

                def k_proj(j):
                    q_made.wait(pe, 1, i, j)
                    mm(misc[:, :], w1k[:, j * P:(j + 1) * P], xsT[:, :], True, True).then_inc(k_full.sem, 1)

                def pick(e):
                    k_made.wait(pe, 1, i, e)
                    mm(misc[:, :], expert_pick[:, e, :], cT[:, :], True, True).then_inc(pick_full.sem, 1)

                cT_made.wait(pe, 1, i, 0)
                q_proj(0)
                k_proj(0)
                pick(0)

                def scores(u):
                    j, h, b = unit1(u)
                    if u % 4 == 0:
                        q_made.wait(pe, 1, i, j)
                        k_made.wait(pe, 1, i, j)
                    if u >= 2:
                        exp_made.wait(pe, 1, i, u - 2)
                    r = slice(HD1 * h, HD1 * (h + 1))
                    for qt in range(2):
                        q0 = SEQ * b + P * qt
                        ins = mm(sco[u % 2][:, 256 * qt:256 * qt + 256], qT[r, j % 2, q0:q0 + P],
                                 kT[r, j % 2, SEQ * b:SEQ * (b + 1)], True, True)
                    ins.then_inc(s_full.sem, 1)

                def av(u):
                    j, h, b = unit1(u)
                    if u % 4 == 0 and j:
                        oT_made.wait(pe, 1, i, j - 1)
                    if u == 0:
                        proj_read_v.wait(pe, 1, i, 3)
                        proj_read_a.wait(pe, 1, i, 3)
                    probT_made.wait(pe, 1, i, u)
                    for kt in range(2):
                        head = 2 * j + h
                        ins = mm(ob[HD1 * h:HD1 * (h + 1), SEQ * b:SEQ * (b + 1)],
                                 v1[:, 2 * b + kt, HD1 * head:HD1 * (head + 1)],
                                 probT[:, u % 2, 256 * kt:256 * kt + 256], kt == 0, kt == 1)
                    ins.then_inc(av_full.sem, 1)

                def down(s):
                    hid_made.wait(pe, 1, i, s)
                    mm(acc[:, :], w1b[:, s, :], hid[:, s % 2, :], s == 0, False).then_inc(down_done.sem, 1)

                def out_proj(j):
                    oT_made.wait(pe, 1, i, j)
                    mm(acc[:, :], w1o[:, j, :], oT[:, j % 2, :], False, j == 7)\
                        .then_inc((acc_full if j == 7 else out_done).sem, 1)

                for s in range(UNITS + 3):
                    if s < UNITS:
                        if s % 4 == 0 and s // 4 + 1 < 8:
                            if s:
                                xc_made.wait(pe, 1, i, s // 4)
                            else:
                                xc_made.wait(pe, 1, i, 0)
                            q_proj(s // 4 + 1)
                        if s % 4 == 1 and s // 4 + 1 < 8:
                            k_proj(s // 4 + 1)
                        if s % 4 == 3 and s // 4 + 1 < 8:
                            pick(s // 4 + 1)
                        if s >= 1:
                            gated.wait(pe, 1, i, s - 1)
                        mm(mo[0][:, :], w1a[:, s * P:(s + 1) * P], xnT[:, :], True, True).then_inc(up_full.sem, 1)
                        if s % 4 == 0:
                            xc_made.wait(pe, 1, i, s // 4)
                        if s >= 1:
                            hid_made.wait(pe, 1, i, s - 1)
                        mm(mo[1][:, :], w1c[:, s * P:(s + 1) * P], xc[:, (s // 4) % 2, :], True, True)\
                            .then_inc(gate_full.sem, 1)
                        scores(s)
                    if 1 <= s <= UNITS:
                        turn_prob(1, i, s - 1)
                        down(s - 1)
                    if 2 <= s <= UNITS + 1:
                        av(s - 2)
                    if s >= 6 and (s - 6) % 4 == 0:
                        out_proj((s - 6) // 4)
                finish(1, i)

            pe.wait_ge(w_in[2], 16 * N_W[2])
            with pe.Fori(0, NCH) as i:
                turn_x(2, i)
                xT_made.wait(pe, 2, i, 0)
                router(2, i, wr2, xnT)
                mm(sco[0][:, :], w2t[:, 0, :], xnT[:, :], True, True).then_inc(proj_full.sem, 1)
                mm(sco[1][:, :], w2t[:, 1, :], xnT[:, :], True, True).then_inc(proj_full.sem, 1)
                for t in range(TILES):
                    ins = mm(pt[:, t * P:(t + 1) * P], xnT[:, t * P:(t + 1) * P], w2t[:, 2, :], True, True)
                ins.then_inc(proj_full.sem, 1)
                turn_cw(2, i)
                cT_made.wait(pe, 2, i, 0)
                mm(acc[:, :], b2_2[:, :], cT[:, :], True, False)
                xT_made.wait(pe, 2, i, 1)
                proj_read_a.wait(pe, 2, i, 1)
                proj_read_v.wait(pe, 2, i, 6)
                for s in range(UNITS + 2):
                    if s < UNITS:
                        if s >= 1:
                            act_made.wait(pe, 2, i, s - 1)
                        mm(mo[0][:, :], w2a[:, s * P:(s + 1) * P], xsT[:, :], True, True).then_inc(up_full.sem, 1)
                        if s % 4 == 0:
                            if s:
                                hid_made.wait(pe, 2, i, s - 1)
                            mm(mo[1][:, :], expert_pick[:, s // 4, :], cT[:, :], True, True).then_inc(pick_full.sem, 1)
                        scores2(2, i, s)
                    if 1 <= s <= UNITS:
                        turn_prob(2, i, s - 1)
                        hid_made.wait(pe, 2, i, s - 1)
                        mm(acc[:, :], w2b[:, s - 1, :], hid[:, (s - 1) % 2, :], False, False).then_inc(down_done.sem, 1)
                    if s >= 2:
                        av2(2, i, s - 2)
                oT_made.wait(pe, 2, i, 0)
                mm(acc[:, :], w2t[:, 3, :], oT[:, 0, :], False, True).then_inc(acc_full.sem, 1)
                finish(2, i)

            pe.wait_ge(w_in[3], 16 * N_W[3])
            pe.wait_ge(w3_prep, 1)
            with pe.Fori(0, NCH) as i:
                turn_x(3, i)
                xT_made.wait(pe, 3, i, 0)
                router(3, i, wg3, xnT)
                mm(sco[0][:, :], w3d, xnT[:, :], True, True).then_inc(proj_full.sem, 1)
                mm(sco[1][:, :], w3q, xnT[:, :], True, True).then_inc(proj_full.sem, 1)
                for n, dst in ((0, ob), (1, mo[1])):
                    ins = mm(dst[:, :], rope_w[:, n, :, :].rearrange("p r c -> p (r c)"), xnT[:, :], True, True)
                ins.then_inc(proj_full.sem, 1)
                proj_read_a.wait(pe, 3, i, 0)
                for t in range(TILES):
                    ins = mm(pt[:, t * P:(t + 1) * P], cT3[:, t * P:(t + 1) * P], w3v, True, True)
                ins.then_inc(proj_full.sem, 1)
                mm(sco[0][:, :], w3k, cT3, True, True).then_inc(proj_full.sem, 1)
                proj_read_v.wait(pe, 3, i, 3)
                mm(ob[:, :], rope_w[:, 2, :, :].rearrange("p r c -> p (r c)"), cT3, True, True)\
                    .then_inc(proj_full.sem, 1)
                mm(mo[1][:, :], rope_w[:, 3, :, :].rearrange("p r c -> p (r c)"), cT3, True, True)\
                    .then_inc(proj_full.sem, 1)
                turn_cw(3, i)
                cT_made.wait(pe, 3, i, 0)
                mm(acc[:, :], b2_3[:, :], cT[:, :], True, False)
                proj_read_a.wait(pe, 3, i, 2)
                proj_read_v.wait(pe, 3, i, 16)
                for s in range(UNITS + 2):
                    if s < UNITS:
                        scores2(3, i, s)
                    if 1 <= s <= UNITS:
                        turn_prob(3, i, s - 1)
                    if s >= 2:
                        av2(3, i, s - 2)
                for s in range(37):
                    if s < 36:
                        if s >= 1:
                            act_made.wait(pe, 3, i, s - 1)
                        mm(mo[0][:, :], w3a[:, s * P:(s + 1) * P], xnT[:, :], True, True).then_inc(up_full.sem, 1)
                        if s % 4 == 0 and s < PIECES:
                            if s:
                                hid_made.wait(pe, 3, i, s - 1)
                            mm(mo[1][:, :], expert_pick[:, s // 4, :], cT[:, :], True, True).then_inc(pick_full.sem, 1)
                    if s >= 1:
                        n = s - 1
                        if n < PIECES:
                            hid_made.wait(pe, 3, i, n)
                            src = hid[:, n % 2, :]
                        else:
                            act_made.wait(pe, 3, i, n)
                            src = act_t[:, n % 2, :]
                        mm(acc[:, :], w3b[:, n, :], src, False, False).then_inc(down_done.sem, 1)
                oT_made.wait(pe, 3, i, 0)
                mm(acc[:, :], w3o, oT[:, 0, :], False, True).then_inc(acc_full.sem, 1)
                finish(3, i)

        @block.vector
        def _(dve):
            dve.memset(ones[:, :], 1.0).then_inc(setup_v, 1)
            dve.wait_ge(const_in, 16 * N_CONST)
            dve.tensor_copy(ident16[:, :], ident[:, :])
            dve.tensor_copy(mask16[:, :], mask32[:, :])
            dve.wait_ge(setup_a, 3)
            dve.tensor_scalar(tsum[:, 2:3], tsum[:, 1:2], 0.7 / (P * P), None, ALU.mult).then_inc(setup_v, 1)
            dve.tensor_scalar(tsum[:, 3:4], tsum[:, 1:2], -0.7 / (P * P), None, ALU.mult).then_inc(setup_v, 1)
            dve.wait_ge(setup_v, 3)
            dve.tensor_scalar(tern[:, 1, :], tern[:, 0, :], tsum[:, 3:4], alpha[:, 0:1], ALU.is_lt, ALU.mult)\
                .then_inc(setup_v, 1)
            dve.tensor_scalar(tern[:, 2, :], tern[:, 0, :], tsum[:, 2:3], alpha[:, 0:1], ALU.is_gt, ALU.mult)\
                .then_inc(setup_v, 1)
            dve.tensor_tensor(bias0[:, :], cols[:, COL["L0_attn_bo"]:COL["L0_attn_bo"] + 1],
                              cols[:, COL["L0_ffn_bias"]:COL["L0_ffn_bias"] + 1], ALU.add)
            dve.wait_ge(setup_v, 5)
            dve.tensor_tensor(tern[:, 2, :], tern[:, 2, :], tern[:, 1, :], ALU.subtract).then_inc(setup_v, 1)

            def normalise(layer, i):
                if layer:
                    x_made.wait(dve, layer - 1, NCH - 1, 0)
                src = x[:, bass.ds(i * TILES, TILES), :]
                for t in range(TILES):
                    dve.bn_stats(stats[:, t, :], src[:, t, :]).then_inc(ln_aggr.sem, 1)
                ln_aggr.wait(dve, layer, i, 3)
                dve.sem_inc(passed_v, 1)
                for t in range(TILES):
                    dve.bn_aggr(mv[:, t, :], stats[:, t, :]).then_inc(ln_aggr.sem, 1)
                ln_rstd.wait(dve, layer, i, 1)
                for t in range(TILES):
                    dve.tensor_scalar(xn[:, t, :], src[:, t, :], mv[:, t, 0:1], rstd[:, 1, t:t + 1],
                                      ALU.subtract, ALU.mult).then_inc(xn_made.sem, 1)
                if layer in (1, 2):
                    ln_rstd.wait(dve, layer, i, 6)
                    for t in range(TILES):
                        dve.tensor_scalar(xs[:, t, :], src[:, t, :], mv[:, t, 0:1], rstd[:, 3, t:t + 1],
                                          ALU.subtract, ALU.mult).then_inc(xn_made.sem, 1)

            def finish(layer, i):
                y_turned.wait(dve, layer, i, 0)
                dst = x[:, bass.ds(i * TILES, TILES), :]
                dve.tensor_tensor(dst, dst, misc[:, :].rearrange("p (t d) -> p t d", t=TILES), ALU.add)\
                    .then_inc(x_made.sem, 1)

            def along(a):
                return a.rearrange("p (t o) -> p t o", o=1).broadcast_to([P, TILES, E])

            def best(ch, src, onehot, top, first):
                ch.link(dve.tensor_reduce(top, src, AX.X, ALU.max))
                ch.link(dve.tensor_tensor(first, src, along(top), ALU.is_equal))
                ch.link(dve.tensor_tensor(first, first, rank_w[:, :, :], ALU.mult))
                ch.link(dve.tensor_reduce(sc[:, 7, :], first, AX.X, ALU.max))
                ch.link(dve.tensor_tensor(onehot, first, along(sc[:, 7, :]), ALU.is_equal))

            def router(layer, i):
                lg_full.wait(dve, layer, i, 0)
                ch = Chain(dve, route, layer, i)
                ch.link(dve.tensor_tensor(lg[:, 0, :, :], misc[:, 0:TILES * E].rearrange("p (t e) -> p t e", t=TILES),
                                          rb[:, layer - 1, :, :], ALU.add))
                best(ch, lg[:, 0, :, :], lg[:, 1, :, :], sc[:, 0, :], lg[:, 2, :, :])
                if layer == 2:
                    ch.last(dve.tensor_tensor(lg[:, 3, :, :], lg[:, 0, :, :], along(sc[:, 0, :]), ALU.subtract))
                    route_exp.wait(dve, 2, i, 0)
                    ch.link(dve.tensor_reduce(sc[:, 1, :], lg[:, 4, :, :], AX.X, ALU.add))
                    ch.link(dve.reciprocal(sc[:, 2, :], sc[:, 1, :]))
                    ch.last(dve.tensor_tensor(cw[:, :, :], lg[:, 1, :, :], along(sc[:, 2, :]), ALU.mult))
                else:
                    ch.link(dve.scalar_tensor_tensor(out=lg[:, 3, :, :], in0=lg[:, 1, :, :], scalar=-BIG,
                                                     in1=lg[:, 0, :, :], op0=ALU.mult, op1=ALU.add))
                    best(ch, lg[:, 3, :, :], lg[:, 4, :, :], sc[:, 1, :], lg[:, 2, :, :])
                    ch.last(dve.tensor_tensor(sc[:, 2, :], sc[:, 1, :], sc[:, 0, :], ALU.subtract))
                    route_exp.wait(dve, layer, i, 0)
                    ch.link(dve.tensor_scalar(sc[:, 4, :], sc[:, 3, :], 1.0, None, ALU.add))
                    ch.link(dve.reciprocal(sc[:, 5, :], sc[:, 4, :]))
                    ch.link(dve.tensor_tensor(sc[:, 6, :], sc[:, 5, :], sc[:, 3, :], ALU.mult))
                    dve.tensor_tensor(lg[:, 5, :, :], lg[:, 1, :, :], along(sc[:, 5, :]), ALU.mult)
                    ch.link(dve.tensor_tensor(lg[:, 6, :, :], lg[:, 4, :, :], along(sc[:, 6, :]), ALU.mult))
                    ch.last(dve.tensor_tensor(cw[:, :, :], lg[:, 5, :, :], lg[:, 6, :, :], ALU.add))
                ch.close()

            def keep_cT(layer, i):
                cw_turned.wait(dve, layer, i, 0)
                dve.tensor_copy(cT[:, :], misc[0:E, :]).then_inc(cT_made.sem, 1)

            def row_max(layer, i, u):
                s_full.wait(dve, layer, i, u)
                if layer == 1:
                    ins = dve.tensor_reduce(nmax[:, u % 4, :], sco[u % 2][:, :].rearrange("p (q k) -> p q k", q=2),
                                            AX.X, ALU.max, negate=True)
                else:
                    for qt in range(2):
                        ins = dve.tensor_reduce(nmax[:, u % 4, qt:qt + 1], sco[u % 2][:, 128 * qt:128 + 256 * qt],
                                                AX.X, ALU.max, negate=True)
                ins.then_inc(nmax_made.sem, 1)

            def row_scale(layer, i, u):
                exp_made.wait(dve, layer, i, u)
                dve.reciprocal(rrow[:, u % 4, :], psum_row[:, u % 4, :]).then_inc(rrow_made.sem, 1)

            dve.wait_ge(x_in, 16 * NCH)
            with dve.Fori(0, NCH) as i:
                normalise(0, i)
                proj_read_a.wait(dve, 0, i, 1)
                dve.tensor_tensor(qT[:, 0, :], tmp[:, 0, :], tmp[:, 1, :], ALU.add).then_inc(proj_read_v.sem, 1)
                proj_full.wait(dve, 0, i, 3)
                dve.tensor_tensor(oT[:, 0, :], kT[:, 0, :], ob[:, :], ALU.mult).then_inc(proj_read_v.sem, 1)
                finish(0, i)

            with dve.Fori(0, NCH) as i:
                normalise(1, i)
                vb = [sco[0], sco[1], pt, ob]
                ch = Chain(dve, proj_read_v, 1, i)
                for n in range(1, 8, 2):
                    proj_full.wait(dve, 1, i, n)
                    ch.last(dve.tensor_copy(v1[:, n // 2, 512:1024], vb[n % 4][:, :]))
                ch.close()
                router(1, i)
                keep_cT(1, i)

                def k_evac(j):
                    k_full.wait(dve, 1, i, j)
                    dve.tensor_copy(kT[:, j % 2, :], misc[:, :]).then_inc(k_made.sem, 1)

                def weigh_x(e):
                    pick_full.wait(dve, 1, i, e)
                    dve.scalar_tensor_tensor(out=xc[:, e % 2, :], in0=xnT[:, :], scalar=0.5, in1=misc[:, :],
                                             op0=ALU.mult, op1=ALU.mult).then_inc(xc_made.sem, 1)

                k_evac(0)
                weigh_x(0)
                for s in range(UNITS + 3):
                    if s < UNITS:
                        if s % 4 == 1 and s // 4 + 1 < 8:
                            k_evac(s // 4 + 1)
                        row_max(1, i, s)
                        act_made.wait(dve, 1, i, s)
                        dve.scalar_tensor_tensor(out=gate_h[:, s % 2, :], in0=act_t[:, s % 2, :], scalar=1.0,
                                                 in1=mo[0][:, :], op0=ALU.add, op1=ALU.mult).then_inc(gated.sem, 1)
                        gated.wait(dve, 1, i, s)
                        gate_full.wait(dve, 1, i, s)
                        if s >= 2:
                            down_done.wait(dve, 1, i, s - 2)
                        dve.tensor_tensor(hid[:, s % 2, :], gate_h[:, s % 2, :], mo[1][:, :], ALU.mult)\
                            .then_inc(hid_made.sem, 1)
                        row_scale(1, i, s)
                        if s % 4 == 3 and s // 4 + 1 < 8:
                            weigh_x(s // 4 + 1)
                    if s >= 5 and (s - 5) % 4 == 0:
                        j = (s - 5) // 4
                        av_full.wait(dve, 1, i, 4 * j + 3)
                        if j >= 2:
                            out_done.wait(dve, 1, i, j - 2)
                        dve.tensor_copy(oT[:, j % 2, :], ob[:, :]).then_inc(oT_made.sem, 1)
                finish(1, i)

            dve.memset(v1[:, :, 0:HEADS * GROUP], 0.0).then_inc(setup_v, 1)
            dve.wait_ge(setup_v, 7)

            def pad_values(ch):
                for j in range(4):
                    ch.last(dve.tensor_copy(vpad[:, :, :, j, 8 * j:8 * j + 8],
                                            pt[:, :].rearrange("p (t g j c) -> p t g j c", t=TILES, g=4, j=4)[:, :, :, j, :]))

            with dve.Fori(0, NCH) as i:
                normalise(2, i)
                router(2, i)
                ch = Chain(dve, proj_read_v, 2, i)
                proj_full.wait(dve, 2, i, 0)
                proj_read_a.wait(dve, 2, i, 1)
                for j in (1, 3):
                    ch.last(dve.tensor_scalar(qT[:, j, :], sco[0][:, :], head_pick[:, 0, j:j + 1], None, ALU.mult))
                proj_full.wait(dve, 2, i, 1)
                ch.last(dve.tensor_copy(kT[:, 0, :], sco[1][:, :]))
                proj_full.wait(dve, 2, i, 2)
                pad_values(ch)
                ch.close()
                keep_cT(2, i)
                for s in range(UNITS + 2):
                    if s < UNITS:
                        row_max(2, i, s)
                        act_made.wait(dve, 2, i, s)
                        pick_full.wait(dve, 2, i, s // 4)
                        if s >= 2:
                            down_done.wait(dve, 2, i, s - 2)
                        dve.tensor_tensor(hid[:, s % 2, :], act_t[:, s % 2, :], mo[1][:, :], ALU.mult)\
                            .then_inc(hid_made.sem, 1)
                        row_scale(2, i, s)
                av_full.wait(dve, 2, i, UNITS - 1)
                dve.tensor_copy(oT[:, 0, :], ob[:, :]).then_inc(oT_made.sem, 1)
                finish(2, i)

            with dve.Fori(0, NCH) as i:
                normalise(3, i)
                router(3, i)
                ch = Chain(dve, proj_read_v, 3, i)

                def rotate(dst, scale):
                    for b in range(2):
                        c = slice(SEQ * b, SEQ * (b + 1))
                        ch.last(dve.scalar_tensor_tensor(out=tmp[:, 0, c], in0=ob[:, c], scalar=scale,
                                                         in1=cos_t[:, :], op0=ALU.mult, op1=ALU.mult))
                        ch.last(dve.scalar_tensor_tensor(out=tmp[:, 1, c], in0=mo[1][:, c], scalar=scale,
                                                         in1=sin_t[:, :], op0=ALU.mult, op1=ALU.mult))
                    ch.settle()
                    ch.last(dve.tensor_tensor(dst, tmp[:, 0, :], tmp[:, 1, :], ALU.add))

                proj_full.wait(dve, 3, i, 2)
                rotate(qr, SCALE3)
                proj_read_a.wait(dve, 3, i, 2)
                for j in (1, 3):
                    ch.last(dve.tensor_scalar(qT[:, j, :], sco[1][:, :], head_pick[:, 1, j:j + 1], None, ALU.mult))
                proj_full.wait(dve, 3, i, 3)
                pad_values(ch)
                proj_full.wait(dve, 3, i, 4)
                ch.last(dve.tensor_copy(kT[:, 0, :], sco[0][:, :]))
                ch.settle()
                proj_full.wait(dve, 3, i, 6)
                rotate(kr, 1.0)
                ch.close()
                keep_cT(3, i)
                for s in range(UNITS):
                    row_max(3, i, s)
                    row_scale(3, i, s)
                av_full.wait(dve, 3, i, UNITS - 1)
                dve.tensor_copy(oT[:, 0, :], ob[:, :]).then_inc(oT_made.sem, 1)
                for s in range(PIECES):
                    act_made.wait(dve, 3, i, s)
                    pick_full.wait(dve, 3, i, s // 4)
                    if s >= 2:
                        down_done.wait(dve, 3, i, s - 2)
                    dve.tensor_tensor(hid[:, s % 2, :], act_t[:, s % 2, :], mo[1][:, :], ALU.mult)\
                        .then_inc(hid_made.sem, 1)
                finish(3, i)


_INS = ["L0_attn_x", "L0_attn_Wq", "L0_attn_bq", "L0_attn_Wk", "L0_attn_bk", "L0_attn_Wv", "L0_attn_bv", "L0_attn_Wo",
        "L0_attn_bo", "L0_ffn_weight", "L0_ffn_alpha", "L0_ffn_bias", "L1_attn_norm_scale", "L1_attn_wq", "L1_attn_wk",
        "L1_attn_wv", "L1_attn_w_out", "L1_attn_b_out", "L1_ffn_gate_w", "L1_ffn_gate_b", "L1_ffn_w1", "L1_ffn_w3",
        "L1_ffn_w2", "L2_attn_w_qkv", "L2_attn_w_out", "L2_ffn_Wr", "L2_ffn_br", "L2_ffn_ln_g", "L2_ffn_ln_b",
        "L2_ffn_W1", "L2_ffn_b1", "L2_ffn_W2", "L2_ffn_b2", "L3_attn_W_kv_down", "L3_attn_W_k_up", "L3_attn_W_v_up",
        "L3_attn_W_q", "L3_attn_W_q_rope", "L3_attn_W_k_rope", "L3_attn_W_o", "L3_ffn_gate_w", "L3_ffn_gate_b",
        "L3_ffn_w1", "L3_ffn_b1", "L3_ffn_w2", "L3_ffn_b2", "L3_ffn_ws1", "L3_ffn_bs1", "L3_ffn_ws2", "L3_ffn_bs2"]
_OUT = (16, 256, 128)


def constants():
    p = np.arange(P)
    f32 = np.float32
    head = (p % GROUP) // 8
    inv_freq = (f32(1.0) / f32(10000.0) ** (np.arange(0, ROPE, 2, dtype=f32) / f32(ROPE))).astype(f32)
    freqs = np.outer(inv_freq, np.arange(SEQ, dtype=f32)).astype(f32)
    sign = np.where(p % ROPE < ROPE // 2, -1.0, 1.0).astype(f32)
    own = (head[:, None] == np.arange(4)[None, :]).astype(f32)
    return {
        "ident": np.eye(P, dtype=f32),
        "causal": np.where(p[None, :] <= p[:, None], 0.0, -1e30).astype(f32),
        "head_sum": (p[:, None] // 8 == p[None, :] // 8).astype(f32),
        "head_pick": np.stack([own * f32(SCALE2), own * f32(SCALE3)], 1).astype(f32),
        "expert_pick": np.repeat(np.eye(E, dtype=f32)[:, :, None], P, axis=2),
        "rank_w": np.broadcast_to(np.arange(E, 0, -1, dtype=f32), (P, TILES, E)).copy(),
        "cos_t": np.cos(freqs)[p % (ROPE // 2)].astype(f32),
        "sin_t": (np.sin(freqs)[p % (ROPE // 2)] * sign[:, None]).astype(f32),
    }


def kernel(**inputs):
    import numpy as _np
    import concourse.bacc as _bacc
    from concourse import mybir as _mybir
    from concourse.bass_utils import run_bass_kernel_spmd as _run

    nc = _bacc.Bacc("TRN2", target_bir_lowering=False, num_devices=1)
    arrays, aps = {}, {}
    data = {name: _np.ascontiguousarray(inputs[name]) for name in _INS}
    data.update(constants())
    for name, a in data.items():
        arrays[f"in_{name}_dram"] = a
        aps[name] = nc.dram_tensor(f"in_{name}_dram", a.shape, _mybir.dt.from_np(a.dtype), kind="ExternalInput").ap()
    out = nc.dram_tensor("out_0_dram", _OUT, _mybir.dt.float32, kind="ExternalOutput").ap()
    build_program(nc, aps, out)
    r = _run(nc, [arrays], core_ids=[0])
    return r.results[0]["out_0_dram"]
```

```python
from contextlib import ExitStack

import numpy as np

import concourse.bass as bass
from concourse import mybir

ALU = mybir.AluOpType
ACT = mybir.ActivationFunctionType
AX = mybir.AxisListType
F32 = mybir.dt.float32
BF16 = mybir.dt.bfloat16
I32 = mybir.dt.int32

P = 128
SEQ = 256
CHUNK = 512
TILES = CHUNK // P
TOKENS = 16 * SEQ
ALL = TOKENS // P
NCH = TOKENS // CHUNK
HEADS = 16
UNITS = 2 * HEADS
E = 8
FB = 4
PIECES = E * FB
HD1 = 64
ROPE = 32
GROUP = 32
LN_EPS = 1e-5
RMS_EPS = 1e-6
SCALE1 = HD1 ** -0.5
SCALE2 = 8 ** -0.5
SCALE3 = (8 + ROPE) ** -0.5
BIG = 3.0e38

SLOTS = 256
TOP = {1: 2, 2: 1, 3: 2}
SLOT_TILES = {l: (k * TOKENS + E * (SLOTS - 1)) // SLOTS for l, k in TOP.items()}
MOST = max(SLOT_TILES.values())
ROW = P + 2
ID_COL, FIRST_COL = P, P + 1
TRASH = 2 * TOKENS

ROW_B1_2, ROW_B1_3, ROW_BS1 = 0, PIECES, 2 * PIECES
VECTORS = ["L0_attn_bq", "L0_attn_bk", "L0_attn_bv", "L0_attn_bo", "L0_ffn_bias", "L1_attn_norm_scale",
           "L1_attn_b_out", "L2_ffn_ln_g", "L2_ffn_ln_b", "L3_ffn_bs2"]
COL = {name: 2 * PIECES + FB + n for n, name in enumerate(VECTORS)}
ROWS = 2 * PIECES + FB + len(VECTORS)

STAGES = {"N0": NCH, "L0": NCH}
for _l in (1, 2, 3):
    STAGES.update({f"R{_l}": NCH, f"T{_l}": 1, f"A{_l}": NCH, f"M{_l}": SLOT_TILES[_l], f"C{_l}": NCH})


class Event:

    def __init__(self, sem, per):
        self.sem, self.per, self.base, total = sem, per, {}, 0
        for stage, steps in STAGES.items():
            self.base[stage] = total
            total += per.get(stage, 0) * steps

    def value(self, stage, i, k):
        return i * self.per[stage] + (self.base[stage] + k + 1)

    def wait(self, eng, stage, i, k=0):
        assert 0 <= k < self.per[stage], (stage, k)
        eng.wait_ge(self.sem, self.value(stage, i, k))


class Chain:

    def __init__(self, eng, event, stage, i):
        self.eng, self.event, self.stage, self.i, self.k = eng, event, stage, i, 0

    def link(self, ins):
        ins.then_inc(self.event.sem, 1)
        self.event.wait(self.eng, self.stage, self.i, self.k)
        self.k += 1

    def last(self, ins):
        ins.then_inc(self.event.sem, 1)
        self.k += 1

    def settle(self):
        self.event.wait(self.eng, self.stage, self.i, self.k - 1)

    def close(self):
        assert self.k == self.event.per[self.stage], (self.stage, self.k)


def slot_tiles(eng, layer, step):
    n = SLOT_TILES[layer]
    assert n % 2
    for s in range(4):
        step(s, s // 2, s % 2, s < 2)
    with eng.Fori(0, (n - 5) // 2) as i:
        for b in range(2):
            step(i * 2 + (4 + b), i + 2, b, False)
    step(n - 1, n // 2, 0, False)


def chunk_pairs(eng, step):
    for b in range(2):
        step(b, 0, b, True)
    with eng.Fori(0, NCH // 2 - 1) as i:
        for b in range(2):
            step(i * 2 + (2 + b), i + 1, b, False)


def build_program(nc, A, out):
    ctx = ExitStack()
    with ctx:
        def sb(name, shape, dt=F32):
            return ctx.enter_context(nc.sbuf_tensor(name, shape, dt))

        def bank(name):
            return ctx.enter_context(nc.psum_tensor(name, [P, CHUNK], F32))

        def sem(name):
            return ctx.enter_context(nc.semaphore(name))

        def event(name, **per):
            full = {}
            for k, n in per.items():
                full.update({k: n} if k in STAGES else {f"{k}{l}": n for l in (1, 2, 3)})
            return Event(sem(name), full)

        slot_rows = {l: nc.dram_tensor(f"slot_rows{l}", [SLOT_TILES[l] * SLOTS, ROW], F32).ap() for l in TOP}
        results = {l: nc.dram_tensor(f"results{l}", [TRASH + TOKENS + 4 * P, P], F32).ap() for l in TOP}

        x = sb("x", [P, ALL, P])
        xd = sb("xd", [P, ALL, ROW])
        load2 = sb("load2", [P, FB * E * P])
        ident = sb("ident", [P, P])
        ident16 = sb("ident16", [P, P], BF16)
        mask16 = sb("mask16", [P, P], BF16)
        before = sb("before", [P, P])
        head_pick = sb("head_pick", [P, 2, 4])
        pick16 = sb("pick16", [E, E * P], BF16)
        rank_w = sb("rank_w", [P, E])
        before_e = sb("before_e", [P, E, E])
        multiples = sb("multiples", [P, TOKENS // SLOTS])
        tile_no = sb("tile_no", [P, MOST])
        token_id = sb("token_id", [P, ALL])
        cos_t = sb("cos_t", [P, SEQ])
        sin_t = sb("sin_t", [P, SEQ])
        cols = sb("cols", [P, ROWS])
        bias0 = sb("bias0", [P, 1])
        ones = sb("ones", [P, P])
        pow_half = sb("pow_half", [P, ALL])
        tsum = sb("tsum", [P, 8])
        alpha = tsum[:, 4:5]
        w2t = sb("w2t", [P, 4, P])
        wr = sb("wr", [P, 3, E])
        rb = sb("rb", [P, 3, E])
        b2 = sb("b2", [E, 2, 2, P], BF16)
        wm = sb("wm", [P, 2, 3, PIECES * P], BF16)
        wm2 = sb("wm2", [P, 2, 2, PIECES * P], BF16)
        experts = {1: wm, 2: wm2, 3: wm}
        region = sb("region", [P, 4096])
        w1q = region[:, 0:1024]
        w1k = region[:, 1024:2048]
        w1v = region[:, 2048:3072]
        w1o = region[:, 3072:4096].rearrange("p (j d) -> p j d", j=8)
        w3d = region[:, 0:128]
        w3k = region[:, 128:256]
        w3v = region[:, 256:384]
        w3q = region[:, 384:512]
        w3o = region[:, 512:640]
        w3qr = region[:, 640:672]
        w3kr = region[:, 672:704]
        ws1 = region[:, 1024:1536]
        ws2 = region[:, 1536:2048].rearrange("p (n d) -> p n d", n=FB)
        rope_w = region[:, 2048:2560].rearrange("p (n r c) -> p n r c", n=4, r=4)
        stats8 = sb("stats8", [P, TILES, 8])
        stats, mv4 = stats8[:, :, 0:6], stats8[:, :, 6:8]
        mv = sb("mv", [P, ALL, 2])
        rstd = sb("rstd", [P, 4, ALL])
        sc = sb("sc", [P, 9, ALL])
        gate_w = sb("gate_w", [P, 2, ALL])
        slot_no = sb("slot_no", [P, 2, ALL], I32)
        cnt = sb("cnt", [P, 4, E])
        tile_e = sb("tile_e", [P, 2, MOST])
        tile_ei = sb("tile_ei", [1, MOST], I32)
        dest_no = sb("dest_no", [P, 4], I32)
        dest_f = sb("dest_f", [P, 4])
        xnT = sb("xnT", [P, CHUNK])
        v1 = sb("v1", [P, TILES, HEADS * HD1])
        vpad = v1[:, :, 0:HEADS * GROUP].rearrange("p t (g j c) -> p t g j c", g=4, j=4)
        qT = sb("qT", [P, 4, CHUNK])
        kT = sb("kT", [P, 2, CHUNK])
        tmp = sb("tmp", [P, 2, CHUNK])
        prob = sb("prob", [P, 3, CHUNK])
        probT = sb("probT", [P, 2, CHUNK])
        nmax = sb("nmax", [P, 4, 2])
        psum_row = sb("psum_row", [P, 4, 2])
        rrow = sb("rrow", [P, 4, 2])
        scale_d = sb("scale_d", [P, 2, 2, P])
        oT = sb("oT", [P, 2, CHUNK])
        yT = tmp[:, 1, :]
        xn = tmp[:, 0, :].rearrange("p (t d) -> p t d", t=TILES)
        w0 = qT[:, 2, :].rearrange("p (n d) -> p n d", n=4)
        w0f = kT[:, 1, 0:P]
        prob_flat = prob[:, :, :].rearrange("p a c -> p (a c)")
        tern = prob_flat[:, 0:3 * P].rearrange("p (n d) -> p n d", n=3)
        mask32 = prob_flat[:, 3 * P:4 * P]
        rows = v1[0:ROWS, 0, 0:P]
        head_sum = prob_flat[:, 4 * P:5 * P]
        blank = prob_flat[:, 5 * P:5 * P + 4 * ROW].rearrange("p (t c) -> p t c", t=4)
        pick32 = probT[0:E, :, :].rearrange("p a c -> p (a c)").rearrange("p (e d) -> p e d", e=E)
        b2_32 = oT[0:E, 1, 0:2 * P].rearrange("p (n d) -> p n d", n=2)
        qr, kr, cT3 = tmp[:, 0, :], kT[:, 1, :], oT[:, 1, :]
        rot = probT
        w2raw = v1[:, 1, 0:4 * P].rearrange("p (n i) -> p n i", n=4)
        lg = qT[:, :, :].rearrange("p a (b t e) -> p (a b) t e", b=2, e=E)
        flat1 = v1[:, :, :].rearrange("p t c -> p (t c)")
        hid = flat1[:, 0:2 * CHUNK].rearrange("p (h c) -> p h c", h=2)
        hb = flat1[:, 2 * CHUNK:4 * CHUNK].bitcast(BF16).rearrange("p (h n c) -> p h n c", h=2, n=2)
        x32 = flat1[:, 4 * CHUNK:5 * CHUNK].rearrange("p (b c) -> p b c", b=2)
        xb = kT[:, 0, :].bitcast(BF16).rearrange("p (b n c) -> p b n c", b=2, n=2)
        xg = prob_flat[:, 0:4 * ROW].rearrange("p (b t c) -> p b t c", b=2, t=2)
        xg_b = [prob_flat[:, 2 * ROW * b:2 * ROW * (b + 1)]
                .rearrange("p (t c) -> p t c", t=2) for b in range(2)]
        y_sb = probT[:, 0, :].rearrange("p (b t d) -> p b t d", b=2, t=2)
        shared_h = v1[:, 0:2, HEADS * GROUP:HEADS * GROUP + CHUNK]
        xd_flat = xd[:, :, :].rearrange("p t c -> p (t c)")[:, 0:PIECES * P]

        acc = bank("acc")
        mo = [bank("mo0"), bank("mo1")]
        sco = [bank("sco0"), bank("sco1")]
        pt = bank("pt")
        ob = bank("ob")
        misc = bank("misc")
        pts = [pt, mo[1]]
        scos = [sco[0], sco[1], mo[0]]

        x_in = sem("x_in")
        const_in = sem("const_in")
        att_in = [sem(f"att{n}_in") for n in range(4)]
        exp_in = [sem(f"exp{n}_in") for n in range(4)]
        y_out = sem("y_out")
        blank_sent = sem("blank_sent")
        rows_sent = [sem(f"rows{n}_sent") for n in range(4)]
        xg_in = [sem("xg0_in"), sem("xg1_in")]
        y_sent = [sem("y0_sent"), sem("y1_sent")]
        yc_in = [sem("yc0_in"), sem("yc1_in")]
        setup_pe = sem("setup_pe")
        setup_v = sem("setup_v")
        setup_a = sem("setup_a")
        setup_g = sem("setup_g")
        hi_made = sem("hi_made")
        lo_made = sem("lo_made")
        w3_prep = sem("w3_prep")
        done = {name: sem(f"{name}_stages") for name in ("pe", "act", "dve", "pool")}
        passed_v = sem("passed_v")
        passed_g = sem("passed_g")
        ln_stats = event("ln_stats", N0=9, L0=9, C1=9, C2=9)
        rstd_made = sem("rstd_made")
        xn_made = event("xn_made", L0=4, R=8, A=4)
        xn_turned = event("xn_turned", L0=1, R=1, A=1)
        xT_made = event("xT_made", L0=1, R=1, A=1)
        proj_full = event("proj_full", L0=4, A1=8, A2=3, A3=7)
        proj_read_a = event("proj_read_a", L0=4, A1=4, A2=2, A3=3)
        proj_read_v = event("proj_read_v", L0=2, A1=4, A2=7, A3=17)
        lg_full = event("lg_full", R=1)
        lg_made = event("lg_made", R=1)
        route = event("route", T1=49, T2=38, T3=49)
        route_exp = event("route_exp", T=1)
        ranks_full = event("ranks_full", T=1)
        q_full = event("q_full", A1=8)
        q_made = event("q_made", A1=8)
        k_full = event("k_full", A1=8)
        k_made = event("k_made", A1=8)
        s_full = event("s_full", A=32)
        nmax_made = event("nmax_made", A=32)
        exp_made = event("exp_made", A=32)
        rrow_made = event("rrow_made", A=32)
        scale_made = event("scale_made", A=32)
        prob_turned = event("prob_turned", A=32)
        probT_made = event("probT_made", A=32)
        av_full = event("av_full", A=32)
        oT_made = event("oT_made", A1=8, A2=1, A3=1)
        out_done = event("out_done", A1=7)
        sh_up = event("sh_up", A3=FB)
        sh_act = event("sh_act", A3=FB)
        sh_down = event("sh_down", A3=FB)
        acc_full = event("acc_full", L0=1, A=1)
        yT_made = event("yT_made", L0=1, A=1)
        y_turned = event("y_turned", L0=1, A=1)
        x_made = event("x_made", L0=1, A=1, C=1)
        xg_turned = event("xg_turned", M=1)
        dest_f_made = event("dest_f_made", M=2)
        dest_made = event("dest_made", M=1)
        xh_made = event("xh_made", M=1)
        xl_made = event("xl_made", M1=1, M2=2, M3=1)
        up_full = event("up_full", M=2)
        gate_full = event("gate_full", M1=2)
        act_made = event("act_made", M=2)
        gated = event("gated", M1=4)
        hh_made = event("hh_made", M=2)
        hl_made = event("hl_made", M=2)
        down_done = event("down_done", M=2)
        y_made = event("y_made", M=1)
        c_step = event("c_step", C1=3, C2=1, C3=3)

        ORDER = ["L0"] + [f"{s}{l}" for l in (1, 2, 3) for s in "RTAMC"]

        def stage_closed(eng, stage):
            for engine_done in done.values():
                eng.wait_ge(engine_done, ORDER.index(stage) + 1)

        def parity_tiles(layer, b):
            return sum((SLOT_TILES[l] + 1 - b) // 2 for l in TOP if l < layer)

        def results_sent(eng, layer, b, tiles):
            count = tiles * 32 + 32 * parity_tiles(layer, b)
            if not (isinstance(count, int) and count == 0):
                eng.wait_ge(y_sent[b], count)

        CHOSEN = {1: 12, 2: 4, 3: 12}
        N_ATT = [8, 4, 0, 9]

        def split_from(layer):
            return {1: [(load2[:, :], 0), (xd_flat, 1), (flat1, 2)], 2: [(xd_flat, 0), (load2[:, :], 1)],
                    3: [(xd_flat, 0), (load2[:, :], 2)]}[layer]

        SPLITS = {1: 3, 2: 5, 3: 7}
        DOWN = {1: 2, 2: 1, 3: 2}

        def unit1(u):
            return u // 4, (u // 2) % 2, u % 2

        def unit2(u):
            return u // 8, (u // 4) % 2, u % 4

        CONSTS = [(ident[:, :], "ident"), (mask32, "causal"), (head_sum, "head_sum"),
                  (head_pick[:, :, :], "head_pick"), (pick32[:, :, :], "expert_pick"), (rank_w[:, :], "rank_w"),
                  (cos_t[:, :], "cos_t"), (sin_t[:, :], "sin_t"), (before[:, :], "before"),
                  (before_e[:, :, :], "before_e"), (multiples[:, :], "multiples"), (tile_no[:, :], "tile_no"),
                  (token_id[:, :], "token_id"), (blank, "blank")]
        N_CONST = len(CONSTS) + 3 + len(VECTORS) + 8

        block = ctx.enter_context(nc.Block())

        @block.sync
        def _(sp):
            def load(dst, src, s):
                sp.dma_start(dst, src).then_inc(s, 16)

            def load_up(dst, src, s):
                load(dst.rearrange("p (e f) -> p e f", e=E), src.rearrange("e d f -> d e f"), s)

            def load_down(dst, src, s):
                load(dst.rearrange("p (n d) -> p n d", d=P),
                     src.rearrange("e f d -> (e f) d").rearrange("(n p) d -> p n d", p=P), s)

            x_src = A["L0_attn_x"].rearrange("b s d -> (b s) d").rearrange("(c t p) d -> c p t d", p=P, t=TILES)
            load(x[:, 0:TILES, :], x_src[0], x_in)
            for dst, name in CONSTS:
                load(dst, A[name], const_in)
            load(rows[ROW_B1_2:ROW_B1_2 + PIECES, :], A["L2_ffn_b1"].rearrange("e (b p) -> (e b) p", p=P), const_in)
            load(rows[ROW_B1_3:ROW_B1_3 + PIECES, :], A["L3_ffn_b1"].rearrange("e (b p) -> (e b) p", p=P), const_in)
            load(rows[ROW_BS1:ROW_BS1 + FB, :], A["L3_ffn_bs1"].rearrange("(b p) -> b p", p=P), const_in)
            for name in VECTORS:
                load(rows[COL[name]:COL[name] + 1, :], A[name].rearrange("(a p) -> a p", a=1), const_in)
            for n, name in enumerate(("L1_ffn_gate_b", "L2_ffn_br", "L3_ffn_gate_b")):
                load(rb[:, n, :], A[name].rearrange("(a p) -> a p", a=1).broadcast_to([P, E]), const_in)
            for n, name in enumerate(("L1_ffn_gate_w", "L2_ffn_Wr", "L3_ffn_gate_w")):
                load(wr[:, n, :], A[name], const_in)
            for n, name in enumerate(("L2_ffn_b2", "L3_ffn_b2")):
                load(b2_32[:, n, :], A[name], const_in)
            load(tern[:, 0, :], A["L0_ffn_weight"], att_in[0])
            load(alpha, A["L0_ffn_alpha"].rearrange("(a p) -> a p", a=1).broadcast_to([P, 1]), att_in[0])
            for n, name in enumerate(("Wq", "Wk", "Wv", "Wo")):
                load(w0[:, n, :], A["L0_attn_" + name], att_in[0])
            load(w2raw[:, 0:3, :], A["L2_attn_w_qkv"].rearrange("(n p) i -> p n i", p=P), att_in[0])
            load(w2raw[:, 3, :], A["L2_attn_w_out"], att_in[0])
            for c in range(1, NCH):
                load(x[:, TILES * c:TILES * (c + 1), :], x_src[c], x_in)
            load_up(load2[:, :], A["L1_ffn_w1"], exp_in[1])
            load_up(xd_flat, A["L1_ffn_w3"], exp_in[1])
            sp.wait_ge(setup_pe, 3)
            load_down(flat1, A["L1_ffn_w2"], exp_in[1])
            load(w1q, A["L1_attn_wq"].rearrange("d h e -> d (h e)"), att_in[1])
            load(w1k, A["L1_attn_wk"].rearrange("d h e -> d (h e)"), att_in[1])
            load(w1v, A["L1_attn_wv"].rearrange("d h e -> d (h e)"), att_in[1])
            load(w1o, A["L1_attn_w_out"].rearrange("h e d -> (h e) d").rearrange("(j p) d -> p j d", p=P), att_in[1])
            sp.wait_ge(const_in, 16 * N_CONST)
            for l in TOP:
                dst = slot_rows[l].rearrange("(t p) c -> p t c", p=P)
                for t in range(4):
                    n = len(range(t, SLOT_TILES[l] * SLOTS // P, 4))
                    sp.dma_start(dst[:, t:SLOT_TILES[l] * SLOTS // P:4, :],
                                 blank[:, t:t + 1, :].broadcast_to([P, n, ROW])).then_inc(blank_sent, 16)

            def feed_experts(layer):
                sp.wait_ge(rows_sent[layer], 16 * ALL * TOP[layer])
                stage_closed(sp, f"A{layer}")

                def step(s, half, b, first):
                    if not first:
                        xg_turned.wait(sp, f"M{layer}", s - 2)
                        dest_f_made.wait(sp, f"M{layer}", s - 2, 1)
                    sp.dma_start(xg_b[b], slot_rows[layer][bass.ds(s * SLOTS, SLOTS), :]
                                 .rearrange("(t p) c -> p t c", p=P)).then_inc(xg_in[b], 16)

                slot_tiles(sp, layer, step)

            def feed_combine(layer):
                for b in range(2):
                    sp.wait_ge(y_sent[b], 32 * parity_tiles(layer + 1, b))
                stage_closed(sp, f"M{layer}")

                def step(c, half, b, first):
                    if not first:
                        x_made.wait(sp, f"C{layer}", c - 2)
                    for j in range(TOP[layer]):
                        sp.dma_start(qT[:, 2 * b + j, :].rearrange("p (t d) -> p t d", t=TILES),
                                     results[layer][bass.ds(c * CHUNK + TOKENS * j, CHUNK), :]
                                     .rearrange("(t p) d -> p t d", p=P)).then_inc(yc_in[b], 16)

                chunk_pairs(sp, step)

            sp.wait_ge(rows_sent[1], 16 * ALL * TOP[1])
            stage_closed(sp, "T1")
            load_up(xd_flat, A["L2_ffn_W1"], exp_in[2])
            load_down(load2[:, :], A["L2_ffn_W2"], exp_in[2])
            feed_experts(1)
            for dst, name in ((w3d, "W_kv_down"), (w3k, "W_k_up"), (w3v, "W_v_up"), (w3q, "W_q"), (w3o, "W_o"),
                              (w3qr, "W_q_rope"), (w3kr, "W_k_rope")):
                load(dst, A["L3_attn_" + name], att_in[3])
            load(ws1, A["L3_ffn_ws1"], att_in[3])
            load(ws2, A["L3_ffn_ws2"].rearrange("(n p) d -> p n d", p=P), att_in[3])
            feed_combine(1)
            sp.wait_ge(rows_sent[2], 16 * ALL * TOP[2])
            stage_closed(sp, "T2")
            load_up(xd_flat, A["L3_ffn_w1"], exp_in[3])
            load_down(load2[:, :], A["L3_ffn_w2"], exp_in[3])
            feed_experts(2)
            feed_combine(2)
            feed_experts(3)
            feed_combine(3)
            y_dst = out.rearrange("b s d -> (b s) d").rearrange("(c t p) d -> c p t d", p=P, t=TILES)
            for c in range(NCH):
                x_made.wait(sp, "C3", c)
                sp.dma_start(y_dst[c], x[:, TILES * c:TILES * (c + 1), :]).then_inc(y_out, 16)
            sp.wait_ge(y_out, 16 * NCH)

        @block.gpsimd
        def _(pool):
            pool.memset(pow_half[:, :], -0.5).then_inc(setup_g, 1)
            pool.wait_ge(setup_g, 1)

            def norms(layer):
                count = 1 + 2 * layer + (5 if layer > 1 else 0) + (5 if layer > 2 else 0)

                def link(ins):
                    nonlocal count
                    ins.then_inc(setup_g, 1)
                    pool.wait_ge(setup_g, count + 1)
                    count += 1

                before_stage = {0: "N0", 1: "L0", 2: "C1", 3: "C2"}[layer]
                ln_stats.wait(pool, before_stage, NCH - 1, 8)
                link(pool.tensor_scalar(rstd[:, 0, :], mv[:, :, 1], LN_EPS, None, ALU.add))
                last = pool.tensor_tensor(rstd[:, 1, :], rstd[:, 0, :], pow_half[:, :], ALU.pow)
                if layer in (1, 2):
                    link(last)
                    link(pool.tensor_tensor(rstd[:, 2, :], rstd[:, 1, :], rstd[:, 1, :], ALU.mult))
                    link(pool.tensor_tensor(rstd[:, 0, :], rstd[:, 2, :], mv[:, :, 1], ALU.mult))
                    link(pool.tensor_scalar(rstd[:, 2, :], rstd[:, 0, :], RMS_EPS if layer == 1 else LN_EPS,
                                            None, ALU.add))
                    link(pool.tensor_tensor(rstd[:, 0, :], rstd[:, 2, :], pow_half[:, :], ALU.pow))
                    last = pool.tensor_tensor(rstd[:, 3, :], rstd[:, 1, :], rstd[:, 0, :], ALU.mult)
                link(last)
                pool.sem_inc(rstd_made, 1)

            def dispatch(layer):
                stage_closed(pool, f"T{layer}")
                pool.wait_ge(blank_sent, 16 * 4 * len(TOP))
                for j in range(TOP[layer]):
                    for t in range(ALL):
                        pool.indirect_dma_start(
                            out=slot_rows[layer], out_offset=bass.IndirectOffsetOnAxis(ap=slot_no[:, j, t:t + 1], axis=0),
                            in_=xd[:, t, :], in_offset=None).then_inc(rows_sent[layer], 16)

            def send_results(layer):
                def step(s, half, b, first):
                    y_made.wait(pool, f"M{layer}", s)
                    dest_made.wait(pool, f"M{layer}", s)
                    pool.sem_inc(passed_g, 1)
                    for t in range(2):
                        pool.indirect_dma_start(
                            out=results[layer],
                            out_offset=bass.IndirectOffsetOnAxis(ap=dest_no[:, 2 * b + t:2 * b + t + 1], axis=0),
                            in_=y_sb[:, b, t, :], in_offset=None).then_inc(y_sent[b], 16)

                slot_tiles(pool, layer, step)

            norms(0)
            pool.sem_inc(done["pool"], 1)
            for layer in (1, 2, 3):
                norms(layer)
                pool.sem_inc(done["pool"], 1)
                pool.sem_inc(done["pool"], 1)
                dispatch(layer)
                pool.sem_inc(done["pool"], 1)
                if layer == 2:
                    pool.wait_ge(att_in[3], 16 * N_ATT[3])
                    for n, w in ((0, w3qr), (2, w3kr)):
                        for r in range(4):
                            pool.tensor_copy(rope_w[:, n, r, :], w)
                            pool.tensor_copy(rope_w[:, n + 1, r, 0:16], w[:, 16:32])
                            last = pool.tensor_copy(rope_w[:, n + 1, r, 16:32], w[:, 0:16])
                    last.then_inc(w3_prep, 1)
                send_results(layer)
                pool.sem_inc(done["pool"], 1)
                pool.sem_inc(done["pool"], 1)

        @block.scalar
        def _(act):
            def copy(dst, src):
                return act.activation(dst, src, ACT.Copy)

            act.wait_ge(att_in[0], 16 * N_ATT[0])
            act.activation(tern[:, 1, :], tern[:, 0, :], ACT.Abs, accum_out=tsum[:, 0:1]).then_inc(setup_a, 1)
            act.wait_ge(setup_pe, 1)
            copy(cols[:, :], misc[:, 0:ROWS]).then_inc(setup_a, 1)
            act.wait_ge(setup_pe, 2)
            copy(tsum[:, 1:2], misc[:, 0:1]).then_inc(setup_a, 1)
            act.wait_ge(setup_pe, 3)
            copy(w2t[:, :, :], mo[0][:, :].rearrange("p (n i) -> p n i", n=4)).then_inc(setup_a, 1)
            act.wait_ge(setup_pe, 4)
            copy(w0f, misc[:, 0:P]).then_inc(setup_a, 1)
            act.wait_ge(setup_a, 5)

            def split(layer):
                act.wait_ge(exp_in[layer], 16 * len(split_from(layer)))
                for src, n in split_from(layer):
                    copy(experts[layer][:, 0, n, :], src).then_inc(hi_made, 1)

            def turned(stage, i):
                xn_turned.wait(act, stage, i, 0)
                if stage == "A1":
                    ins = act.activation(xnT[:, :], misc[:, :], ACT.Identity,
                                         scale=cols[:, COL["L1_attn_norm_scale"]:COL["L1_attn_norm_scale"] + 1])
                else:
                    ins = copy(xnT[:, :], misc[:, :])
                ins.then_inc(xT_made.sem, 1)

            def finish(stage, i):
                acc_full.wait(act, stage, i, 0)
                bias = {"L0": bias0[:, 0:1], "A1": cols[:, COL["L1_attn_b_out"]:COL["L1_attn_b_out"] + 1],
                        "A3": cols[:, COL["L3_ffn_bs2"]:COL["L3_ffn_bs2"] + 1]}.get(stage)
                ins = copy(yT, acc[:, :]) if bias is None else \
                    act.activation(yT, acc[:, :], ACT.Identity, bias=bias)
                ins.then_inc(yT_made.sem, 1)

            def exps(stage, i, u):
                nmax_made.wait(act, stage, i, u)
                if u >= 3:
                    prob_turned.wait(act, stage, i, u - 3)
                for qt in range(2):
                    lo, hi = (256 * qt, 256 * qt + 256) if stage == "A1" else (128 * qt, 128 + 256 * qt)
                    ins = act.activation(prob[:, u % 3, lo:hi], scos[u % 3][:, lo:hi], ACT.Exp,
                                         bias=nmax[:, u % 4, qt:qt + 1], accum_out=psum_row[:, u % 4, qt:qt + 1])
                ins.then_inc(exp_made.sem, 1)

            def turn_prob(stage, i, u):
                prob_turned.wait(act, stage, i, u)
                if u >= 2:
                    av_full.wait(act, stage, i, u - 2)
                w = 512 if stage == "A1" else 384
                copy(probT[:, u % 2, 0:w], pts[u % 2][:, 0:w]).then_inc(probT_made.sem, 1)

            with act.Fori(0, NCH) as i:
                turned("L0", i)
                ch = Chain(act, proj_read_a, "L0", i)
                for n, name in enumerate(("L0_attn_bq", "L0_attn_bk")):
                    proj_full.wait(act, "L0", i, n)
                    ch.last(act.activation((oT[:, 0, :], yT)[n], sco[n][:, :], ACT.Square,
                                           bias=cols[:, COL[name]:COL[name] + 1]))
                proj_full.wait(act, "L0", i, 2)
                ch.last(act.activation(kT[:, 0, :], pt[:, :], ACT.Identity,
                                       bias=cols[:, COL["L0_attn_bv"]:COL["L0_attn_bv"] + 1]))
                proj_read_v.wait(act, "L0", i, 0)
                ch.last(act.activation(qT[:, 1, :], qT[:, 0, :], ACT.Exp, scale=-0.5))
                ch.close()
                finish("L0", i)
            act.sem_inc(done["act"], 1)
            split(1)

            def router(layer):
                stage = f"R{layer}"
                with act.Fori(0, NCH) as i:
                    xn_turned.wait(act, stage, i)
                    copy(xnT[:, :], pt[:, :]).then_inc(xT_made.sem, 1)
                act.sem_inc(done["act"], 1)
                if layer == 2:
                    route.wait(act, "T2", 0, 5)
                    act.activation(lg[:, 4, :, :], lg[:, 3, :, :], ACT.Exp).then_inc(route_exp.sem, 1)
                else:
                    route.wait(act, f"T{layer}", 0, 11)
                    act.activation(sc[:, 3, :], sc[:, 2, :], ACT.Exp).then_inc(route_exp.sem, 1)
                act.sem_inc(done["act"], 1)

            def experts_act(layer):
                stage = f"M{layer}"
                last = SLOT_TILES[layer] - 1

                def turned_rows(s, b):
                    xg_turned.wait(act, stage, s)
                    src = pt[:, SLOTS * b:SLOTS * (b + 1)]
                    if layer == 2:
                        ins = act.activation(x32[:, b, :], src, ACT.Identity,
                                             scale=cols[:, COL["L2_ffn_ln_g"]:COL["L2_ffn_ln_g"] + 1],
                                             bias=cols[:, COL["L2_ffn_ln_b"]:COL["L2_ffn_ln_b"] + 1])
                    else:
                        ins = copy(xb[:, b, 0, :], src)
                    ins.then_inc(xh_made.sem, 1)

                def hidden_high(s, h):
                    gated.wait(act, stage, s, 2 * h + 1)
                    copy(hb[:, h, 0, :], hid[:, h, :]).then_inc(hh_made.sem, 1)

                def keep_y(s, b):
                    down_done.wait(act, stage, s, 1)
                    copy(y_sb[:, b, :, :], (ob, misc)[b][:, 0:2 * P].rearrange("p (t d) -> p t d", t=2))\
                        .then_inc(y_made.sem, 1)

                stage_closed(act, f"A{layer}")
                turned_rows(0, 0)

                def step(s, half, b, first):
                    end = isinstance(s, int) and s == last
                    start = isinstance(s, int) and s == 0
                    if layer > 1:
                        e = act.value_load(tile_ei[0:1, bass.ds(s, 1)], min_val=0, max_val=E - 1)
                    for h in range(2):
                        up_full.wait(act, stage, s, h)
                        if not start:
                            hl_made.wait(act, stage, s - 1, h)
                        if layer == 1:
                            ins = act.activation(hid[:, h, :], sco[h][:, :], ACT.Tanh, scale=0.5)
                        else:
                            for f in range(2):
                                at = (ROW_B1_2 if layer == 2 else ROW_B1_3) + 2 * h + f
                                ins = act.activation(hid[:, h, SLOTS * f:SLOTS * (f + 1)],
                                                     sco[h][:, SLOTS * f:SLOTS * (f + 1)],
                                                     ACT.Relu if layer == 2 else ACT.Gelu,
                                                     bias=cols[:, bass.ds(e * FB + at, 1)])
                        ins.then_inc(act_made.sem, 1)
                        if h == 0:
                            if not (start or (isinstance(s, int) and s == 1)):
                                y_sent_before(act, b, half)
                                keep_y(s - 2, b)
                            if layer == 1 and not start:
                                if not first:
                                    down_done.wait(act, stage, s - 2, 1)
                                hidden_high(s - 1, 1)
                            if not end:
                                if not start:
                                    up_full.wait(act, stage, s - 1, 1)
                                    if layer == 1:
                                        gate_full.wait(act, stage, s - 1, 1)
                                    if layer == 2:
                                        xl_made.wait(act, stage, s - 1, 1)
                                turned_rows(s + 1, 1 - b)
                        elif layer == 1:
                            if not start:
                                down_done.wait(act, stage, s - 1, 0)
                            hidden_high(s, 0)

                def y_sent_before(eng, b, half):
                    results_sent(eng, layer, b, half - 1)

                slot_tiles(act, layer, step)
                if layer == 1:
                    down_done.wait(act, stage, last - 1, 1)
                    hidden_high(last, 1)
                y_sent_before(act, 1, last // 2)
                keep_y(last - 1, 1)
                y_sent_before(act, 0, last // 2 + 1)
                keep_y(last, 0)
                act.sem_inc(done["act"], 1)

            stage_closed(act, "L0")
            router(1)
            act.wait_ge(blank_sent, 16 * 4 * len(TOP))
            with act.Fori(0, NCH) as i:
                turned("A1", i)
                ch = Chain(act, proj_read_a, "A1", i)
                vb = [sco[0], sco[1], pt, ob]
                for n in range(0, 8, 2):
                    proj_full.wait(act, "A1", i, n)
                    ch.last(copy(v1[:, n // 2, 0:512], vb[n % 4][:, :]))
                ch.close()

                def q_evac(j):
                    q_full.wait(act, "A1", i, j)
                    act.activation(qT[:, j % 2, :], misc[:, :], ACT.Copy, scale=SCALE1).then_inc(q_made.sem, 1)

                q_evac(0)
                for s in range(UNITS + 2):
                    if s < UNITS:
                        if s % 4 == 0 and s // 4 + 1 < 8:
                            q_evac(s // 4 + 1)
                        exps("A1", i, s)
                    if s >= 2:
                        turn_prob("A1", i, s - 2)
                finish("A1", i)
            act.sem_inc(done["act"], 1)
            split(2)
            experts_act(1)
            act.sem_inc(done["act"], 1)

            stage_closed(act, "C1")
            router(2)
            with act.Fori(0, NCH) as i:
                turned("A2", i)
                ch = Chain(act, proj_read_a, "A2", i)
                proj_full.wait(act, "A2", i, 0)
                for j in (0, 2):
                    ch.last(act.activation(qT[:, j, :], sco[0][:, :], ACT.Copy, scale=head_pick[:, 0, j:j + 1]))
                ch.close()
                for s in range(UNITS + 2):
                    if s < UNITS:
                        exps("A2", i, s)
                    if s >= 2:
                        turn_prob("A2", i, s - 2)
                finish("A2", i)
            act.sem_inc(done["act"], 1)
            split(3)
            experts_act(2)
            act.sem_inc(done["act"], 1)

            stage_closed(act, "C2")
            router(3)
            with act.Fori(0, NCH) as i:
                turned("A3", i)
                ch = Chain(act, proj_read_a, "A3", i)
                proj_full.wait(act, "A3", i, 0)
                ch.last(copy(cT3, sco[0][:, :]))
                proj_full.wait(act, "A3", i, 1)
                for j in (0, 2):
                    ch.last(act.activation(qT[:, j, :], sco[1][:, :], ACT.Copy, scale=head_pick[:, 1, j:j + 1]))
                ch.close()
                for s in range(UNITS + 2):
                    if s < UNITS:
                        exps("A3", i, s)
                    if s >= 2:
                        turn_prob("A3", i, s - 2)
                for s in range(FB):
                    sh_up.wait(act, "A3", i, s)
                    if s >= 2:
                        sh_down.wait(act, "A3", i, s - 2)
                    act.activation(shared_h[:, s % 2, :], mo[0][:, :], ACT.Gelu,
                                   bias=cols[:, ROW_BS1 + s:ROW_BS1 + s + 1]).then_inc(sh_act.sem, 1)
                finish("A3", i)
            act.sem_inc(done["act"], 1)
            experts_act(3)
            act.sem_inc(done["act"], 1)

        @block.tensor
        def _(pe):
            def mm(dst, lhsT, rhs, start, stop):
                return pe.matmul(dst, lhsT, rhs, start=start, stop=stop)

            def mm3(dst, left, right, start, stop):
                mm(dst, left(0), right(0), start, False)
                mm(dst, left(1), right(0), False, False)
                return mm(dst, left(0), right(1), False, stop)

            pe.wait_ge(const_in, 16 * N_CONST)
            pe.transpose(misc[:, 0:ROWS], rows[:, :], ident[0:ROWS, 0:ROWS]).then_inc(setup_pe, 1)
            pe.wait_ge(setup_a, 2)
            pe.wait_ge(setup_v, 1)
            mm(misc[:, 0:1], ones[:, :], tsum[:, 0:1], True, True).then_inc(setup_pe, 1)
            pe.wait_ge(att_in[0], 16 * N_ATT[0])
            for n in range(4):
                ins = pe.transpose(mo[0][:, n * P:(n + 1) * P], w2raw[:, n, :], ident[:, :])
            ins.then_inc(setup_pe, 1)
            pe.wait_ge(setup_v, 6)
            pe.transpose(misc[:, 0:P], tern[:, 2, :], ident[:, :]).then_inc(setup_pe, 1)
            pe.wait_ge(setup_a, 5)

            def turn_x(stage, i, dst=misc):
                xn_made.wait(pe, stage, i, 3)
                for t in range(TILES):
                    ins = pe.transpose(dst[:, t * P:(t + 1) * P], xn[:, t, :], ident[:, :])
                ins.then_inc(xn_turned.sem, 1)

            def finish(stage, i):
                yT_made.wait(pe, stage, i, 0)
                for t in range(TILES):
                    ins = pe.transpose(misc[:, t * P:(t + 1) * P], yT[:, t * P:(t + 1) * P], ident[:, :])
                ins.then_inc(y_turned.sem, 1)

            def router(layer):
                stage = f"R{layer}"
                stage_closed(pe, ORDER[ORDER.index(stage) - 1])
                with pe.Fori(0, NCH) as i:
                    xn_made.wait(pe, stage, i, 7)
                    for t in range(TILES):
                        ins = pe.transpose(pt[:, t * P:(t + 1) * P], xn[:, t, :], ident[:, :])
                    ins.then_inc(xn_turned.sem, 1)
                    xT_made.wait(pe, stage, i)
                    for t in range(TILES):
                        ins = mm(misc[:, t * E:(t + 1) * E], xnT[:, t * P:(t + 1) * P], wr[:, layer - 1, :], True, True)
                    ins.then_inc(lg_full.sem, 1)
                pe.sem_inc(done["pe"], 1)
                route.wait(pe, f"T{layer}", 0, CHOSEN[layer])
                chosen = lg[:, 1 if layer == 2 else 5, :, :].rearrange("p t e -> p (t e)")
                mm(misc[:, 0:ALL * E], before[:, :], chosen, True, True)
                mm(misc[:, ALL * E:2 * ALL * E], ones[:, :], chosen, True, True).then_inc(ranks_full.sem, 1)
                pe.sem_inc(done["pe"], 1)
                stage_closed(pe, f"T{layer}")

            def experts_pe(layer):
                stage = f"M{layer}"
                w = experts[layer]
                last = SLOT_TILES[layer] - 1
                xl_last = xl_made.per[stage] - 1

                def expert(s):
                    return pe.value_load(tile_ei[0:1, bass.ds(s, 1)], min_val=0, max_val=E - 1)

                def turn_rows(s, b, half, start):
                    pe.wait_ge(xg_in[b], half * 16 + 16 * (1 + parity_tiles(layer, b)))
                    if not start:
                        xl_made.wait(pe, stage, s - 2, xl_last)
                    for t in range(2):
                        ins = pe.transpose(pt[:, SLOTS * b + P * t:SLOTS * b + P * (t + 1)], xg_b[b][:, t, 0:P],
                                           ident[:, :])
                    ins.then_inc(xg_turned.sem, 1)

                def up(s, b, h, e, start):
                    if h == 0:
                        xl_made.wait(pe, stage, s, xl_last)
                    for n, bank_, full in ((0, sco[h], up_full), (1, mo[h], gate_full))[:2 if layer == 1 else 1]:
                        if not start:
                            if layer == 1:
                                gated.wait(pe, stage, s - 1, 2 * h + n)
                            else:
                                act_made.wait(pe, stage, s - 1, h)
                        for f in range(2):
                            at = (2 * h + f) * P
                            ins = mm3(bank_[:, SLOTS * f:SLOTS * (f + 1)],
                                      lambda hl: w[:, hl, n, bass.ds(e * (FB * P) + at, P)],
                                      lambda hl: xb[:, b, hl, :], True, True)
                        ins.then_inc(full.sem, 1)

                def down(s, b, h, e, start):
                    dst = (ob, misc)[b]
                    if h == 0 and not start:
                        y_made.wait(pe, stage, s - 2)
                    hl_made.wait(pe, stage, s, h)
                    for t in range(2):
                        y = dst[:, P * t:P * (t + 1)]
                        if h == 0 and layer > 1:
                            for hl in range(2):
                                mm(y, pick16[:, bass.ds(e * P, P)], b2[:, layer - 2, hl, :], t == 0 and hl == 0, False)
                        for f in range(2):
                            at = (2 * h + f) * P
                            ins = mm3(y, lambda hl: hb[:, h, hl, SLOTS * f + P * t:SLOTS * f + P * (t + 1)],
                                      lambda hl: w[:, hl, DOWN[layer], bass.ds(e * (FB * P) + at, P)],
                                      t == 0 and h == 0 and f == 0 and layer == 1, t == 1 and h == 1 and f == 1)
                    ins.then_inc(down_done.sem, 1)

                stage_closed(pe, f"A{layer}")
                pe.wait_ge(lo_made, SPLITS[layer])
                turn_rows(0, 0, 0, True)

                def step(s, half, b, first):
                    end = isinstance(s, int) and s == last
                    start = isinstance(s, int) and s == 0
                    e = expert(s)
                    if not start:
                        e_before = expert(s - 1)
                    for h in range(2):
                        up(s, b, h, e, start)
                        if not start:
                            down(s - 1, 1 - b, h, e_before, isinstance(s, int) and s <= 2)
                        if h == 0 and not end:
                            turn_rows(s + 1, 1 - b, half + b, start)

                slot_tiles(pe, layer, step)
                e = expert(last)
                for h in range(2):
                    down(last, 0, h, e, False)
                pe.sem_inc(done["pe"], 1)

            def turn_prob(stage, i, u):
                scale_made.wait(pe, stage, i, u)
                if u >= 2:
                    probT_made.wait(pe, stage, i, u - 2)
                for kt in range(2):
                    for qt in range(2):
                        if stage == "A1":
                            dst, src = 256 * kt + 128 * qt, 256 * qt + 128 * kt
                        elif kt <= qt:
                            dst, src = 256 * kt + 128 * (qt - kt), 128 * qt + 128 * kt
                        else:
                            continue
                        ins = mm(pts[u % 2][:, dst:dst + P], prob[:, u % 3, src:src + P], scale_d[:, u % 2, qt, :],
                                 True, True)
                ins.then_inc(prob_turned.sem, 1)

            def av2(stage, i, u):
                g, b, j = unit2(u)
                probT_made.wait(pe, stage, i, u)
                lhs = [vpad[:, 2 * b + kt, g, j, :] for kt in range(2)]
                rows_o = slice(GROUP * g, GROUP * (g + 1))
                mm(ob[rows_o, SEQ * b:SEQ * b + 256], lhs[0], probT[:, u % 2, 0:256], j == 0, False)
                mm(ob[rows_o, SEQ * b + 128:SEQ * b + 256], lhs[1], probT[:, u % 2, 256:384], False, j == 3)\
                    .then_inc(av_full.sem, 1)

            def scores2(stage, i, u):
                g, b, j = unit2(u)
                if u >= 3:
                    exp_made.wait(pe, stage, i, u - 3)
                r = slice(GROUP * g, GROUP * (g + 1))
                for qt in range(2):
                    dst = scos[u % 3][:, 128 * qt:128 + 256 * qt]
                    q0, w = SEQ * b + 128 * qt, 128 + 128 * qt
                    mm(dst, qT[r, j, q0:q0 + P], kT[r, 0, SEQ * b:SEQ * b + w], True, False)
                    if stage == "A3":
                        mm(dst, qr[r, q0:q0 + P], kr[r, SEQ * b:SEQ * b + w], False, False)
                    ins = mm(scos[u % 3][:, 256 * qt:256 * qt + 128], ident16[:, :], mask16[:, :], False, True)
                ins.then_inc(s_full.sem, 1)

            with pe.Fori(0, NCH) as i:
                turn_x("L0", i)
                xT_made.wait(pe, "L0", i, 0)
                for n, dst in enumerate((sco[0], sco[1], pt)):
                    mm(dst[:, :], w0[:, n, :], xnT[:, :], True, True).then_inc(proj_full.sem, 1)
                mm(acc[:, :], w0f, xnT[:, :], True, False)
                proj_read_a.wait(pe, "L0", i, 3)
                mm(ob[:, :], head_sum, qT[:, 1, :], True, True).then_inc(proj_full.sem, 1)
                proj_read_v.wait(pe, "L0", i, 1)
                mm(acc[:, :], w0[:, 3, :], oT[:, 0, :], False, True).then_inc(acc_full.sem, 1)
                finish("L0", i)
            pe.sem_inc(done["pe"], 1)

            router(1)
            pe.wait_ge(att_in[1], 16 * N_ATT[1])
            with pe.Fori(0, NCH) as i:
                turn_x("A1", i)
                xT_made.wait(pe, "A1", i, 0)
                vb = [sco[0], sco[1], pt, ob]
                for n in range(8):
                    t, half = n // 2, n % 2
                    if n >= 4:
                        (proj_read_v if half else proj_read_a).wait(pe, "A1", i, (n - 4) // 2)
                    mm(vb[n % 4][:, :], xnT[:, t * P:(t + 1) * P], w1v[:, 512 * half:512 * half + 512], True, True)\
                        .then_inc(proj_full.sem, 1)

                def q_proj(j):
                    if j:
                        k_made.wait(pe, "A1", i, j - 1)
                    mm(misc[:, :], w1q[:, j * P:(j + 1) * P], xnT[:, :], True, True).then_inc(q_full.sem, 1)

                def k_proj(j):
                    q_made.wait(pe, "A1", i, j)
                    mm(misc[:, :], w1k[:, j * P:(j + 1) * P], xnT[:, :], True, True).then_inc(k_full.sem, 1)

                q_proj(0)
                k_proj(0)

                def scores(u):
                    j, h, b = unit1(u)
                    if u % 4 == 0:
                        q_made.wait(pe, "A1", i, j)
                        k_made.wait(pe, "A1", i, j)
                    if u >= 3:
                        exp_made.wait(pe, "A1", i, u - 3)
                    r = slice(HD1 * h, HD1 * (h + 1))
                    for qt in range(2):
                        q0 = SEQ * b + P * qt
                        ins = mm(scos[u % 3][:, 256 * qt:256 * qt + 256], qT[r, j % 2, q0:q0 + P],
                                 kT[r, j % 2, SEQ * b:SEQ * (b + 1)], True, True)
                    ins.then_inc(s_full.sem, 1)

                def av(u):
                    j, h, b = unit1(u)
                    if u % 4 == 0 and j:
                        oT_made.wait(pe, "A1", i, j - 1)
                    if u == 0:
                        proj_read_v.wait(pe, "A1", i, 3)
                        proj_read_a.wait(pe, "A1", i, 3)
                    probT_made.wait(pe, "A1", i, u)
                    for kt in range(2):
                        head = 2 * j + h
                        ins = mm(ob[HD1 * h:HD1 * (h + 1), SEQ * b:SEQ * (b + 1)],
                                 v1[:, 2 * b + kt, HD1 * head:HD1 * (head + 1)],
                                 probT[:, u % 2, 256 * kt:256 * kt + 256], kt == 0, kt == 1)
                    ins.then_inc(av_full.sem, 1)

                def out_proj(j):
                    oT_made.wait(pe, "A1", i, j)
                    mm(acc[:, :], w1o[:, j, :], oT[:, j % 2, :], j == 0, j == 7)\
                        .then_inc((acc_full if j == 7 else out_done).sem, 1)

                proj_read_a.wait(pe, "A1", i, 3)
                proj_read_v.wait(pe, "A1", i, 3)
                for s in range(UNITS + 5):
                    if s < UNITS:
                        if s % 4 == 0 and s // 4 + 1 < 8:
                            q_proj(s // 4 + 1)
                        if s % 4 == 2 and s // 4 + 1 < 8:
                            k_proj(s // 4 + 1)
                        scores(s)
                    if 2 <= s < UNITS + 2:
                        turn_prob("A1", i, s - 2)
                    if 3 <= s < UNITS + 3:
                        av(s - 3)
                    if s >= 8 and s % 4 == 0:
                        out_proj((s - 8) // 4)
                finish("A1", i)
            pe.sem_inc(done["pe"], 1)
            experts_pe(1)
            pe.sem_inc(done["pe"], 1)

            router(2)
            with pe.Fori(0, NCH) as i:
                turn_x("A2", i)
                xT_made.wait(pe, "A2", i, 0)
                mm(sco[0][:, :], w2t[:, 0, :], xnT[:, :], True, True).then_inc(proj_full.sem, 1)
                mm(sco[1][:, :], w2t[:, 1, :], xnT[:, :], True, True).then_inc(proj_full.sem, 1)
                for t in range(TILES):
                    ins = mm(pt[:, t * P:(t + 1) * P], xnT[:, t * P:(t + 1) * P], w2t[:, 2, :], True, True)
                ins.then_inc(proj_full.sem, 1)
                proj_read_a.wait(pe, "A2", i, 1)
                proj_read_v.wait(pe, "A2", i, 6)
                for s in range(UNITS + 3):
                    if s < UNITS:
                        scores2("A2", i, s)
                    if 2 <= s < UNITS + 2:
                        turn_prob("A2", i, s - 2)
                    if s >= 3:
                        av2("A2", i, s - 3)
                oT_made.wait(pe, "A2", i, 0)
                mm(acc[:, :], w2t[:, 3, :], oT[:, 0, :], True, True).then_inc(acc_full.sem, 1)
                finish("A2", i)
            pe.sem_inc(done["pe"], 1)
            experts_pe(2)
            pe.sem_inc(done["pe"], 1)

            router(3)
            pe.wait_ge(w3_prep, 1)
            pe.wait_ge(att_in[3], 16 * N_ATT[3])
            with pe.Fori(0, NCH) as i:
                turn_x("A3", i)
                xT_made.wait(pe, "A3", i, 0)
                mm(sco[0][:, :], w3d, xnT[:, :], True, True).then_inc(proj_full.sem, 1)
                mm(sco[1][:, :], w3q, xnT[:, :], True, True).then_inc(proj_full.sem, 1)
                for n, dst in ((0, ob), (1, mo[1])):
                    ins = mm(dst[:, :], rope_w[:, n, :, :].rearrange("p r c -> p (r c)"), xnT[:, :], True, True)
                ins.then_inc(proj_full.sem, 1)
                proj_read_a.wait(pe, "A3", i, 0)
                for t in range(TILES):
                    ins = mm(pt[:, t * P:(t + 1) * P], cT3[:, t * P:(t + 1) * P], w3v, True, True)
                ins.then_inc(proj_full.sem, 1)
                mm(sco[0][:, :], w3k, cT3, True, True).then_inc(proj_full.sem, 1)
                proj_read_v.wait(pe, "A3", i, 3)
                mm(ob[:, :], rope_w[:, 2, :, :].rearrange("p r c -> p (r c)"), cT3, True, True)\
                    .then_inc(proj_full.sem, 1)
                mm(mo[1][:, :], rope_w[:, 3, :, :].rearrange("p r c -> p (r c)"), cT3, True, True)\
                    .then_inc(proj_full.sem, 1)
                proj_read_a.wait(pe, "A3", i, 2)
                proj_read_v.wait(pe, "A3", i, 16)
                for s in range(UNITS + 3):
                    if s < UNITS:
                        scores2("A3", i, s)
                    if 2 <= s < UNITS + 2:
                        turn_prob("A3", i, s - 2)
                    if s >= 3:
                        av2("A3", i, s - 3)
                for s in range(FB + 1):
                    if s < FB:
                        if s >= 1:
                            sh_act.wait(pe, "A3", i, s - 1)
                        mm(mo[0][:, :], ws1[:, s * P:(s + 1) * P], xnT[:, :], True, True).then_inc(sh_up.sem, 1)
                    if s >= 1:
                        sh_act.wait(pe, "A3", i, s - 1)
                        mm(acc[:, :], ws2[:, s - 1, :], shared_h[:, (s - 1) % 2, :], s == 1, False)\
                            .then_inc(sh_down.sem, 1)
                oT_made.wait(pe, "A3", i, 0)
                mm(acc[:, :], w3o, oT[:, 0, :], False, True).then_inc(acc_full.sem, 1)
                finish("A3", i)
            pe.sem_inc(done["pe"], 1)
            experts_pe(3)
            pe.sem_inc(done["pe"], 1)

        @block.vector
        def _(dve):
            dve.memset(ones[:, :], 1.0).then_inc(setup_v, 1)
            dve.wait_ge(const_in, 16 * N_CONST)
            dve.wait_ge(setup_a, 3)
            dve.tensor_scalar(tsum[:, 2:3], tsum[:, 1:2], 0.7 / (P * P), None, ALU.mult).then_inc(setup_v, 1)
            dve.tensor_scalar(tsum[:, 3:4], tsum[:, 1:2], -0.7 / (P * P), None, ALU.mult).then_inc(setup_v, 1)
            dve.wait_ge(setup_v, 3)
            dve.tensor_scalar(tern[:, 1, :], tern[:, 0, :], tsum[:, 3:4], alpha, ALU.is_lt, ALU.mult)\
                .then_inc(setup_v, 1)
            dve.tensor_scalar(tern[:, 2, :], tern[:, 0, :], tsum[:, 2:3], alpha, ALU.is_gt, ALU.mult)\
                .then_inc(setup_v, 1)
            dve.wait_ge(setup_v, 5)
            dve.tensor_tensor(tern[:, 2, :], tern[:, 2, :], tern[:, 1, :], ALU.subtract).then_inc(setup_v, 1)
            dve.tensor_tensor(bias0[:, :], cols[:, COL["L0_attn_bo"]:COL["L0_attn_bo"] + 1],
                              cols[:, COL["L0_ffn_bias"]:COL["L0_ffn_bias"] + 1], ALU.add).then_inc(setup_v, 1)
            dve.tensor_copy(ident16[:, :], ident[:, :]).then_inc(setup_v, 1)
            dve.tensor_copy(mask16[:, :], mask32).then_inc(setup_v, 1)
            dve.tensor_copy(pick16[:, :].rearrange("p (e d) -> p e d", e=E), pick32).then_inc(setup_v, 1)
            dve.tensor_copy(b2[:, :, 0, :], b2_32).then_inc(setup_v, 1)
            dve.wait_ge(setup_v, 11)
            dve.tensor_tensor(b2[:, :, 1, :], b2_32, b2[:, :, 0, :], ALU.subtract).then_inc(setup_v, 1)
            dve.wait_ge(setup_v, 12)

            def split(layer):
                for n, (src, kind) in enumerate(split_from(layer)):
                    made = SPLITS[layer] - len(split_from(layer)) + n + 1
                    dve.wait_ge(hi_made, made)
                    dve.tensor_tensor(experts[layer][:, 1, kind, :], src, experts[layer][:, 0, kind, :], ALU.subtract)\
                        .then_inc(lo_made, 1)
                dve.wait_ge(lo_made, SPLITS[layer])

            def measure(stage, i):
                dve.sem_inc(passed_v, 1)
                for t in range(TILES):
                    dve.bn_stats(stats[:, t, :], x[:, bass.ds(i * TILES + t, 1), :].rearrange("p a d -> p (a d)"))\
                        .then_inc(ln_stats.sem, 1)
                ln_stats.wait(dve, stage, i, 3)
                dve.sem_inc(passed_v, 1)
                for t in range(TILES):
                    dve.bn_aggr(mv4[:, t, :], stats[:, t, :]).then_inc(ln_stats.sem, 1)
                ln_stats.wait(dve, stage, i, 7)
                dve.sem_inc(passed_v, 1)
                dve.tensor_copy(mv[:, bass.ds(i * TILES, TILES), :], mv4).then_inc(ln_stats.sem, 1)

            def normalise(stage, i, dst, slot, k):
                for t in range(TILES):
                    tile = i * TILES + t
                    dve.tensor_scalar(dst(tile, t), x[:, bass.ds(tile, 1), :].rearrange("p a d -> p (a d)"),
                                      mv[:, bass.ds(tile, 1), 0:1].rearrange("p a d -> p (a d)"),
                                      rstd[:, slot, bass.ds(tile, 1)],
                                      ALU.subtract, ALU.mult).then_inc(xn_made.sem, 1)

            def to_xn(tile, t):
                return xn[:, t, :]

            def to_rows(tile, t):
                return xd[:, bass.ds(tile, 1), 0:P].rearrange("p a d -> p (a d)")

            def finish(stage, i):
                y_turned.wait(dve, stage, i, 0)
                dst = x[:, bass.ds(i * TILES, TILES), :]
                dve.tensor_tensor(dst, dst, misc[:, :].rearrange("p (t d) -> p t d", t=TILES), ALU.add)\
                    .then_inc(x_made.sem, 1)

            def along(a, n=ALL, m=E):
                return a.rearrange("p (t o) -> p t o", o=1).broadcast_to([P, n, m])

            def across(a, n=ALL, m=E):
                return a.rearrange("p (o e) -> p o e", o=1).broadcast_to([P, n, m])

            def best(ch, src, onehot, top, first, rank):
                ch.link(dve.tensor_reduce(top, src, AX.X, ALU.max))
                ch.link(dve.tensor_tensor(first, src, along(top), ALU.is_equal))
                ch.link(dve.tensor_tensor(first, first, across(rank_w[:, :]), ALU.mult))
                ch.link(dve.tensor_reduce(rank, first, AX.X, ALU.max))
                ch.link(dve.tensor_tensor(onehot, first, along(rank), ALU.is_equal))

            def router(layer):
                stage = f"R{layer}"
                stage_closed(dve, ORDER[ORDER.index(stage) - 1])
                dve.wait_ge(rstd_made, layer + 1)
                with dve.Fori(0, NCH) as i:
                    normalise(stage, i, to_rows, 3 if layer == 2 else 1, 0)
                    normalise(stage, i, to_xn, 1, 4)
                    lg_full.wait(dve, stage, i)
                    dve.tensor_tensor(lg[:, 0, bass.ds(i * TILES, TILES), :],
                                      misc[:, 0:TILES * E].rearrange("p (t e) -> p t e", t=TILES),
                                      across(rb[:, layer - 1, :], TILES), ALU.add).then_inc(lg_made.sem, 1)
                lg_made.wait(dve, stage, NCH - 1)
                xn_made.wait(dve, stage, NCH - 1, 7)
                dve.sem_inc(done["dve"], 1)
                ch = Chain(dve, route, f"T{layer}", 0)
                best(ch, lg[:, 0, :, :], lg[:, 1, :, :], sc[:, 0, :], lg[:, 2, :, :], sc[:, 7, :])
                if layer == 2:
                    ch.last(dve.tensor_tensor(lg[:, 3, :, :], lg[:, 0, :, :], along(sc[:, 0, :]), ALU.subtract))
                    route_exp.wait(dve, "T2", 0)
                    ch.link(dve.tensor_reduce(sc[:, 1, :], lg[:, 4, :, :], AX.X, ALU.add))
                    ch.link(dve.reciprocal(gate_w[:, 0, :], sc[:, 1, :]))
                    chosen = lg[:, 1, :, :]
                else:
                    ch.link(dve.scalar_tensor_tensor(out=lg[:, 3, :, :], in0=lg[:, 1, :, :], scalar=-BIG,
                                                     in1=lg[:, 0, :, :], op0=ALU.mult, op1=ALU.add))
                    best(ch, lg[:, 3, :, :], lg[:, 4, :, :], sc[:, 1, :], lg[:, 2, :, :], sc[:, 8, :])
                    ch.last(dve.tensor_tensor(sc[:, 2, :], sc[:, 1, :], sc[:, 0, :], ALU.subtract))
                    ch.link(dve.tensor_tensor(lg[:, 5, :, :], lg[:, 1, :, :], lg[:, 4, :, :], ALU.add))
                    route_exp.wait(dve, f"T{layer}", 0)
                    ch.link(dve.tensor_scalar(sc[:, 4, :], sc[:, 3, :], 1.0, 2.0 if layer == 1 else 1.0,
                                              ALU.add, ALU.mult))
                    ch.link(dve.reciprocal(gate_w[:, 0, :], sc[:, 4, :]))
                    ch.link(dve.tensor_tensor(gate_w[:, 1, :], gate_w[:, 0, :], sc[:, 3, :], ALU.mult))
                ranks_full.wait(dve, f"T{layer}", 0)
                in_tile = misc[:, 0:ALL * E].rearrange("p (t e) -> p t e", e=E)
                tile_sum = misc[:, ALL * E:2 * ALL * E].rearrange("p (t e) -> p t e", e=E)
                a, b = lg[:, 2, :, :], lg[:, 6, :, :]
                ch.link(dve.tensor_copy(a, tile_sum))
                reach = 1
                while reach < ALL:
                    ch.last(dve.tensor_copy(b[:, 0:reach, :], a[:, 0:reach, :]))
                    ch.link(dve.tensor_tensor(b[:, reach:ALL, :], a[:, reach:ALL, :], a[:, 0:ALL - reach, :], ALU.add))
                    ch.settle()
                    a, b, reach = b, a, 2 * reach
                small = lg[:, 3, :, :].rearrange("p t e -> p (t e)")
                ch.link(dve.tensor_copy(cnt[:, 0, :], a[:, ALL - 1, :]))
                n_mult = TOKENS // SLOTS
                cmp = small[:, 0:E * n_mult].rearrange("p (e j) -> p e j", e=E)
                ch.link(dve.tensor_tensor(cmp, along(cnt[:, 0, :], E, n_mult), across(multiples[:, :], E, n_mult),
                                          ALU.is_gt))
                ch.link(dve.tensor_reduce(cnt[:, 1, :], cmp, AX.X, ALU.add))
                pair = small[:, 0:E * E].rearrange("p (e f) -> p e f", e=E)
                ch.link(dve.tensor_tensor(pair, across(cnt[:, 1, :], E), before_e[:, :, :], ALU.mult))
                ch.link(dve.tensor_reduce(cnt[:, 2, :], pair, AX.X, ALU.add))
                ch.link(dve.tensor_tensor(cnt[:, 3, :], cnt[:, 2, :], cnt[:, 1, :], ALU.add))
                at = lg[:, 7, :, :]
                ch.link(dve.tensor_tensor(at, a, tile_sum, ALU.subtract))
                ch.link(dve.tensor_tensor(at, at, in_tile, ALU.add))
                ch.link(dve.scalar_tensor_tensor(out=at, in0=across(cnt[:, 2, :]), scalar=float(SLOTS), in1=at,
                                                 op0=ALU.mult, op1=ALU.add))
                for j in range(TOP[layer]):
                    ch.link(dve.tensor_tensor(lg[:, 0, :, :], lg[:, (1, 4)[j], :, :], at, ALU.mult))
                    ch.link(dve.tensor_reduce(sc[:, 2, :], lg[:, 0, :, :], AX.X, ALU.add))
                    ch.link(dve.tensor_copy(slot_no[:, j, :], sc[:, 2, :]))
                n_tiles = SLOT_TILES[layer]
                big = lg[:, 2:4, :, :].rearrange("p a t e -> p (a t e)")[:, 0:n_tiles * E]\
                    .rearrange("p (s e) -> p s e", e=E)
                ch.link(dve.tensor_tensor(big, across(cnt[:, 3, :], n_tiles), along(tile_no[:, 0:n_tiles], n_tiles),
                                          ALU.is_le))
                ch.link(dve.tensor_reduce(tile_e[:, 0, 0:n_tiles], big, AX.X, ALU.add))
                ch.link(dve.tensor_scalar(tile_e[:, 0, 0:n_tiles], tile_e[:, 0, 0:n_tiles], float(E - 1), None, ALU.min))
                ch.last(dve.tensor_scalar(tile_e[:, 1, 0:n_tiles], tile_e[:, 0, 0:n_tiles], -1.0, float(E),
                                          ALU.mult, ALU.add))
                ch.last(dve.tensor_copy(tile_ei[0:1, 0:n_tiles], tile_e[0:1, 0, 0:n_tiles]))
                ch.last(dve.tensor_copy(xd[:, :, ID_COL], token_id[:, :]))
                ch.link(dve.tensor_copy(xd[:, :, FIRST_COL], sc[:, 7, :]))
                ch.close()
                dve.sem_inc(done["dve"], 1)
                stage_closed(dve, f"T{layer}")

            def experts_dve(layer):
                stage = f"M{layer}"
                last = SLOT_TILES[layer] - 1

                def rows_low(s, b, first):
                    xh_made.wait(dve, stage, s)
                    src = pt[:, SLOTS * b:SLOTS * (b + 1)]
                    if layer == 2:
                        if not first:
                            up_full.wait(dve, stage, s - 2, 1)
                        src = x32[:, b, :]
                        dve.tensor_copy(xb[:, b, 0, :], src).then_inc(xl_made.sem, 1)
                        xl_made.wait(dve, stage, s, 0)
                    dve.tensor_tensor(xb[:, b, 1, :], src, xb[:, b, 0, :], ALU.subtract).then_inc(xl_made.sem, 1)

                def hidden_low(s, h):
                    hh_made.wait(dve, stage, s, h)
                    dve.tensor_tensor(hb[:, h, 1, :], hid[:, h, :], hb[:, h, 0, :], ALU.subtract)\
                        .then_inc(hl_made.sem, 1)

                def gate(s, h):
                    act_made.wait(dve, stage, s, h)
                    dve.scalar_tensor_tensor(out=hid[:, h, :], in0=hid[:, h, :], scalar=1.0, in1=sco[h][:, :],
                                             op0=ALU.add, op1=ALU.mult).then_inc(gated.sem, 1)
                    gated.wait(dve, stage, s, 2 * h)
                    gate_full.wait(dve, stage, s, h)
                    dve.tensor_tensor(hid[:, h, :], hid[:, h, :], mo[h][:, :], ALU.mult).then_inc(gated.sem, 1)

                def place(s, b):
                    f = dest_f[:, 2 * b:2 * b + 2]
                    dve.tensor_scalar(f, xg_b[b][:, :, FIRST_COL], tile_e[:, 1, bass.ds(s, 1)], float(TOKENS),
                                      ALU.not_equal, ALU.mult).then_inc(dest_f_made.sem, 1)
                    dest_f_made.wait(dve, stage, s, 0)
                    dve.tensor_tensor(f, f, xg_b[b][:, :, ID_COL], ALU.add).then_inc(dest_f_made.sem, 1)

                def place_int(s, b, sent):
                    dest_f_made.wait(dve, stage, s, 1)
                    results_sent(dve, layer, b, sent)
                    dve.tensor_copy(dest_no[:, 2 * b:2 * b + 2], dest_f[:, 2 * b:2 * b + 2]).then_inc(dest_made.sem, 1)

                stage_closed(dve, f"A{layer}")
                rows_low(0, 0, True)

                def step(s, half, b, first):
                    end = isinstance(s, int) and s == last
                    start = isinstance(s, int) and s == 0
                    for h in range(2):
                        if layer == 1:
                            gate(s, h)
                            if h:
                                hidden_low(s, 0)
                            elif not start:
                                hidden_low(s - 1, 1)
                        else:
                            act_made.wait(dve, stage, s, h)
                            if not start:
                                down_done.wait(dve, stage, s - 1, h)
                            dve.tensor_copy(hb[:, h, 0, :], hid[:, h, :]).then_inc(hh_made.sem, 1)
                            hidden_low(s, h)
                        if h == 0 and not end:
                            rows_low(s + 1, 1 - b, start)
                    if not first:
                        dest_made.wait(dve, stage, s - 2)
                    if start:
                        dve.wait_ge(xg_in[0], 16 * (1 + parity_tiles(layer, 0)))
                    place(s, b)
                    if not start:
                        place_int(s - 1, 1 - b, half - 1 + b)

                slot_tiles(dve, layer, step)
                if layer == 1:
                    hidden_low(last, 1)
                place_int(last, 0, last // 2)
                dest_made.wait(dve, stage, last)
                dve.sem_inc(done["dve"], 1)

            def combine(layer):
                stage = f"C{layer}"
                stage_closed(dve, f"M{layer}")
                before_layer = {1: 0, 2: TOP[1], 3: TOP[1] + TOP[2]}[layer] * NCH // 2 * 16

                def step(c, half, b, first):
                    dve.wait_ge(yc_in[b], half * (16 * TOP[layer]) + (16 * TOP[layer] + before_layer))
                    dst = x[:, bass.ds(c * TILES, TILES), :]
                    for j in range(TOP[layer]):
                        y = qT[:, 2 * b + j, :].rearrange("p (t d) -> p t d", t=TILES)
                        dve.tensor_tensor(y, y, along(gate_w[:, j, bass.ds(c * TILES, TILES)], TILES, P), ALU.mult)\
                            .then_inc(c_step.sem, 1)
                        c_step.wait(dve, stage, c, 2 * j)
                        last = dve.tensor_tensor(dst, dst, y, ALU.add)
                        if j < TOP[layer] - 1:
                            last.then_inc(c_step.sem, 1)
                            c_step.wait(dve, stage, c, 2 * j + 1)
                    last.then_inc(x_made.sem, 1)
                    if layer < 3:
                        x_made.wait(dve, stage, c)
                        measure(stage, c)

                chunk_pairs(dve, step)
                dve.sem_inc(done["dve"], 1)

            def row_max(stage, i, u):
                s_full.wait(dve, stage, i, u)
                if stage == "A1":
                    ins = dve.tensor_reduce(nmax[:, u % 4, :], scos[u % 3][:, :].rearrange("p (q k) -> p q k", q=2),
                                            AX.X, ALU.max, negate=True)
                else:
                    for qt in range(2):
                        ins = dve.tensor_reduce(nmax[:, u % 4, qt:qt + 1], scos[u % 3][:, 128 * qt:128 + 256 * qt],
                                                AX.X, ALU.max, negate=True)
                ins.then_inc(nmax_made.sem, 1)

            def row_scale(stage, i, u):
                exp_made.wait(dve, stage, i, u)
                if u >= 2:
                    prob_turned.wait(dve, stage, i, u - 2)
                dve.reciprocal(rrow[:, u % 4, :], psum_row[:, u % 4, :]).then_inc(rrow_made.sem, 1)
                rrow_made.wait(dve, stage, i, u)
                for qt in range(2):
                    ins = dve.tensor_scalar(scale_d[:, u % 2, qt, :], ident[:, :], rrow[:, u % 4, qt:qt + 1],
                                            None, ALU.mult)
                ins.then_inc(scale_made.sem, 1)

            dve.wait_ge(x_in, 16 * NCH)
            with dve.Fori(0, NCH) as i:
                measure("N0", i)
            dve.wait_ge(rstd_made, 1)
            with dve.Fori(0, NCH) as i:
                normalise("L0", i, to_xn, 1, 0)
                proj_read_a.wait(dve, "L0", i, 1)
                dve.tensor_tensor(qT[:, 0, :], oT[:, 0, :], yT, ALU.add).then_inc(proj_read_v.sem, 1)
                proj_full.wait(dve, "L0", i, 3)
                dve.tensor_tensor(oT[:, 0, :], kT[:, 0, :], ob[:, :], ALU.mult).then_inc(proj_read_v.sem, 1)
                finish("L0", i)
                x_made.wait(dve, "L0", i)
                measure("L0", i)
            dve.sem_inc(done["dve"], 1)
            split(1)

            router(1)
            with dve.Fori(0, NCH) as i:
                normalise("A1", i, to_xn, 3, 0)
                vb = [sco[0], sco[1], pt, ob]
                ch = Chain(dve, proj_read_v, "A1", i)
                for n in range(1, 8, 2):
                    proj_full.wait(dve, "A1", i, n)
                    ch.last(dve.tensor_copy(v1[:, n // 2, 512:1024], vb[n % 4][:, :]))
                ch.close()

                def k_evac(j):
                    k_full.wait(dve, "A1", i, j)
                    dve.tensor_copy(kT[:, j % 2, :], misc[:, :]).then_inc(k_made.sem, 1)

                k_evac(0)
                for s in range(UNITS + 4):
                    if s < UNITS:
                        if s % 4 == 2 and s // 4 + 1 < 8:
                            k_evac(s // 4 + 1)
                        row_max("A1", i, s)
                    if 1 <= s <= UNITS:
                        row_scale("A1", i, s - 1)
                    if s >= 7 and s % 4 == 3:
                        j = (s - 7) // 4
                        av_full.wait(dve, "A1", i, 4 * j + 3)
                        if j >= 2:
                            out_done.wait(dve, "A1", i, j - 2)
                        dve.tensor_copy(oT[:, j % 2, :], ob[:, :]).then_inc(oT_made.sem, 1)
                finish("A1", i)
            x_made.wait(dve, "A1", NCH - 1)
            dve.sem_inc(done["dve"], 1)
            split(2)
            experts_dve(1)
            combine(1)

            def pad_values(ch):
                for j in range(4):
                    ch.last(dve.tensor_copy(vpad[:, :, :, j, 8 * j:8 * j + 8],
                                            pt[:, :].rearrange("p (t g j c) -> p t g j c", t=TILES, g=4, j=4)[:, :, :, j, :]))

            def clear_values(count):
                dve.memset(v1[:, :, 0:HEADS * GROUP], 0.0).then_inc(setup_v, 1)
                dve.wait_ge(setup_v, count)

            router(2)
            clear_values(13)
            with dve.Fori(0, NCH) as i:
                normalise("A2", i, to_xn, 1, 0)
                ch = Chain(dve, proj_read_v, "A2", i)
                proj_full.wait(dve, "A2", i, 0)
                proj_read_a.wait(dve, "A2", i, 1)
                for j in (1, 3):
                    ch.last(dve.tensor_scalar(qT[:, j, :], sco[0][:, :], head_pick[:, 0, j:j + 1], None, ALU.mult))
                proj_full.wait(dve, "A2", i, 1)
                ch.last(dve.tensor_copy(kT[:, 0, :], sco[1][:, :]))
                proj_full.wait(dve, "A2", i, 2)
                pad_values(ch)
                ch.close()
                for s in range(UNITS + 1):
                    if s < UNITS:
                        row_max("A2", i, s)
                    if s >= 1:
                        row_scale("A2", i, s - 1)
                av_full.wait(dve, "A2", i, UNITS - 1)
                dve.tensor_copy(oT[:, 0, :], ob[:, :]).then_inc(oT_made.sem, 1)
                finish("A2", i)
            x_made.wait(dve, "A2", NCH - 1)
            dve.sem_inc(done["dve"], 1)
            split(3)
            experts_dve(2)
            combine(2)

            router(3)
            clear_values(14)
            with dve.Fori(0, NCH) as i:
                normalise("A3", i, to_xn, 1, 0)
                ch = Chain(dve, proj_read_v, "A3", i)

                def rotate(dst, scale):
                    for b in range(2):
                        c = slice(SEQ * b, SEQ * (b + 1))
                        ch.last(dve.scalar_tensor_tensor(out=rot[:, 0, c], in0=ob[:, c], scalar=scale,
                                                         in1=cos_t[:, :], op0=ALU.mult, op1=ALU.mult))
                        ch.last(dve.scalar_tensor_tensor(out=rot[:, 1, c], in0=mo[1][:, c], scalar=scale,
                                                         in1=sin_t[:, :], op0=ALU.mult, op1=ALU.mult))
                    ch.settle()
                    ch.last(dve.tensor_tensor(dst, rot[:, 0, :], rot[:, 1, :], ALU.add))

                proj_full.wait(dve, "A3", i, 2)
                rotate(qr, SCALE3)
                proj_read_a.wait(dve, "A3", i, 2)
                for j in (1, 3):
                    ch.last(dve.tensor_scalar(qT[:, j, :], sco[1][:, :], head_pick[:, 1, j:j + 1], None, ALU.mult))
                proj_full.wait(dve, "A3", i, 3)
                pad_values(ch)
                proj_full.wait(dve, "A3", i, 4)
                ch.last(dve.tensor_copy(kT[:, 0, :], sco[0][:, :]))
                ch.settle()
                proj_full.wait(dve, "A3", i, 6)
                rotate(kr, 1.0)
                ch.close()
                for s in range(UNITS + 1):
                    if s < UNITS:
                        row_max("A3", i, s)
                    if s >= 1:
                        row_scale("A3", i, s - 1)
                av_full.wait(dve, "A3", i, UNITS - 1)
                dve.tensor_copy(oT[:, 0, :], ob[:, :]).then_inc(oT_made.sem, 1)
                finish("A3", i)
            x_made.wait(dve, "A3", NCH - 1)
            dve.sem_inc(done["dve"], 1)
            experts_dve(3)
            combine(3)


_INS = ["L0_attn_x", "L0_attn_Wq", "L0_attn_bq", "L0_attn_Wk", "L0_attn_bk", "L0_attn_Wv", "L0_attn_bv", "L0_attn_Wo",
        "L0_attn_bo", "L0_ffn_weight", "L0_ffn_alpha", "L0_ffn_bias", "L1_attn_norm_scale", "L1_attn_wq", "L1_attn_wk",
        "L1_attn_wv", "L1_attn_w_out", "L1_attn_b_out", "L1_ffn_gate_w", "L1_ffn_gate_b", "L1_ffn_w1", "L1_ffn_w3",
        "L1_ffn_w2", "L2_attn_w_qkv", "L2_attn_w_out", "L2_ffn_Wr", "L2_ffn_br", "L2_ffn_ln_g", "L2_ffn_ln_b",
        "L2_ffn_W1", "L2_ffn_b1", "L2_ffn_W2", "L2_ffn_b2", "L3_attn_W_kv_down", "L3_attn_W_k_up", "L3_attn_W_v_up",
        "L3_attn_W_q", "L3_attn_W_q_rope", "L3_attn_W_k_rope", "L3_attn_W_o", "L3_ffn_gate_w", "L3_ffn_gate_b",
        "L3_ffn_w1", "L3_ffn_b1", "L3_ffn_w2", "L3_ffn_b2", "L3_ffn_ws1", "L3_ffn_bs1", "L3_ffn_ws2", "L3_ffn_bs2"]
_OUT = (16, 256, 128)


def constants():
    p = np.arange(P)
    f32 = np.float32
    head = (p % GROUP) // 8
    inv_freq = (f32(1.0) / f32(10000.0) ** (np.arange(0, ROPE, 2, dtype=f32) / f32(ROPE))).astype(f32)
    freqs = np.outer(inv_freq, np.arange(SEQ, dtype=f32)).astype(f32)
    sign = np.where(p % ROPE < ROPE // 2, -1.0, 1.0).astype(f32)
    own = (head[:, None] == np.arange(4)[None, :]).astype(f32)
    return {
        "ident": np.eye(P, dtype=f32),
        "causal": np.where(p[None, :] <= p[:, None], 0.0, -1e30).astype(f32),
        "head_sum": (p[:, None] // 8 == p[None, :] // 8).astype(f32),
        "head_pick": np.stack([own * f32(SCALE2), own * f32(SCALE3)], 1).astype(f32),
        "expert_pick": np.repeat(np.eye(E, dtype=f32)[:, :, None], P, axis=2),
        "rank_w": np.broadcast_to(np.arange(E, 0, -1, dtype=f32), (P, E)).copy(),
        "before": np.triu(np.ones((P, P), f32), 1),
        "before_e": np.broadcast_to(np.tril(np.ones((E, E), f32), -1), (P, E, E)).copy(),
        "multiples": np.broadcast_to(np.arange(0, TOKENS, SLOTS, dtype=f32), (P, TOKENS // SLOTS)).copy(),
        "tile_no": np.broadcast_to(np.arange(MOST, dtype=f32), (P, MOST)).copy(),
        "token_id": (np.arange(ALL, dtype=f32)[None, :] * P + p[:, None]).astype(f32),
        "blank": np.concatenate([np.zeros((P, 4, P)), TRASH + P * np.arange(4)[None, :, None] + p[:, None, None],
                                 np.zeros((P, 4, 1))], 2).astype(f32),
        "cos_t": np.cos(freqs)[p % (ROPE // 2)].astype(f32),
        "sin_t": (np.sin(freqs)[p % (ROPE // 2)] * sign[:, None]).astype(f32),
    }


def kernel(**inputs):
    import numpy as _np
    import concourse.bacc as _bacc
    from concourse import mybir as _mybir
    from concourse.bass_utils import run_bass_kernel_spmd as _run

    nc = _bacc.Bacc("TRN2", target_bir_lowering=False, num_devices=1)
    arrays, aps = {}, {}
    data = {name: _np.ascontiguousarray(inputs[name]) for name in _INS}
    data.update(constants())
    for name, a in data.items():
        arrays[f"in_{name}_dram"] = a
        aps[name] = nc.dram_tensor(f"in_{name}_dram", a.shape, _mybir.dt.from_np(a.dtype), kind="ExternalInput").ap()
    out = nc.dram_tensor("out_0_dram", _OUT, _mybir.dt.float32, kind="ExternalOutput").ap()
    build_program(nc, aps, out)
    r = _run(nc, [arrays], core_ids=[0])
    return r.results[0]["out_0_dram"]
```

```python
from contextlib import ExitStack

import numpy as np

import concourse.bass as bass
from concourse import mybir

ALU = mybir.AluOpType
ACT = mybir.ActivationFunctionType
AX = mybir.AxisListType
F32 = mybir.dt.float32
BF16 = mybir.dt.bfloat16
HALF = mybir.dt.float16
I32 = mybir.dt.int32

P = 128
SEQ = 256
CHUNK = 512
TILES = CHUNK // P
TOKENS = 16 * SEQ
ALL = TOKENS // P
NCH = TOKENS // CHUNK
HEADS = 16
UNITS = 2 * HEADS
E = 8
FB = 4
PIECES = E * FB
HD1 = 64
ROPE = 32
GROUP = 32
LN_EPS = 1e-5
RMS_EPS = 1e-6
SCALE1 = HD1 ** -0.5
SCALE2 = 8 ** -0.5
SCALE3 = (8 + ROPE) ** -0.5
BIG = 3.0e38

SLOTS = 256
TOP = {1: 2, 2: 1, 3: 2}
SLOT_TILES = {l: (k * TOKENS + E * (SLOTS - 1)) // SLOTS for l, k in TOP.items()}
MOST = max(SLOT_TILES.values())
ROW = P + 2
ID_COL, FIRST_COL = P, P + 1
TRASH = 2 * TOKENS

ROW_B1_2, ROW_B1_3, ROW_BS1 = 0, PIECES, 2 * PIECES
VECTORS = ["L0_attn_bq", "L0_attn_bk", "L0_attn_bv", "L0_attn_bo", "L0_ffn_bias", "L1_attn_norm_scale",
           "L1_attn_b_out", "L2_ffn_ln_g", "L2_ffn_ln_b", "L3_ffn_bs2"]
COL = {name: 2 * PIECES + FB + n for n, name in enumerate(VECTORS)}
ROWS = 2 * PIECES + FB + len(VECTORS)

STAGES = {"N0": NCH, "L0": NCH}
for _l in (1, 2, 3):
    STAGES.update({f"R{_l}": NCH, f"T{_l}": 1, f"A{_l}": NCH, f"M{_l}": SLOT_TILES[_l], f"C{_l}": NCH})


class Event:

    def __init__(self, sem, per):
        self.sem, self.per, self.base, total = sem, per, {}, 0
        for stage, steps in STAGES.items():
            self.base[stage] = total
            total += per.get(stage, 0) * steps

    def value(self, stage, i, k):
        return i * self.per[stage] + (self.base[stage] + k + 1)

    def wait(self, eng, stage, i, k=0):
        assert 0 <= k < self.per[stage], (stage, k)
        eng.wait_ge(self.sem, self.value(stage, i, k))


class Chain:

    def __init__(self, eng, event, stage, i):
        self.eng, self.event, self.stage, self.i, self.k = eng, event, stage, i, 0

    def link(self, ins):
        ins.then_inc(self.event.sem, 1)
        self.event.wait(self.eng, self.stage, self.i, self.k)
        self.k += 1

    def last(self, ins):
        ins.then_inc(self.event.sem, 1)
        self.k += 1

    def settle(self):
        self.event.wait(self.eng, self.stage, self.i, self.k - 1)

    def close(self):
        assert self.k == self.event.per[self.stage], (self.stage, self.k)


def slot_tiles(eng, layer, step):
    n = SLOT_TILES[layer]
    assert n % 2
    for s in range(4):
        step(s, s // 2, s % 2, s < 2)
    with eng.Fori(0, (n - 5) // 2) as i:
        for b in range(2):
            step(i * 2 + (4 + b), i + 2, b, False)
    step(n - 1, n // 2, 0, False)


def chunk_pairs(eng, step):
    for b in range(2):
        step(b, 0, b, True)
    with eng.Fori(0, NCH // 2 - 1) as i:
        for b in range(2):
            step(i * 2 + (2 + b), i + 1, b, False)


def build_program(nc, A, out):
    ctx = ExitStack()
    with ctx:
        def sb(name, shape, dt=F32):
            return ctx.enter_context(nc.sbuf_tensor(name, shape, dt))

        def bank(name):
            return ctx.enter_context(nc.psum_tensor(name, [P, CHUNK], F32))

        def sem(name):
            return ctx.enter_context(nc.semaphore(name))

        def event(name, **per):
            full = {}
            for k, n in per.items():
                full.update({k: n} if k in STAGES else {f"{k}{l}": n for l in (1, 2, 3)})
            return Event(sem(name), full)

        slot_rows = {l: nc.dram_tensor(f"slot_rows{l}", [SLOT_TILES[l] * SLOTS, ROW], F32).ap() for l in TOP}
        results = {l: nc.dram_tensor(f"results{l}", [TRASH + TOKENS + 4 * P, P], F32).ap() for l in TOP}

        x = sb("x", [P, ALL, P])
        xd = sb("xd", [P, ALL, ROW])
        load2 = sb("load2", [P, FB * E * P])
        ident = sb("ident", [P, P])
        ident16 = sb("ident16", [P, P], BF16)
        mask16 = sb("mask16", [P, P], BF16)
        before = sb("before", [P, P])
        head_pick = sb("head_pick", [P, 4])
        pick16 = sb("pick16", [E, E * P], HALF)
        rank_w = sb("rank_w", [P, E])
        before_e = sb("before_e", [P, E, E])
        multiples = sb("multiples", [P, TOKENS // SLOTS])
        tile_no = sb("tile_no", [P, MOST])
        token_id = sb("token_id", [P, ALL])
        cos_t = sb("cos_t", [P, SEQ])
        sin_t = sb("sin_t", [P, SEQ])
        cols = sb("cols", [P, ROWS])
        bias0 = sb("bias0", [P, 1])
        ones = sb("ones", [P, P])
        pow_half = sb("pow_half", [P, ALL])
        tsum = sb("tsum", [P, 8])
        alpha = tsum[:, 4:5]
        w2t = sb("w2t", [P, 4, P])
        wr = sb("wr", [P, 3, E])
        rb = sb("rb", [P, 3, E])
        b2 = sb("b2", [E, 2, 2, P], HALF)
        wm = sb("wm", [P, 2, 3, PIECES * P], HALF)
        wm2 = sb("wm2", [P, 2, 2, PIECES * P], HALF)
        experts = {1: wm, 2: wm2, 3: wm}
        region = sb("region", [P, 4096])
        w1 = wm2[:, :, 0, :]
        W1Q, W1K, W1V, W1O = 0, 1024, 2048, 3072
        w3d = region[:, 0:128]
        w3k = region[:, 128:256]
        w3v = region[:, 256:384]
        w3q = region[:, 384:512]
        w3o = region[:, 512:640]
        w3qr = region[:, 640:672]
        w3kr = region[:, 672:704]
        ws1 = region[:, 1024:1536]
        ws2 = region[:, 1536:2048].rearrange("p (n d) -> p n d", n=FB)
        bs2_row = region[0:1, 2560:2560 + P]
        rope_w = region[:, 2048:2560].rearrange("p (n r c) -> p n r c", n=4, r=4)
        stats8 = sb("stats8", [P, TILES, 8])
        stats, mv4 = stats8[:, :, 0:6], stats8[:, :, 6:8]
        mv = sb("mv", [P, ALL, 2])
        rstd = sb("rstd", [P, 4, ALL])
        sc = sb("sc", [P, 9, ALL])
        gate_w = sb("gate_w", [P, 2, ALL])
        slot_no = sb("slot_no", [P, 2, ALL], I32)
        cnt = sb("cnt", [P, 4, E])
        tile_e = sb("tile_e", [P, 2, MOST])
        tile_ei = sb("tile_ei", [1, MOST], I32)
        dest_no = sb("dest_no", [P, 4], I32)
        dest_f = sb("dest_f", [P, 4])
        xnT = sb("xnT", [P, CHUNK])
        v1 = sb("v1", [P, TILES, HEADS * HD1])
        qT = sb("qT", [P, 4, CHUNK])
        kT = sb("kT", [P, 2, CHUNK])
        tmp = sb("tmp", [P, 2, CHUNK])
        prob = sb("prob", [P, 3, CHUNK])
        probT = sb("probT", [P, 2, CHUNK])
        nmax = sb("nmax", [P, 4, 2])
        psum_row = sb("psum_row", [P, 4, 2])
        rrow = sb("rrow", [P, 4, 2])
        scale_d = sb("scale_d", [P, 2, 2, P])
        oT = sb("oT", [P, 2, CHUNK])
        yT = tmp[:, 1, :]
        xn = tmp[:, 0, :].rearrange("p (t d) -> p t d", t=TILES)
        w0 = qT[:, 2, :].rearrange("p (n d) -> p n d", n=4)
        w0f = kT[:, 1, 0:P]
        prob_flat = prob[:, :, :].rearrange("p a c -> p (a c)")
        tern = prob_flat[:, 0:3 * P].rearrange("p (n d) -> p n d", n=3)
        mask32 = prob_flat[:, 3 * P:4 * P]
        rows = v1[0:ROWS, 0, 0:P]
        head_sum = prob_flat[:, 4 * P:5 * P]
        blank = prob_flat[:, 5 * P:5 * P + 4 * ROW].rearrange("p (t c) -> p t c", t=4)
        pick32 = probT[0:E, :, :].rearrange("p a c -> p (a c)").rearrange("p (e d) -> p e d", e=E)
        b2_32 = oT[0:E, 1, 0:2 * P].rearrange("p (n d) -> p n d", n=2)
        w2raw = v1[:, 1, 0:4 * P].rearrange("p (n i) -> p n i", n=4)
        lg = qT[:, :, :].rearrange("p a (b t e) -> p (a b) t e", b=2, e=E)
        flat1 = v1[:, :, :].rearrange("p t c -> p (t c)")
        hids = [flat1[:, c * CHUNK:(c + 2) * CHUNK].rearrange("p (h c) -> p h c", h=2) for c in (0, 5)]
        hb = flat1[:, 2 * CHUNK:4 * CHUNK].bitcast(HALF).rearrange("p (h n c) -> p h n c", h=2, n=2)
        x32 = flat1[:, 4 * CHUNK:5 * CHUNK].rearrange("p (b c) -> p b c", b=2)
        xb = kT[:, 0, :].bitcast(HALF).rearrange("p (b n c) -> p b n c", b=2, n=2)
        xg_b = [prob_flat[:, 2 * ROW * b:2 * ROW * (b + 1)]
                .rearrange("p (t c) -> p t c", t=2) for b in range(2)]
        y_sb = probT[:, 0, :].rearrange("p (b t d) -> p b t d", b=2, t=2)
        x16 = xnT[:, :].bitcast(HALF).rearrange("p (n c) -> p n c", n=2)
        q16 = qT[:, 0:2, :].rearrange("p a c -> p (a c)").bitcast(HALF).rearrange("p (b n c) -> p b n c", b=2, n=2)
        k16 = kT[:, :, :].rearrange("p a c -> p (a c)").bitcast(HALF).rearrange("p (b n c) -> p b n c", b=2, n=2)
        v16 = flat1.bitcast(HALF).rearrange("p (t n c) -> p t n c", t=TILES, n=2)
        p16 = [a[:, n, :].bitcast(HALF).rearrange("p (n c) -> p n c", n=2) for a, n in
               ((probT, 0), (probT, 1), (qT, 2), (qT, 3))]
        o16 = oT[:, :, :].rearrange("p a c -> p (a c)").bitcast(HALF).rearrange("p (b n c) -> p b n c", b=2, n=2)
        v2 = flat1[:, 0:CHUNK].rearrange("p (t d) -> p t d", t=TILES)
        q_raw = flat1[:, CHUNK:CHUNK + CHUNK // 2].bitcast(HALF)
        rsum = flat1[:, CHUNK + 320:CHUNK + 320 + TILES * HEADS].rearrange("p (t h) -> p t h", t=TILES)
        sums = flat1[:, CHUNK + 384:CHUNK + 384 + TILES * HEADS].rearrange("p (t h) -> p t h", t=TILES)
        parts = flat1[:, 2 * CHUNK:4 * CHUNK].bitcast(HALF).rearrange("p (n c) -> p n c", n=4)
        turned_q = flat1[:, 4 * CHUNK:4 * CHUNK + CHUNK // 2].bitcast(HALF)
        turned_k = flat1[:, 4 * CHUNK + CHUNK // 2:5 * CHUNK].bitcast(HALF)
        rot = flat1[:, 5 * CHUNK:7 * CHUNK].rearrange("p (h c) -> p h c", h=2)
        rotated = flat1[:, 7 * CHUNK:8 * CHUNK]
        shared_h = rot
        cT3 = oT[:, 1, :]
        q_stack = qT[:, :, :].rearrange("p a c -> p (a c)").bitcast(HALF).rearrange("p (b j c) -> p b j c", b=2, j=4)
        k_stack = kT[:, :, :].rearrange("p a c -> p (a c)").bitcast(HALF).rearrange("p (g c) -> p g c", g=4)
        o_tok, oT2 = tmp[:, 1, :], tmp[:, 0, :]
        ahead = {}
        for layer, free in ((2, wm), (3, wm2)):
            place = free[:, 0, 0, :]
            ahead[layer] = {"xT": place[:, 0:2 * CHUNK].bitcast(F32), "v": place[:, 2 * CHUNK:4 * CHUNK].bitcast(F32),
                            "q": place[:, 4 * CHUNK:5 * CHUNK], "k": place[:, 5 * CHUNK:6 * CHUNK]}
        pick_rows = region[:, 3072:4096].bitcast(HALF).rearrange("p (n g r c) -> p n g r c", n=4, g=4, r=4)
        xd_flat = xd[:, :, :].rearrange("p t c -> p (t c)")[:, 0:PIECES * P]

        acc = bank("acc")
        mo = [bank("mo0"), bank("mo1")]
        sco = [bank("sco0"), bank("sco1")]
        pt = bank("pt")
        ob = bank("ob")
        misc = bank("misc")
        pts = [pt, mo[1]]
        scos = [sco[0], sco[1], mo[0]]

        x_in = sem("x_in")
        const_in = sem("const_in")
        att_in = [sem(f"att{n}_in") for n in range(4)]
        exp_in = [sem(f"exp{n}_in") for n in range(4)]
        y_out = sem("y_out")
        blank_sent = sem("blank_sent")
        rows_sent = [sem(f"rows{n}_sent") for n in range(4)]
        xg_in = [sem("xg0_in"), sem("xg1_in")]
        y_sent = [sem("y0_sent"), sem("y1_sent")]
        yc_in = [sem("yc0_in"), sem("yc1_in")]
        setup_pe = sem("setup_pe")
        setup_v = sem("setup_v")
        setup_a = sem("setup_a")
        setup_g = sem("setup_g")
        hi_made = sem("hi_made")
        lo_made = sem("lo_made")
        w1_high = sem("w1_high")
        w1_low = sem("w1_low")
        w3_prep = sem("w3_prep")
        rows_pick = sem("rows_pick")
        done = {name: sem(f"{name}_stages") for name in ("pe", "act", "dve", "pool")}
        passed_v = sem("passed_v")
        passed_g = sem("passed_g")
        ln_stats = event("ln_stats", N0=9, L0=9, C1=9, C2=9)
        rstd_made = sem("rstd_made")
        xn_made = event("xn_made", L0=4, R=8, A=4)
        xn_turned = event("xn_turned", L0=1, R=1, A=1)
        xT_made = event("xT_made", L0=1, R=1, A=1)
        proj_full = event("proj_full", L0=4, A1=8, A2=3, A3=8)
        proj_read_a = event("proj_read_a", L0=4, A1=8, A2=2, A3=3)
        proj_read_v = event("proj_read_v", L0=2, A1=8, A2=3, A3=14)
        lg_full = event("lg_full", R=1)
        lg_made = event("lg_made", T=1)
        route = event("route", T1=49, T2=38, T3=49)
        route_exp = event("route_exp", T=1)
        ranks_full = event("ranks_full", T=1)
        xT_low = event("xT_low", A1=1)
        q_high = event("q_high", A1=8)
        k_high = event("k_high", A1=8)
        probT_high = event("probT_high", A1=32)
        oT_high = event("oT_high", A1=8)
        q_full = event("q_full", A1=8)
        q_made = event("q_made", A1=8)
        k_full = event("k_full", A1=8)
        k_made = event("k_made", A1=8)
        s_full = event("s_full", A=32)
        nmax_made = event("nmax_made", A=32)
        exp_made = event("exp_made", A=32)
        rrow_made = event("rrow_made", A1=32)
        scale_made = event("scale_made", A1=32)
        prob_turned = event("prob_turned", A=32)
        probT_made = event("probT_made", A=32)
        av_full = event("av_full", A=32)
        oT_made = event("oT_made", A1=8, A2=1, A3=1)
        moved = event("moved", A2=1, A3=4)
        sel_full = event("sel_full", A2=8, A3=8)
        stacked = event("stacked", A2=8, A3=8)
        masked = event("masked", A2=4, A3=4)
        o_scaled = event("o_scaled", A2=2, A3=2)
        o_turned = event("o_turned", A2=1, A3=1)
        out_done = event("out_done", A1=7)
        sh_up = event("sh_up", A3=FB)
        sh_act = event("sh_act", A3=FB)
        sh_down = event("sh_down", A3=FB)
        acc_full = event("acc_full", L0=1, A=1)
        yT_made = event("yT_made", L0=1, A1=1)
        y_turned = event("y_turned", L0=1, A1=1)
        x_made = event("x_made", L0=1, A=1, C=1)
        xg_turned = event("xg_turned", M=1)
        dest_f_made = event("dest_f_made", M=2)
        dest_made = event("dest_made", M=1)
        xh_made = event("xh_made", M=1)
        xl_made = event("xl_made", M1=1, M2=2, M3=1)
        up_full = event("up_full", M=2)
        gate_full = event("gate_full", M1=2)
        act_made = event("act_made", M=2)
        gated = event("gated", M1=4)
        hh_made = event("hh_made", M=2)
        hl_made = event("hl_made", M=2)
        down_done = event("down_done", M=2)
        y_made = event("y_made", M=1)
        c_step = event("c_step", C1=1, C3=1)

        ORDER = ["L0"] + [f"{s}{l}" for l in (1, 2, 3) for s in "RTAMC"]

        def stage_closed(eng, stage):
            for engine_done in done.values():
                eng.wait_ge(engine_done, ORDER.index(stage) + 1)

        def parity_tiles(layer, b):
            return sum((SLOT_TILES[l] + 1 - b) // 2 for l in TOP if l < layer)

        def results_sent(eng, layer, b, tiles):
            count = tiles * 32 + 32 * parity_tiles(layer, b)
            if not (isinstance(count, int) and count == 0):
                eng.wait_ge(y_sent[b], count)

        CHOSEN = {1: 12, 2: 4, 3: 12}
        N_ATT = [8, 4, 0, 10]

        def split_from(layer):
            return {1: [(load2[:, :], 0), (xd_flat, 1), (flat1, 2)], 2: [(xd_flat, 0), (load2[:, :], 1)],
                    3: [(xd_flat, 0), (load2[:, :], 2)]}[layer]

        SPLITS = {1: 3, 2: 5, 3: 7}
        DOWN = {1: 2, 2: 1, 3: 2}

        def unit1(u):
            return u // 4, (u // 2) % 2, u % 2

        def last_chunk_apart(eng, chunk):
            with eng.Fori(0, NCH - 1) as i:
                chunk(i, True)
            chunk(NCH - 1, False)

        AHEAD = 17

        def unit2(u):
            return u // 8, (u // 4) % 2, u % 4

        CONSTS = [(ident[:, :], "ident"), (mask32, "causal"), (head_sum, "head_sum"),
                  (head_pick[:, :], "head_pick"), (pick32[:, :, :], "expert_pick"), (rank_w[:, :], "rank_w"),
                  (cos_t[:, :], "cos_t"), (sin_t[:, :], "sin_t"), (before[:, :], "before"),
                  (before_e[:, :, :], "before_e"), (multiples[:, :], "multiples"), (tile_no[:, :], "tile_no"),
                  (token_id[:, :], "token_id"), (blank, "blank")]
        N_CONST = len(CONSTS) + 3 + len(VECTORS) + 8

        block = ctx.enter_context(nc.Block())

        @block.sync
        def _(sp):
            def load(dst, src, s):
                sp.dma_start(dst, src).then_inc(s, 16)

            def load_up(dst, src, s):
                load(dst.rearrange("p (e f) -> p e f", e=E), src.rearrange("e d f -> d e f"), s)

            def load_down(dst, src, s):
                load(dst.rearrange("p (n d) -> p n d", d=P),
                     src.rearrange("e f d -> (e f) d").rearrange("(n p) d -> p n d", p=P), s)

            x_src = A["L0_attn_x"].rearrange("b s d -> (b s) d").rearrange("(c t p) d -> c p t d", p=P, t=TILES)
            load(x[:, 0:TILES, :], x_src[0], x_in)
            for dst, name in CONSTS:
                load(dst, A[name], const_in)
            load(rows[ROW_B1_2:ROW_B1_2 + PIECES, :], A["L2_ffn_b1"].rearrange("e (b p) -> (e b) p", p=P), const_in)
            load(rows[ROW_B1_3:ROW_B1_3 + PIECES, :], A["L3_ffn_b1"].rearrange("e (b p) -> (e b) p", p=P), const_in)
            load(rows[ROW_BS1:ROW_BS1 + FB, :], A["L3_ffn_bs1"].rearrange("(b p) -> b p", p=P), const_in)
            for name in VECTORS:
                load(rows[COL[name]:COL[name] + 1, :], A[name].rearrange("(a p) -> a p", a=1), const_in)
            for n, name in enumerate(("L1_ffn_gate_b", "L2_ffn_br", "L3_ffn_gate_b")):
                load(rb[:, n, :], A[name].rearrange("(a p) -> a p", a=1).broadcast_to([P, E]), const_in)
            for n, name in enumerate(("L1_ffn_gate_w", "L2_ffn_Wr", "L3_ffn_gate_w")):
                load(wr[:, n, :], A[name], const_in)
            for n, name in enumerate(("L2_ffn_b2", "L3_ffn_b2")):
                load(b2_32[:, n, :], A[name], const_in)
            load(tern[:, 0, :], A["L0_ffn_weight"], att_in[0])
            load(alpha, A["L0_ffn_alpha"].rearrange("(a p) -> a p", a=1).broadcast_to([P, 1]), att_in[0])
            for n, name in enumerate(("Wq", "Wk", "Wv", "Wo")):
                load(w0[:, n, :], A["L0_attn_" + name], att_in[0])
            load(w2raw[:, 0:3, :], A["L2_attn_w_qkv"].rearrange("(n p) i -> p n i", p=P), att_in[0])
            load(w2raw[:, 3, :], A["L2_attn_w_out"], att_in[0])
            for c in range(1, NCH):
                load(x[:, TILES * c:TILES * (c + 1), :], x_src[c], x_in)
            load_up(load2[:, :], A["L1_ffn_w1"], exp_in[1])
            load_up(xd_flat, A["L1_ffn_w3"], exp_in[1])
            sp.wait_ge(setup_pe, 3)
            load_down(flat1, A["L1_ffn_w2"], exp_in[1])
            load(region[:, W1Q:W1Q + 1024], A["L1_attn_wq"].rearrange("d h e -> d (h e)"), att_in[1])
            load(region[:, W1K:W1K + 1024], A["L1_attn_wk"].rearrange("d h e -> d (h e)"), att_in[1])
            load(region[:, W1V:W1V + 1024], A["L1_attn_wv"].rearrange("d h e -> d (h e)"), att_in[1])
            load(region[:, W1O:W1O + 1024].rearrange("p (j d) -> p j d", j=8), A["L1_attn_w_out"].rearrange("h e d -> (h e) d").rearrange("(j p) d -> p j d", p=P), att_in[1])
            sp.wait_ge(const_in, 16 * N_CONST)
            for l in TOP:
                dst = slot_rows[l].rearrange("(t p) c -> p t c", p=P)
                for t in range(4):
                    n = len(range(t, SLOT_TILES[l] * SLOTS // P, 4))
                    sp.dma_start(dst[:, t:SLOT_TILES[l] * SLOTS // P:4, :],
                                 blank[:, t:t + 1, :].broadcast_to([P, n, ROW])).then_inc(blank_sent, 16)

            def feed_experts(layer):
                sp.wait_ge(rows_sent[layer], 16 * ALL * TOP[layer])
                stage_closed(sp, f"A{layer}")

                def step(s, half, b, first):
                    if not first:
                        xg_turned.wait(sp, f"M{layer}", s - 2)
                        dest_f_made.wait(sp, f"M{layer}", s - 2, 1)
                    sp.dma_start(xg_b[b], slot_rows[layer][bass.ds(s * SLOTS, SLOTS), :]
                                 .rearrange("(t p) c -> p t c", p=P)).then_inc(xg_in[b], 16)

                slot_tiles(sp, layer, step)

            def feed_combine(layer):
                for b in range(2):
                    sp.wait_ge(y_sent[b], 32 * parity_tiles(layer + 1, b))
                stage_closed(sp, f"M{layer}")

                def step(c, half, b, first):
                    if not first:
                        x_made.wait(sp, f"C{layer}", c - 2)
                    for j in range(TOP[layer]):
                        sp.dma_start(qT[:, 2 * b + j, :].rearrange("p (t d) -> p t d", t=TILES),
                                     results[layer][bass.ds(c * CHUNK + TOKENS * j, CHUNK), :]
                                     .rearrange("(t p) d -> p t d", p=P)).then_inc(yc_in[b], 16)

                chunk_pairs(sp, step)

            sp.wait_ge(rows_sent[1], 16 * ALL * TOP[1])
            stage_closed(sp, "T1")
            load_up(xd_flat, A["L2_ffn_W1"], exp_in[2])
            load_down(load2[:, :], A["L2_ffn_W2"], exp_in[2])
            feed_experts(1)
            for dst, name in ((w3d, "W_kv_down"), (w3k, "W_k_up"), (w3v, "W_v_up"), (w3q, "W_q"), (w3o, "W_o"),
                              (w3qr, "W_q_rope"), (w3kr, "W_k_rope")):
                load(dst, A["L3_attn_" + name], att_in[3])
            load(ws1, A["L3_ffn_ws1"], att_in[3])
            load(bs2_row, A["L3_ffn_bs2"].rearrange("(a p) -> a p", a=1), att_in[3])
            load(ws2, A["L3_ffn_ws2"].rearrange("(n p) d -> p n d", p=P), att_in[3])
            feed_combine(1)
            sp.wait_ge(rows_sent[2], 16 * ALL * TOP[2])
            stage_closed(sp, "T2")
            load_up(xd_flat, A["L3_ffn_w1"], exp_in[3])
            load_down(load2[:, :], A["L3_ffn_w2"], exp_in[3])
            feed_experts(2)
            feed_combine(2)
            feed_experts(3)
            feed_combine(3)
            y_dst = out.rearrange("b s d -> (b s) d").rearrange("(c t p) d -> c p t d", p=P, t=TILES)
            for c in range(NCH):
                x_made.wait(sp, "C3", c)
                sp.dma_start(y_dst[c], x[:, TILES * c:TILES * (c + 1), :]).then_inc(y_out, 16)
            sp.wait_ge(y_out, 16 * NCH)

        @block.gpsimd
        def _(pool):
            pool.memset(pow_half[:, :], -0.5).then_inc(setup_g, 1)
            pool.wait_ge(setup_g, 1)

            def norms(layer):
                count = 1 + 2 * layer + (5 if layer > 1 else 0) + (5 if layer > 2 else 0)

                def link(ins):
                    nonlocal count
                    ins.then_inc(setup_g, 1)
                    pool.wait_ge(setup_g, count + 1)
                    count += 1

                before_stage = {0: "N0", 1: "L0", 2: "C1", 3: "C2"}[layer]
                ln_stats.wait(pool, before_stage, NCH - 1, 8)
                link(pool.tensor_scalar(rstd[:, 0, :], mv[:, :, 1], LN_EPS, None, ALU.add))
                last = pool.tensor_tensor(rstd[:, 1, :], rstd[:, 0, :], pow_half[:, :], ALU.pow)
                if layer in (1, 2):
                    link(last)
                    link(pool.tensor_tensor(rstd[:, 2, :], rstd[:, 1, :], rstd[:, 1, :], ALU.mult))
                    link(pool.tensor_tensor(rstd[:, 0, :], rstd[:, 2, :], mv[:, :, 1], ALU.mult))
                    link(pool.tensor_scalar(rstd[:, 2, :], rstd[:, 0, :], RMS_EPS if layer == 1 else LN_EPS,
                                            None, ALU.add))
                    link(pool.tensor_tensor(rstd[:, 0, :], rstd[:, 2, :], pow_half[:, :], ALU.pow))
                    last = pool.tensor_tensor(rstd[:, 3, :], rstd[:, 1, :], rstd[:, 0, :], ALU.mult)
                link(last)
                pool.sem_inc(rstd_made, 1)

            def dispatch(layer):
                stage_closed(pool, f"T{layer}")
                pool.wait_ge(blank_sent, 16 * 4 * len(TOP))
                for j in range(TOP[layer]):
                    for t in range(ALL):
                        pool.indirect_dma_start(
                            out=slot_rows[layer], out_offset=bass.IndirectOffsetOnAxis(ap=slot_no[:, j, t:t + 1], axis=0),
                            in_=xd[:, t, :], in_offset=None).then_inc(rows_sent[layer], 16)

            def send_results(layer):
                def step(s, half, b, first):
                    y_made.wait(pool, f"M{layer}", s)
                    dest_made.wait(pool, f"M{layer}", s)
                    pool.sem_inc(passed_g, 1)
                    for t in range(2):
                        pool.indirect_dma_start(
                            out=results[layer],
                            out_offset=bass.IndirectOffsetOnAxis(ap=dest_no[:, 2 * b + t:2 * b + t + 1], axis=0),
                            in_=y_sb[:, b, t, :], in_offset=None).then_inc(y_sent[b], 16)

                slot_tiles(pool, layer, step)

            norms(0)
            pool.sem_inc(done["pool"], 1)
            for layer in (1, 2, 3):
                norms(layer)
                pool.sem_inc(done["pool"], 1)
                pool.sem_inc(done["pool"], 1)
                dispatch(layer)
                pool.sem_inc(done["pool"], 1)
                if layer == 2:
                    pool.wait_ge(att_in[3], 16 * N_ATT[3])
                    for n, w in ((0, w3qr), (2, w3kr)):
                        for r in range(4):
                            pool.tensor_copy(rope_w[:, n, r, :], w)
                            pool.tensor_copy(rope_w[:, n + 1, r, 0:16], w[:, 16:32])
                            last = pool.tensor_copy(rope_w[:, n + 1, r, 16:32], w[:, 0:16])
                    last.then_inc(w3_prep, 1)
                send_results(layer)
                pool.sem_inc(done["pool"], 1)
                if layer == 1:
                    pool.memset(pick_rows, 0.0).then_inc(rows_pick, 1)
                    pool.wait_ge(rows_pick, 1)
                    blocks = ident[:, :].rearrange("p (g c) -> p g c", g=4)
                    for part, r in ((0, 0), (0, 1), (1, 2), (1, 3), (2, 0), (2, 2), (3, 1), (3, 3)):
                        pool.tensor_copy(pick_rows[:, part, :, r, :], blocks).then_inc(rows_pick, 1)
                pool.sem_inc(done["pool"], 1)

        @block.scalar
        def _(act):
            def copy(dst, src):
                return act.activation(dst, src, ACT.Copy)

            act.wait_ge(att_in[0], 16 * N_ATT[0])
            act.activation(tern[:, 1, :], tern[:, 0, :], ACT.Abs, accum_out=tsum[:, 0:1]).then_inc(setup_a, 1)
            act.wait_ge(setup_pe, 1)
            copy(cols[:, :], misc[:, 0:ROWS]).then_inc(setup_a, 1)
            act.wait_ge(setup_pe, 2)
            copy(tsum[:, 1:2], misc[:, 0:1]).then_inc(setup_a, 1)
            act.wait_ge(setup_pe, 3)
            copy(w2t[:, :, :], mo[0][:, :].rearrange("p (n i) -> p n i", n=4)).then_inc(setup_a, 1)
            act.wait_ge(setup_pe, 4)
            copy(w0f, misc[:, 0:P]).then_inc(setup_a, 1)
            act.wait_ge(setup_a, 5)

            def split(layer):
                act.wait_ge(exp_in[layer], 16 * len(split_from(layer)))
                for src, n in split_from(layer):
                    copy(experts[layer][:, 0, n, :], src).then_inc(hi_made, 1)

            def turned(stage, i):
                xn_turned.wait(act, stage, i, 0)
                if stage == "A1":
                    ins = act.activation(x16[:, 0, :], misc[:, :], ACT.Identity,
                                         scale=cols[:, COL["L1_attn_norm_scale"]:COL["L1_attn_norm_scale"] + 1])
                else:
                    ins = copy(xnT[:, :], misc[:, :])
                ins.then_inc(xT_made.sem, 1)

            def finish(stage, i):
                acc_full.wait(act, stage, i, 0)
                bias = {"L0": bias0[:, 0:1], "A1": cols[:, COL["L1_attn_b_out"]:COL["L1_attn_b_out"] + 1],
                        }.get(stage)
                ins = copy(yT, acc[:, :]) if bias is None else \
                    act.activation(yT, acc[:, :], ACT.Identity, bias=bias)
                ins.then_inc(yT_made.sem, 1)

            def exps(stage, i, u):
                nmax_made.wait(act, stage, i, u)
                if u >= 3:
                    prob_turned.wait(act, stage, i, u - 3)
                for qt in range(2):
                    lo, hi = (256 * qt, 256 * qt + 256) if stage == "A1" else (128 * qt, 128 + 256 * qt)
                    ins = act.activation(prob[:, u % 3, lo:hi], scos[u % 3][:, lo:hi], ACT.Exp,
                                         bias=nmax[:, u % 4, qt:qt + 1], accum_out=psum_row[:, u % 4, qt:qt + 1])
                ins.then_inc(exp_made.sem, 1)

            def turn_prob(stage, i, u):
                prob_turned.wait(act, stage, i, u)
                if u >= 4:
                    av_full.wait(act, stage, i, u - 4)
                copy(p16[u % 4][:, 0, :], pts[u % 2][:, :]).then_inc(probT_high.sem, 1)

            with act.Fori(0, NCH) as i:
                turned("L0", i)
                ch = Chain(act, proj_read_a, "L0", i)
                for n, name in enumerate(("L0_attn_bq", "L0_attn_bk")):
                    proj_full.wait(act, "L0", i, n)
                    ch.last(act.activation((oT[:, 0, :], yT)[n], sco[n][:, :], ACT.Square,
                                           bias=cols[:, COL[name]:COL[name] + 1]))
                proj_full.wait(act, "L0", i, 2)
                ch.last(act.activation(kT[:, 0, :], pt[:, :], ACT.Identity,
                                       bias=cols[:, COL["L0_attn_bv"]:COL["L0_attn_bv"] + 1]))
                proj_read_v.wait(act, "L0", i, 0)
                ch.last(act.activation(qT[:, 1, :], qT[:, 0, :], ACT.Exp, scale=-0.5))
                ch.close()
                finish("L0", i)
            act.sem_inc(done["act"], 1)
            split(1)
            act.wait_ge(att_in[1], 16 * N_ATT[1])
            copy(w1[:, 0, :], region[:, :]).then_inc(w1_high, 1)

            def router(layer):
                stage = f"R{layer}"
                def turned_chunk(i, first):
                    xn_turned.wait(act, stage, i)
                    if not first:
                        lg_full.wait(act, stage, i - 1)
                    copy(xnT[:, :], pt[:, :]).then_inc(xT_made.sem, 1)

                turned_chunk(0, True)
                with act.Fori(0, NCH - 1) as i:
                    turned_chunk(i + 1, False)
                act.sem_inc(done["act"], 1)
                if layer == 2:
                    route.wait(act, "T2", 0, 5)
                    act.activation(lg[:, 4, :, :], lg[:, 3, :, :], ACT.Exp).then_inc(route_exp.sem, 1)
                else:
                    route.wait(act, f"T{layer}", 0, 11)
                    act.activation(sc[:, 3, :], sc[:, 2, :], ACT.Exp).then_inc(route_exp.sem, 1)
                act.sem_inc(done["act"], 1)

            def experts_act(layer):
                stage = f"M{layer}"
                last = SLOT_TILES[layer] - 1

                def turned_rows(s, b):
                    xg_turned.wait(act, stage, s)
                    src = pt[:, SLOTS * b:SLOTS * (b + 1)]
                    if layer == 2:
                        ins = act.activation(x32[:, b, :], src, ACT.Identity,
                                             scale=cols[:, COL["L2_ffn_ln_g"]:COL["L2_ffn_ln_g"] + 1],
                                             bias=cols[:, COL["L2_ffn_ln_b"]:COL["L2_ffn_ln_b"] + 1])
                    else:
                        ins = copy(xb[:, b, 0, :], src)
                    ins.then_inc(xh_made.sem, 1)

                def hidden_high(s, h):
                    gated.wait(act, stage, s, 2 * h + 1)
                    copy(hb[:, h, 0, :], hids[0][:, h, :]).then_inc(hh_made.sem, 1)

                def keep_y(s, b):
                    down_done.wait(act, stage, s, 1)
                    copy(y_sb[:, b, :, :], (ob, misc)[b][:, 0:2 * P].rearrange("p (t d) -> p t d", t=2))\
                        .then_inc(y_made.sem, 1)

                stage_closed(act, f"A{layer}")
                turned_rows(0, 0)

                def step(s, half, b, first):
                    end = isinstance(s, int) and s == last
                    start = isinstance(s, int) and s == 0
                    if layer > 1:
                        e = act.value_load(tile_ei[0:1, bass.ds(s, 1)], min_val=0, max_val=E - 1)
                    for h in range(2):
                        up_full.wait(act, stage, s, h)
                        if layer == 1:
                            if not start:
                                gated.wait(act, stage, s - 1, 2 * h)
                            ins = act.activation(hids[1][:, h, :], sco[h][:, :], ACT.Tanh, scale=0.5)
                        else:
                            if not first:
                                hl_made.wait(act, stage, s - 2, h)
                            for f in range(2):
                                at = (ROW_B1_2 if layer == 2 else ROW_B1_3) + 2 * h + f
                                ins = act.activation(hids[b][:, h, SLOTS * f:SLOTS * (f + 1)],
                                                     sco[h][:, SLOTS * f:SLOTS * (f + 1)],
                                                     ACT.Relu if layer == 2 else ACT.Gelu,
                                                     bias=cols[:, bass.ds(e * FB + at, 1)])
                        ins.then_inc(act_made.sem, 1)
                        if h == 0:
                            if not (start or (isinstance(s, int) and s == 1)):
                                y_sent_before(act, b, half)
                                keep_y(s - 2, b)
                            if layer == 1 and not start:
                                if not first:
                                    down_done.wait(act, stage, s - 2, 1)
                                hidden_high(s - 1, 1)
                            if not end:
                                if not start:
                                    up_full.wait(act, stage, s - 1, 1)
                                    if layer == 1:
                                        gate_full.wait(act, stage, s - 1, 1)
                                    if layer == 2:
                                        xl_made.wait(act, stage, s - 1, 1)
                                turned_rows(s + 1, 1 - b)
                        elif layer == 1:
                            if not start:
                                down_done.wait(act, stage, s - 1, 0)
                            hidden_high(s, 0)

                def y_sent_before(eng, b, half):
                    results_sent(eng, layer, b, half - 1)

                slot_tiles(act, layer, step)
                if layer == 1:
                    down_done.wait(act, stage, last - 1, 1)
                    hidden_high(last, 1)
                y_sent_before(act, 1, last // 2)
                keep_y(last - 1, 1)
                y_sent_before(act, 0, last // 2 + 1)
                keep_y(last, 0)
                act.sem_inc(done["act"], 1)

            def attention(layer):
                stage = f"A{layer}"

                def stack(i, n):
                    g, kind = n // 2, n % 2
                    sel_full.wait(act, stage, i, n)
                    if kind == 0 and g:
                        masked.wait(act, stage, i, g - 1)
                    copy(k_stack[:, g, :] if kind else q_raw, (acc if n == 0 else misc)[:, :]).then_inc(stacked.sem, 1)

                def high(i, n, at, src, scale):
                    proj_full.wait(act, stage, i, at)
                    act.activation(parts[:, n, :], src[:, :], ACT.Copy, scale=scale).then_inc(proj_read_a.sem, 1)

                def prepare(i, s):
                    if s == (21 if layer == 2 else 19):
                        xn_turned.wait(act, stage, i)
                        copy(ahead[layer]["xT"], acc[:, :]).then_inc(xT_made.sem, 1)
                    if layer == 2:
                        if s == 23:
                            high(i, 0, 0, misc, SCALE2)
                            high(i, 2, 1, acc, 1.0)
                        if s == 26:
                            stack(i, 0)
                        if s == 28:
                            stack(i, 1)
                    else:
                        if s == 21:
                            proj_full.wait(act, stage, i, 0)
                            copy(cT3, acc[:, :]).then_inc(proj_read_a.sem, 1)
                        if s == 22:
                            high(i, 0, 1, misc, SCALE3)
                        if s == 25:
                            high(i, 2, 4, acc, 1.0)
                        if s == 30:
                            stack(i, 0)
                        if s == 31:
                            stack(i, 1)

                def chunk(i, more):
                    for s in range(UNITS):
                        nmax_made.wait(act, stage, i, s)
                        if s >= 3:
                            prob_turned.wait(act, stage, i, s - 3)
                        g, b, j = unit2(s)
                        for qt in range(2):
                            lo, hi = 128 * qt, 128 + 256 * qt
                            ins = act.activation(prob[:, s % 3, lo:hi], scos[s % 3][:, lo:hi], ACT.Exp,
                                                 bias=nmax[:, s % 4, qt:qt + 1],
                                                 accum_out=sums[:, 2 * b + qt, 4 * g + j:4 * g + j + 1])
                        ins.then_inc(exp_made.sem, 1)
                        if s % 8 == 1 and g < 3:
                            stack(i, 2 * g + 2)
                        if s % 8 == 4 and g < 3:
                            stack(i, 2 * g + 3)
                        if more:
                            prepare(i + 1, s)
                    if layer == 3:
                        for s in range(FB):
                            sh_up.wait(act, stage, i, s)
                            if s >= 2:
                                sh_down.wait(act, stage, i, s - 2)
                            act.activation(shared_h[:, s % 2, :], sco[s % 2][:, :], ACT.Gelu,
                                           bias=cols[:, ROW_BS1 + s:ROW_BS1 + s + 1]).then_inc(sh_act.sem, 1)
                    o_turned.wait(act, stage, i)
                    copy(oT2, misc[:, :]).then_inc(oT_made.sem, 1)

                for s in range(AHEAD, UNITS):
                    prepare(0, s)
                last_chunk_apart(act, chunk)

            stage_closed(act, "L0")
            router(1)
            act.wait_ge(blank_sent, 16 * 4 * len(TOP))
            vb = [sco[0], sco[1], pt, ob]

            def q_evac(i, j):
                q_full.wait(act, "A1", i, j)
                act.activation(q16[:, j % 2, 0, :], misc[:, :], ACT.Copy, scale=SCALE1).then_inc(q_high.sem, 1)

            def k_evac(i, j):
                k_full.wait(act, "A1", i, j)
                copy(k16[:, j % 2, 0, :], misc[:, :]).then_inc(k_high.sem, 1)

            def prepare(i, s):
                if s == 31:
                    turned("A1", i)
                if s == 34:
                    q_evac(i, 0)
                if s == 36:
                    k_evac(i, 0)

            def keep_values(i):
                for n in range(8):
                    proj_full.wait(act, "A1", i, n)
                    copy(v16[:, n // 2, 0, 512 * (n % 2):512 * (n % 2) + 512], vb[n % 4][:, :])\
                        .then_inc(proj_read_a.sem, 1)

            def chunk(i, more):
                for s in range(UNITS + 5):
                    if s >= 8 and s % 4 == 0:
                        j = (s - 8) // 4
                        av_full.wait(act, "A1", i, 4 * j + 3)
                        if j >= 2:
                            out_done.wait(act, "A1", i, j - 2)
                        copy(o16[:, j % 2, 0, :], ob[:, :]).then_inc(oT_high.sem, 1)
                    if s < UNITS:
                        if s % 4 == 0 and s // 4 + 1 < 8:
                            q_evac(i, s // 4 + 1)
                        if s % 4 == 2 and s // 4 + 1 < 8:
                            k_evac(i, s // 4 + 1)
                        exps("A1", i, s)
                    if 2 <= s < UNITS + 2:
                        turn_prob("A1", i, s - 2)
                    if more:
                        prepare(i + 1, s)
                finish("A1", i)
                if more:
                    keep_values(i + 1)

            for s in range(AHEAD, UNITS + 5):
                prepare(0, s)
            keep_values(0)
            last_chunk_apart(act, chunk)
            act.sem_inc(done["act"], 1)
            split(2)
            experts_act(1)
            act.sem_inc(done["act"], 1)

            stage_closed(act, "C1")
            router(2)
            attention(2)
            act.sem_inc(done["act"], 1)
            split(3)
            experts_act(2)
            act.sem_inc(done["act"], 1)

            stage_closed(act, "C2")
            router(3)
            attention(3)
            act.sem_inc(done["act"], 1)
            experts_act(3)
            act.sem_inc(done["act"], 1)

        @block.tensor
        def _(pe):
            def mm(dst, lhsT, rhs, start, stop):
                return pe.matmul(dst, lhsT, rhs, start=start, stop=stop)

            def mm3(dst, left, right, start, stop):
                mm(dst, left(0), right(0), start, False)
                mm(dst, left(1), right(0), False, False)
                return mm(dst, left(0), right(1), False, stop)

            pe.wait_ge(const_in, 16 * N_CONST)
            pe.transpose(misc[:, 0:ROWS], rows[:, :], ident[0:ROWS, 0:ROWS]).then_inc(setup_pe, 1)
            pe.wait_ge(setup_a, 2)
            pe.wait_ge(setup_v, 1)
            mm(misc[:, 0:1], ones[:, :], tsum[:, 0:1], True, True).then_inc(setup_pe, 1)
            pe.wait_ge(att_in[0], 16 * N_ATT[0])
            for n in range(4):
                ins = pe.transpose(mo[0][:, n * P:(n + 1) * P], w2raw[:, n, :], ident[:, :])
            ins.then_inc(setup_pe, 1)
            pe.wait_ge(setup_v, 6)
            pe.transpose(misc[:, 0:P], tern[:, 2, :], ident[:, :]).then_inc(setup_pe, 1)
            pe.wait_ge(setup_a, 5)

            def turn_x(stage, i, dst=misc):
                xn_made.wait(pe, stage, i, 3)
                for t in range(TILES):
                    ins = pe.transpose(dst[:, t * P:(t + 1) * P], xn[:, t, :], ident[:, :])
                ins.then_inc(xn_turned.sem, 1)

            def finish(stage, i):
                yT_made.wait(pe, stage, i, 0)
                for t in range(TILES):
                    ins = pe.transpose(misc[:, t * P:(t + 1) * P], yT[:, t * P:(t + 1) * P], ident[:, :])
                ins.then_inc(y_turned.sem, 1)

            def router(layer):
                stage = f"R{layer}"
                stage_closed(pe, ORDER[ORDER.index(stage) - 1])

                def turn_chunk(i, first):
                    xn_made.wait(pe, stage, i, 7)
                    if not first:
                        xT_made.wait(pe, stage, i - 1)
                    for t in range(TILES):
                        ins = pe.transpose(pt[:, t * P:(t + 1) * P], xn[:, t, :], ident[:, :])
                    ins.then_inc(xn_turned.sem, 1)

                def logits(i):
                    xT_made.wait(pe, stage, i)
                    for t in range(TILES):
                        ins = mm(misc[:, bass.ds(i * (TILES * E) + t * E, E)], xnT[:, t * P:(t + 1) * P],
                                 wr[:, layer - 1, :], True, True)
                    ins.then_inc(lg_full.sem, 1)

                turn_chunk(0, True)
                with pe.Fori(0, NCH - 1) as i:
                    turn_chunk(i + 1, False)
                    logits(i)
                logits(NCH - 1)
                lg_made.wait(pe, f"T{layer}", 0)
                pe.sem_inc(done["pe"], 1)
                route.wait(pe, f"T{layer}", 0, CHOSEN[layer])
                chosen = lg[:, 1 if layer == 2 else 5, :, :].rearrange("p t e -> p (t e)")
                mm(misc[:, 0:ALL * E], before[:, :], chosen, True, True)
                mm(misc[:, ALL * E:2 * ALL * E], ones[:, :], chosen, True, True).then_inc(ranks_full.sem, 1)
                pe.sem_inc(done["pe"], 1)
                stage_closed(pe, f"T{layer}")

            def experts_pe(layer):
                stage = f"M{layer}"
                w = experts[layer]
                last = SLOT_TILES[layer] - 1
                xl_last = xl_made.per[stage] - 1

                def expert(s):
                    return pe.value_load(tile_ei[0:1, bass.ds(s, 1)], min_val=0, max_val=E - 1)

                def turn_rows(s, b, half, start):
                    pe.wait_ge(xg_in[b], half * 16 + 16 * (1 + parity_tiles(layer, b)))
                    if not start:
                        xl_made.wait(pe, stage, s - 2, xl_last)
                    for t in range(2):
                        ins = pe.transpose(pt[:, SLOTS * b + P * t:SLOTS * b + P * (t + 1)], xg_b[b][:, t, 0:P],
                                           ident[:, :])
                    ins.then_inc(xg_turned.sem, 1)

                def up(s, b, h, e, start):
                    if h == 0:
                        xl_made.wait(pe, stage, s, xl_last)
                    for n, bank_, full in ((0, sco[h], up_full), (1, mo[h], gate_full))[:2 if layer == 1 else 1]:
                        if not start:
                            if layer == 1:
                                gated.wait(pe, stage, s - 1, 2 * h + n)
                            else:
                                act_made.wait(pe, stage, s - 1, h)
                        for f in range(2):
                            at = (2 * h + f) * P
                            ins = mm3(bank_[:, SLOTS * f:SLOTS * (f + 1)],
                                      lambda hl: w[:, hl, n, bass.ds(e * (FB * P) + at, P)],
                                      lambda hl: xb[:, b, hl, :], True, True)
                        ins.then_inc(full.sem, 1)

                def down(s, b, h, e, start):
                    dst = (ob, misc)[b]
                    if h == 0 and not start:
                        y_made.wait(pe, stage, s - 2)
                    hl_made.wait(pe, stage, s, h)
                    for t in range(2):
                        y = dst[:, P * t:P * (t + 1)]
                        if h == 0 and layer > 1:
                            for hl in range(2):
                                mm(y, pick16[:, bass.ds(e * P, P)], b2[:, layer - 2, hl, :], t == 0 and hl == 0, False)
                        for f in range(2):
                            at = (2 * h + f) * P
                            ins = mm3(y, lambda hl: hb[:, h, hl, SLOTS * f + P * t:SLOTS * f + P * (t + 1)],
                                      lambda hl: w[:, hl, DOWN[layer], bass.ds(e * (FB * P) + at, P)],
                                      t == 0 and h == 0 and f == 0 and layer == 1, t == 1 and h == 1 and f == 1)
                    ins.then_inc(down_done.sem, 1)

                stage_closed(pe, f"A{layer}")
                pe.wait_ge(lo_made, SPLITS[layer])
                turn_rows(0, 0, 0, True)

                def step(s, half, b, e_before, e, load_next):
                    end = isinstance(s, int) and s == last
                    start = isinstance(s, int) and s == 0
                    e_next = None
                    for h in range(2):
                        up(s, b, h, e, start)
                        if h == 1 and load_next:
                            e_next = expert(s + 1)
                        if not start:
                            down(s - 1, 1 - b, h, e_before, isinstance(s, int) and s <= 2)
                        if h == 0 and not end:
                            turn_rows(s + 1, 1 - b, half + b, start)
                    return e_next

                def run(s, half, count):
                    e_before, e = None if isinstance(s, int) and s == 0 else expert(s - 1), expert(s)
                    for k in range(count):
                        e_before, e = e, step(s + k, half + k // 2, k % 2, e_before, e, k < count - 1)
                    return e_before

                assert last % 4 == 2
                run(0, 0, 4)
                with pe.Fori(0, (last - 6) // 4) as i:
                    run(i * 4 + 4, i * 2 + 2, 4)
                e = run(last - 2, (last - 2) // 2, 3)
                for h in range(2):
                    down(last, 0, h, e, False)
                pe.sem_inc(done["pe"], 1)

            def turn_prob(stage, i, u):
                scale_made.wait(pe, stage, i, u)
                if u >= 2:
                    probT_made.wait(pe, stage, i, u - 2)
                for kt in range(2):
                    for qt in range(2):
                        if stage == "A1":
                            dst, src = 256 * kt + 128 * qt, 256 * qt + 128 * kt
                        elif kt <= qt:
                            dst, src = 256 * kt + 128 * (qt - kt), 128 * qt + 128 * kt
                        else:
                            continue
                        ins = mm(pts[u % 2][:, dst:dst + P], prob[:, u % 3, src:src + P], scale_d[:, u % 2, qt, :],
                                 True, True)
                ins.then_inc(prob_turned.sem, 1)

            def attention(layer):
                stage = f"A{layer}"
                if layer == 2:
                    pe.wait_ge(rows_pick, 9)
                else:
                    pe.wait_ge(w3_prep, 1)
                    pe.wait_ge(att_in[3], 16 * N_ATT[3])
                xT = ahead[layer]["xT"]

                def project(dst, w, src):
                    mm(dst[:, :], w, src, True, True).then_inc(proj_full.sem, 1)

                def values(dst, src, w):
                    for t in range(TILES):
                        ins = mm(dst[:, t * P:(t + 1) * P], src[:, t * P:(t + 1) * P], w, True, True)
                    ins.then_inc(proj_full.sem, 1)

                def rope(dst, n, src):
                    project(dst, rope_w[:, n, :, :].rearrange("p r c -> p (r c)"), src)

                def select(i, n):
                    g, kind = n // 2, n % 2
                    dst = acc if n == 0 else misc
                    if n >= 2:
                        stacked.wait(pe, stage, i, n - 1)
                    mm(dst[:, :], pick_rows[:, 2 * kind, g, :, :].rearrange("p r c -> p (r c)"),
                       parts[:, 2 * kind, :], True, False)
                    mm(dst[:, :], pick_rows[:, 2 * kind + 1, g, :, :].rearrange("p r c -> p (r c)"),
                       parts[:, 2 * kind + 1, :], False, True).then_inc(sel_full.sem, 1)

                def prepare(i, s):
                    if s == (20 if layer == 2 else 18):
                        if not isinstance(i, int):
                            x_made.wait(pe, stage, i - 2)
                        turn_x(stage, i, acc)
                    if layer == 2:
                        if s == 22:
                            xT_made.wait(pe, stage, i)
                            if not isinstance(i, int):
                                stacked.wait(pe, stage, i - 1, 7)
                            project(misc, w2t[:, 0, :], xT)
                            project(acc, w2t[:, 1, :], xT)
                        if s == 25:
                            proj_read_v.wait(pe, stage, i, 0)
                            values(misc, xT, w2t[:, 2, :])
                            proj_read_v.wait(pe, stage, i, 1)
                            select(i, 0)
                        if s == 27:
                            proj_read_v.wait(pe, stage, i, 2)
                            select(i, 1)
                    else:
                        if s == 20:
                            xT_made.wait(pe, stage, i)
                            project(acc, w3d, xT)
                        if s == 21:
                            if not isinstance(i, int):
                                stacked.wait(pe, stage, i - 1, 7)
                            project(misc, w3q, xT)
                        if s == 22:
                            proj_read_a.wait(pe, stage, i, 0)
                            rope(acc, 0, xT)
                        if s == 24:
                            proj_read_v.wait(pe, stage, i, 0)
                            rope(misc, 1, xT)
                            proj_read_v.wait(pe, stage, i, 1)
                            project(acc, w3k, cT3)
                        if s == 26:
                            proj_read_v.wait(pe, stage, i, 2)
                            rope(misc, 2, cT3)
                        if s == 27:
                            proj_read_v.wait(pe, stage, i, 6)
                            rope(acc, 3, cT3)
                        if s == 28:
                            proj_read_v.wait(pe, stage, i, 7)
                            values(misc, cT3, w3v)
                        if s == 29:
                            proj_read_v.wait(pe, stage, i, 8)
                            select(i, 0)
                        if s == 30:
                            proj_read_v.wait(pe, stage, i, 13)
                            select(i, 1)

                def scores(i, u):
                    g, b, j = unit2(u)
                    if u % 8 == 0:
                        masked.wait(pe, stage, i, g)
                        stacked.wait(pe, stage, i, 2 * g + 1)
                    if u >= 3:
                        exp_made.wait(pe, stage, i, u - 3)
                    for qt in range(2):
                        dst = scos[u % 3][:, 128 * qt:128 + 256 * qt]
                        q0, w = SEQ * b + 128 * qt, 128 + 128 * qt
                        mm(dst, q_stack[:, g % 2, j, q0:q0 + P], k_stack[:, g, SEQ * b:SEQ * b + w], True, False)
                        if layer == 3:
                            mm(dst, turned_q[:, q0:q0 + P], turned_k[:, SEQ * b:SEQ * b + w], False, False)
                        ins = mm(scos[u % 3][:, 256 * qt:256 * qt + 128], ident16[:, :], mask16[:, :], False, True)
                    ins.then_inc(s_full.sem, 1)

                def turn(i, u):
                    exp_made.wait(pe, stage, i, u)
                    if u >= 2:
                        probT_made.wait(pe, stage, i, u - 2)
                    for at in (0, 128, 256):
                        ins = pe.transpose(pts[u % 2][:, at:at + P], prob[:, u % 3, at:at + P], ident[:, :])
                    ins.then_inc(prob_turned.sem, 1)

                def average(i, u):
                    g, b, j = unit2(u)
                    c = 8 * (4 * g + j)
                    probT_made.wait(pe, stage, i, u)
                    for qt in range(2):
                        dst = ob[:, P * (2 * b + qt) + c:P * (2 * b + qt) + c + 8]
                        for kt in range(qt + 1):
                            ins = mm(dst, probT[:, u % 2, (256 if kt else P * qt):(256 if kt else P * qt) + P],
                                     v2[:, 2 * b + kt, c:c + 8], kt == 0, kt == qt)
                    ins.then_inc(av_full.sem, 1)

                def chunk(i, more):
                    moved.wait(pe, stage, i, moved.per[stage] - 1)
                    for s in range(UNITS + 3):
                        if s < UNITS:
                            scores(i, s)
                            if s % 8 == 0 and s // 8 < 3:
                                select(i, 2 * (s // 8) + 2)
                            if s % 8 == 3 and s // 8 < 3:
                                select(i, 2 * (s // 8) + 3)
                            if more:
                                prepare(i + 1, s)
                        if 2 <= s < UNITS + 2:
                            turn(i, s - 2)
                        if s >= 3:
                            average(i, s - 3)
                    if more:
                        stacked.wait(pe, stage, i + 1, 1)
                    if layer == 3:
                        for t in range(TILES):
                            mm(acc[:, P * t:P * (t + 1)], ones[0:1, :], bs2_row, t == 0, False)
                        exp_made.wait(pe, stage, i, UNITS - 1)
                        for s in range(FB + 1):
                            if s < FB:
                                if s >= 2:
                                    sh_act.wait(pe, stage, i, s - 2)
                                mm(sco[s % 2][:, :], ws1[:, s * P:(s + 1) * P], xnT[:, :], True, True)\
                                    .then_inc(sh_up.sem, 1)
                            if s >= 1:
                                sh_act.wait(pe, stage, i, s - 1)
                                for t in range(TILES):
                                    ins = mm(acc[:, P * t:P * (t + 1)], shared_h[:, (s - 1) % 2, P * t:P * (t + 1)],
                                             ws2[:, s - 1, :], False, False)
                                ins.then_inc(sh_down.sem, 1)
                    o_scaled.wait(pe, stage, i, 1)
                    for t in range(TILES):
                        ins = pe.transpose(misc[:, t * P:(t + 1) * P], o_tok[:, t * P:(t + 1) * P], ident[:, :])
                    ins.then_inc(o_turned.sem, 1)
                    oT_made.wait(pe, stage, i)
                    for t in range(TILES):
                        ins = mm(acc[:, P * t:P * (t + 1)], oT2[:, P * t:P * (t + 1)], w2t[:, 3, :] if layer == 2 else w3o,
                                 layer == 2 and t == 0, t == TILES - 1)
                    ins.then_inc(acc_full.sem, 1)

                for s in range(AHEAD, UNITS):
                    prepare(0, s)
                last_chunk_apart(pe, chunk)

            with pe.Fori(0, NCH) as i:
                turn_x("L0", i)
                xT_made.wait(pe, "L0", i, 0)
                for n, dst in enumerate((sco[0], sco[1], pt)):
                    mm(dst[:, :], w0[:, n, :], xnT[:, :], True, True).then_inc(proj_full.sem, 1)
                mm(acc[:, :], w0f, xnT[:, :], True, False)
                proj_read_a.wait(pe, "L0", i, 3)
                mm(ob[:, :], head_sum, qT[:, 1, :], True, True).then_inc(proj_full.sem, 1)
                proj_read_v.wait(pe, "L0", i, 1)
                mm(acc[:, :], w0[:, 3, :], oT[:, 0, :], False, True).then_inc(acc_full.sem, 1)
                finish("L0", i)
            pe.sem_inc(done["pe"], 1)

            router(1)
            pe.wait_ge(w1_low, 1)

            def w1_block(offset, j):
                return lambda hl: w1[:, hl, offset + j * P:offset + (j + 1) * P]

            vb = [sco[0], sco[1], pt, ob]

            def values(i, n):
                t, half = n // 2, n % 2
                if n >= 4:
                    proj_read_v.wait(pe, "A1", i, n - 4)
                mm3(vb[n % 4][:, :], lambda hl: x16[:, hl, t * P:(t + 1) * P],
                    lambda hl: w1[:, hl, W1V + 512 * half:W1V + 512 * half + 512], True, True)\
                    .then_inc(proj_full.sem, 1)

            def q_proj(i, j):
                if j:
                    k_made.wait(pe, "A1", i, j - 1)
                mm3(misc[:, :], w1_block(W1Q, j), lambda hl: x16[:, hl, :], True, True).then_inc(q_full.sem, 1)

            def k_proj(i, j):
                q_made.wait(pe, "A1", i, j)
                mm3(misc[:, :], w1_block(W1K, j), lambda hl: x16[:, hl, :], True, True).then_inc(k_full.sem, 1)

            def scores(i, u):
                j, h, b = unit1(u)
                if u % 4 == 0:
                    q_made.wait(pe, "A1", i, j)
                    k_made.wait(pe, "A1", i, j)
                if u >= 3:
                    exp_made.wait(pe, "A1", i, u - 3)
                r = slice(HD1 * h, HD1 * (h + 1))
                for qt in range(2):
                    q0 = SEQ * b + P * qt
                    ins = mm3(scos[u % 3][:, 256 * qt:256 * qt + 256], lambda hl: q16[r, j % 2, hl, q0:q0 + P],
                              lambda hl: k16[r, j % 2, hl, SEQ * b:SEQ * (b + 1)], True, True)
                ins.then_inc(s_full.sem, 1)

            def av(i, u):
                j, h, b = unit1(u)
                if u % 4 == 0 and j:
                    oT_made.wait(pe, "A1", i, j - 1)
                probT_made.wait(pe, "A1", i, u)
                for kt in range(2):
                    head = 2 * j + h
                    ins = mm3(ob[HD1 * h:HD1 * (h + 1), SEQ * b:SEQ * (b + 1)],
                              lambda hl: v16[:, 2 * b + kt, hl, HD1 * head:HD1 * (head + 1)],
                              lambda hl: p16[u % 4][:, hl, 256 * kt:256 * kt + 256], kt == 0, kt == 1)
                ins.then_inc(av_full.sem, 1)

            def out_proj(i, j):
                oT_made.wait(pe, "A1", i, j)
                mm3(acc[:, :], w1_block(W1O, j), lambda hl: o16[:, j % 2, hl, :], j == 0, j == 7)\
                    .then_inc((acc_full if j == 7 else out_done).sem, 1)

            def prepare(i, s):
                if s == 30:
                    if not isinstance(i, int):
                        k_made.wait(pe, "A1", i - 1, 7)
                    turn_x("A1", i)
                if s == 33:
                    xT_low.wait(pe, "A1", i)
                    q_proj(i, 0)
                if s == 35:
                    k_proj(i, 0)

            def chunk(i, more):
                proj_read_v.wait(pe, "A1", i, 7)
                for s in range(UNITS + 6):
                    if s < UNITS:
                        if s % 4 == 0 and s // 4 + 1 < 8:
                            q_proj(i, s // 4 + 1)
                        if s % 4 == 2 and s // 4 + 1 < 8:
                            k_proj(i, s // 4 + 1)
                        scores(i, s)
                    if more:
                        prepare(i + 1, s)
                    if 2 <= s < UNITS + 2:
                        turn_prob("A1", i, s - 2)
                    if 4 <= s < UNITS + 4:
                        av(i, s - 4)
                    if s >= 9 and s % 4 == 1:
                        out_proj(i, (s - 9) // 4)
                if more:
                    for n in range(4):
                        values(i + 1, n)
                    k_made.wait(pe, "A1", i + 1, 0)
                finish("A1", i)
                if more:
                    for n in range(4, 8):
                        values(i + 1, n)

            for s in range(AHEAD, UNITS + 6):
                prepare(0, s)
            for n in range(8):
                values(0, n)
            last_chunk_apart(pe, chunk)
            pe.sem_inc(done["pe"], 1)
            experts_pe(1)
            pe.sem_inc(done["pe"], 1)

            router(2)
            attention(2)
            pe.sem_inc(done["pe"], 1)
            experts_pe(2)
            pe.sem_inc(done["pe"], 1)

            router(3)
            attention(3)
            pe.sem_inc(done["pe"], 1)
            experts_pe(3)
            pe.sem_inc(done["pe"], 1)

        @block.vector
        def _(dve):
            dve.memset(ones[:, :], 1.0).then_inc(setup_v, 1)
            dve.wait_ge(const_in, 16 * N_CONST)
            dve.wait_ge(setup_a, 3)
            dve.tensor_scalar(tsum[:, 2:3], tsum[:, 1:2], 0.7 / (P * P), None, ALU.mult).then_inc(setup_v, 1)
            dve.tensor_scalar(tsum[:, 3:4], tsum[:, 1:2], -0.7 / (P * P), None, ALU.mult).then_inc(setup_v, 1)
            dve.wait_ge(setup_v, 3)
            dve.tensor_scalar(tern[:, 1, :], tern[:, 0, :], tsum[:, 3:4], alpha, ALU.is_lt, ALU.mult)\
                .then_inc(setup_v, 1)
            dve.tensor_scalar(tern[:, 2, :], tern[:, 0, :], tsum[:, 2:3], alpha, ALU.is_gt, ALU.mult)\
                .then_inc(setup_v, 1)
            dve.wait_ge(setup_v, 5)
            dve.tensor_tensor(tern[:, 2, :], tern[:, 2, :], tern[:, 1, :], ALU.subtract).then_inc(setup_v, 1)
            dve.tensor_tensor(bias0[:, :], cols[:, COL["L0_attn_bo"]:COL["L0_attn_bo"] + 1],
                              cols[:, COL["L0_ffn_bias"]:COL["L0_ffn_bias"] + 1], ALU.add).then_inc(setup_v, 1)
            dve.tensor_copy(ident16[:, :], ident[:, :]).then_inc(setup_v, 1)
            dve.tensor_copy(mask16[:, :], mask32).then_inc(setup_v, 1)
            dve.tensor_copy(pick16[:, :].rearrange("p (e d) -> p e d", e=E), pick32).then_inc(setup_v, 1)
            dve.tensor_copy(b2[:, :, 0, :], b2_32).then_inc(setup_v, 1)
            dve.wait_ge(setup_v, 11)
            dve.tensor_tensor(b2[:, :, 1, :], b2_32, b2[:, :, 0, :], ALU.subtract).then_inc(setup_v, 1)
            dve.wait_ge(setup_v, 12)

            def split(layer):
                for n, (src, kind) in enumerate(split_from(layer)):
                    made = SPLITS[layer] - len(split_from(layer)) + n + 1
                    dve.wait_ge(hi_made, made)
                    dve.tensor_tensor(experts[layer][:, 1, kind, :], src, experts[layer][:, 0, kind, :], ALU.subtract)\
                        .then_inc(lo_made, 1)
                dve.wait_ge(lo_made, SPLITS[layer])

            def measure(stage, i):
                dve.sem_inc(passed_v, 1)
                for t in range(TILES):
                    dve.bn_stats(stats[:, t, :], x[:, bass.ds(i * TILES + t, 1), :].rearrange("p a d -> p (a d)"))\
                        .then_inc(ln_stats.sem, 1)
                ln_stats.wait(dve, stage, i, 3)
                dve.sem_inc(passed_v, 1)
                for t in range(TILES):
                    dve.bn_aggr(mv4[:, t, :], stats[:, t, :]).then_inc(ln_stats.sem, 1)
                ln_stats.wait(dve, stage, i, 7)
                dve.sem_inc(passed_v, 1)
                dve.tensor_copy(mv[:, bass.ds(i * TILES, TILES), :], mv4).then_inc(ln_stats.sem, 1)

            def normalise(stage, i, dst, slot, k):
                for t in range(TILES):
                    tile = i * TILES + t
                    dve.tensor_scalar(dst(tile, t), x[:, bass.ds(tile, 1), :].rearrange("p a d -> p (a d)"),
                                      mv[:, bass.ds(tile, 1), 0:1].rearrange("p a d -> p (a d)"),
                                      rstd[:, slot, bass.ds(tile, 1)],
                                      ALU.subtract, ALU.mult).then_inc(xn_made.sem, 1)

            def to_xn(tile, t):
                return xn[:, t, :]

            def to_rows(tile, t):
                return xd[:, bass.ds(tile, 1), 0:P].rearrange("p a d -> p (a d)")

            def finish(stage, i):
                y_turned.wait(dve, stage, i, 0)
                dst = x[:, bass.ds(i * TILES, TILES), :]
                dve.tensor_tensor(dst, dst, misc[:, :].rearrange("p (t d) -> p t d", t=TILES), ALU.add)\
                    .then_inc(x_made.sem, 1)

            def along(a, n=ALL, m=E):
                return a.rearrange("p (t o) -> p t o", o=1).broadcast_to([P, n, m])

            def across(a, n=ALL, m=E):
                return a.rearrange("p (o e) -> p o e", o=1).broadcast_to([P, n, m])

            def best(ch, src, onehot, top, first, rank):
                ch.link(dve.tensor_reduce(top, src, AX.X, ALU.max))
                ch.link(dve.tensor_tensor(first, src, along(top), ALU.is_equal))
                ch.link(dve.tensor_tensor(first, first, across(rank_w[:, :]), ALU.mult))
                ch.link(dve.tensor_reduce(rank, first, AX.X, ALU.max))
                ch.link(dve.tensor_tensor(onehot, first, along(rank), ALU.is_equal))

            def router(layer):
                stage = f"R{layer}"
                stage_closed(dve, ORDER[ORDER.index(stage) - 1])
                dve.wait_ge(rstd_made, layer + 1)

                def both_norms(i, first):
                    normalise(stage, i, to_rows, 3 if layer == 2 else 1, 0)
                    if not first:
                        xn_turned.wait(dve, stage, i - 1)
                        dve.sem_inc(passed_v, 1)
                    normalise(stage, i, to_xn, 1, 4)

                both_norms(0, True)
                with dve.Fori(0, NCH - 1) as i:
                    both_norms(i + 1, False)
                lg_full.wait(dve, stage, NCH - 1)
                dve.tensor_tensor(lg[:, 0, :, :], misc[:, 0:ALL * E].rearrange("p (t e) -> p t e", t=ALL),
                                  across(rb[:, layer - 1, :]), ALU.add).then_inc(lg_made.sem, 1)
                lg_made.wait(dve, f"T{layer}", 0)
                xn_made.wait(dve, stage, NCH - 1, 7)
                dve.sem_inc(done["dve"], 1)
                ch = Chain(dve, route, f"T{layer}", 0)
                best(ch, lg[:, 0, :, :], lg[:, 1, :, :], sc[:, 0, :], lg[:, 2, :, :], sc[:, 7, :])
                if layer == 2:
                    ch.last(dve.tensor_tensor(lg[:, 3, :, :], lg[:, 0, :, :], along(sc[:, 0, :]), ALU.subtract))
                    route_exp.wait(dve, "T2", 0)
                    ch.link(dve.tensor_reduce(sc[:, 1, :], lg[:, 4, :, :], AX.X, ALU.add))
                    ch.link(dve.reciprocal(gate_w[:, 0, :], sc[:, 1, :]))
                    chosen = lg[:, 1, :, :]
                else:
                    ch.link(dve.scalar_tensor_tensor(out=lg[:, 3, :, :], in0=lg[:, 1, :, :], scalar=-BIG,
                                                     in1=lg[:, 0, :, :], op0=ALU.mult, op1=ALU.add))
                    best(ch, lg[:, 3, :, :], lg[:, 4, :, :], sc[:, 1, :], lg[:, 2, :, :], sc[:, 8, :])
                    ch.last(dve.tensor_tensor(sc[:, 2, :], sc[:, 1, :], sc[:, 0, :], ALU.subtract))
                    ch.link(dve.tensor_tensor(lg[:, 5, :, :], lg[:, 1, :, :], lg[:, 4, :, :], ALU.add))
                    route_exp.wait(dve, f"T{layer}", 0)
                    ch.link(dve.tensor_scalar(sc[:, 4, :], sc[:, 3, :], 1.0, 2.0 if layer == 1 else 1.0,
                                              ALU.add, ALU.mult))
                    ch.link(dve.reciprocal(gate_w[:, 0, :], sc[:, 4, :]))
                    ch.link(dve.tensor_tensor(gate_w[:, 1, :], gate_w[:, 0, :], sc[:, 3, :], ALU.mult))
                ranks_full.wait(dve, f"T{layer}", 0)
                in_tile = misc[:, 0:ALL * E].rearrange("p (t e) -> p t e", e=E)
                tile_sum = misc[:, ALL * E:2 * ALL * E].rearrange("p (t e) -> p t e", e=E)
                a, b = lg[:, 2, :, :], lg[:, 6, :, :]
                ch.link(dve.tensor_copy(a, tile_sum))
                reach = 1
                while reach < ALL:
                    ch.last(dve.tensor_copy(b[:, 0:reach, :], a[:, 0:reach, :]))
                    ch.link(dve.tensor_tensor(b[:, reach:ALL, :], a[:, reach:ALL, :], a[:, 0:ALL - reach, :], ALU.add))
                    ch.settle()
                    a, b, reach = b, a, 2 * reach
                small = lg[:, 3, :, :].rearrange("p t e -> p (t e)")
                ch.link(dve.tensor_copy(cnt[:, 0, :], a[:, ALL - 1, :]))
                n_mult = TOKENS // SLOTS
                cmp = small[:, 0:E * n_mult].rearrange("p (e j) -> p e j", e=E)
                ch.link(dve.tensor_tensor(cmp, along(cnt[:, 0, :], E, n_mult), across(multiples[:, :], E, n_mult),
                                          ALU.is_gt))
                ch.link(dve.tensor_reduce(cnt[:, 1, :], cmp, AX.X, ALU.add))
                pair = small[:, 0:E * E].rearrange("p (e f) -> p e f", e=E)
                ch.link(dve.tensor_tensor(pair, across(cnt[:, 1, :], E), before_e[:, :, :], ALU.mult))
                ch.link(dve.tensor_reduce(cnt[:, 2, :], pair, AX.X, ALU.add))
                ch.link(dve.tensor_tensor(cnt[:, 3, :], cnt[:, 2, :], cnt[:, 1, :], ALU.add))
                at = lg[:, 7, :, :]
                ch.link(dve.tensor_tensor(at, a, tile_sum, ALU.subtract))
                ch.link(dve.tensor_tensor(at, at, in_tile, ALU.add))
                ch.link(dve.scalar_tensor_tensor(out=at, in0=across(cnt[:, 2, :]), scalar=float(SLOTS), in1=at,
                                                 op0=ALU.mult, op1=ALU.add))
                for j in range(TOP[layer]):
                    ch.link(dve.tensor_tensor(lg[:, 0, :, :], lg[:, (1, 4)[j], :, :], at, ALU.mult))
                    ch.link(dve.tensor_reduce(sc[:, 2, :], lg[:, 0, :, :], AX.X, ALU.add))
                    ch.link(dve.tensor_copy(slot_no[:, j, :], sc[:, 2, :]))
                n_tiles = SLOT_TILES[layer]
                big = lg[:, 2:4, :, :].rearrange("p a t e -> p (a t e)")[:, 0:n_tiles * E]\
                    .rearrange("p (s e) -> p s e", e=E)
                ch.link(dve.tensor_tensor(big, across(cnt[:, 3, :], n_tiles), along(tile_no[:, 0:n_tiles], n_tiles),
                                          ALU.is_le))
                ch.link(dve.tensor_reduce(tile_e[:, 0, 0:n_tiles], big, AX.X, ALU.add))
                ch.link(dve.tensor_scalar(tile_e[:, 0, 0:n_tiles], tile_e[:, 0, 0:n_tiles], float(E - 1), None, ALU.min))
                ch.last(dve.tensor_scalar(tile_e[:, 1, 0:n_tiles], tile_e[:, 0, 0:n_tiles], -1.0, float(E),
                                          ALU.mult, ALU.add))
                ch.last(dve.tensor_copy(tile_ei[0:1, 0:n_tiles], tile_e[0:1, 0, 0:n_tiles]))
                ch.last(dve.tensor_copy(xd[:, :, ID_COL], token_id[:, :]))
                ch.link(dve.tensor_copy(xd[:, :, FIRST_COL], sc[:, 7, :]))
                ch.close()
                dve.sem_inc(done["dve"], 1)
                stage_closed(dve, f"T{layer}")

            def experts_dve(layer):
                stage = f"M{layer}"
                last = SLOT_TILES[layer] - 1

                def rows_low(s, b, first):
                    xh_made.wait(dve, stage, s)
                    src = pt[:, SLOTS * b:SLOTS * (b + 1)]
                    if layer == 2:
                        if not first:
                            up_full.wait(dve, stage, s - 2, 1)
                        src = x32[:, b, :]
                        dve.tensor_copy(xb[:, b, 0, :], src).then_inc(xl_made.sem, 1)
                        xl_made.wait(dve, stage, s, 0)
                    dve.tensor_tensor(xb[:, b, 1, :], src, xb[:, b, 0, :], ALU.subtract).then_inc(xl_made.sem, 1)

                def hidden_low(s, h, hid):
                    hh_made.wait(dve, stage, s, h)
                    dve.tensor_tensor(hb[:, h, 1, :], hid[:, h, :], hb[:, h, 0, :], ALU.subtract)\
                        .then_inc(hl_made.sem, 1)

                def gate(s, h, hid=hids[0]):
                    act_made.wait(dve, stage, s, h)
                    if not (isinstance(s, int) and s == 0):
                        hl_made.wait(dve, stage, s - 1, h)
                    dve.scalar_tensor_tensor(out=hid[:, h, :], in0=hids[1][:, h, :], scalar=1.0, in1=sco[h][:, :],
                                             op0=ALU.add, op1=ALU.mult).then_inc(gated.sem, 1)
                    gated.wait(dve, stage, s, 2 * h)
                    gate_full.wait(dve, stage, s, h)
                    dve.tensor_tensor(hid[:, h, :], hid[:, h, :], mo[h][:, :], ALU.mult).then_inc(gated.sem, 1)

                def place(s, b):
                    f = dest_f[:, 2 * b:2 * b + 2]
                    dve.tensor_scalar(f, xg_b[b][:, :, FIRST_COL], tile_e[:, 1, bass.ds(s, 1)], float(TOKENS),
                                      ALU.not_equal, ALU.mult).then_inc(dest_f_made.sem, 1)
                    dest_f_made.wait(dve, stage, s, 0)
                    dve.tensor_tensor(f, f, xg_b[b][:, :, ID_COL], ALU.add).then_inc(dest_f_made.sem, 1)

                def place_int(s, b, sent):
                    dest_f_made.wait(dve, stage, s, 1)
                    results_sent(dve, layer, b, sent)
                    dve.tensor_copy(dest_no[:, 2 * b:2 * b + 2], dest_f[:, 2 * b:2 * b + 2]).then_inc(dest_made.sem, 1)

                stage_closed(dve, f"A{layer}")
                rows_low(0, 0, True)
                dve.wait_ge(xg_in[0], 16 * (1 + parity_tiles(layer, 0)))
                place(0, 0)

                def step(s, half, b, first):
                    end = isinstance(s, int) and s == last
                    start = isinstance(s, int) and s == 0
                    for h in range(2):
                        if layer == 1:
                            gate(s, h)
                            if h:
                                hidden_low(s, 0, hids[0])
                            elif not start:
                                hidden_low(s - 1, 1, hids[0])
                        else:
                            act_made.wait(dve, stage, s, h)
                            if not start:
                                down_done.wait(dve, stage, s - 1, h)
                            dve.tensor_copy(hb[:, h, 0, :], hids[b][:, h, :]).then_inc(hh_made.sem, 1)
                            hidden_low(s, h, hids[b])
                        if h == 0:
                            if not end:
                                rows_low(s + 1, 1 - b, start)
                            if not start:
                                place_int(s - 1, 1 - b, half - 1 + b)
                                dest_made.wait(dve, stage, s - 1)
                            if not end:
                                place(s + 1, 1 - b)

                slot_tiles(dve, layer, step)
                if layer == 1:
                    hidden_low(last, 1, hids[0])
                place_int(last, 0, last // 2)
                dest_made.wait(dve, stage, last)
                dve.sem_inc(done["dve"], 1)

            def combine(layer):
                stage = f"C{layer}"
                stage_closed(dve, f"M{layer}")
                before_layer = {1: 0, 2: TOP[1], 3: TOP[1] + TOP[2]}[layer] * NCH // 2 * 16

                def step(c, half, b, first):
                    dve.wait_ge(yc_in[b], half * (16 * TOP[layer]) + (16 * TOP[layer] + before_layer))
                    for j in range(TOP[layer]):
                        for t in range(TILES):
                            tile = c * TILES + t
                            xt = x[:, bass.ds(tile, 1), :].rearrange("p a d -> p (a d)")
                            last = dve.scalar_tensor_tensor(out=xt, in0=qT[:, 2 * b + j, t * P:(t + 1) * P],
                                                            scalar=gate_w[:, j, bass.ds(tile, 1)], in1=xt,
                                                            op0=ALU.mult, op1=ALU.add)
                        if j < TOP[layer] - 1:
                            last.then_inc(c_step.sem, 1)
                            c_step.wait(dve, stage, c, 0)
                    last.then_inc(x_made.sem, 1)
                    if layer < 3:
                        x_made.wait(dve, stage, c)
                        measure(stage, c)

                chunk_pairs(dve, step)
                dve.sem_inc(done["dve"], 1)

            def row_max(stage, i, u):
                s_full.wait(dve, stage, i, u)
                if stage == "A1":
                    ins = dve.tensor_reduce(nmax[:, u % 4, :], scos[u % 3][:, :].rearrange("p (q k) -> p q k", q=2),
                                            AX.X, ALU.max, negate=True)
                else:
                    for qt in range(2):
                        ins = dve.tensor_reduce(nmax[:, u % 4, qt:qt + 1], scos[u % 3][:, 128 * qt:128 + 256 * qt],
                                                AX.X, ALU.max, negate=True)
                ins.then_inc(nmax_made.sem, 1)

            def row_scale(stage, i, u):
                exp_made.wait(dve, stage, i, u)
                if u >= 2:
                    prob_turned.wait(dve, stage, i, u - 2)
                dve.reciprocal(rrow[:, u % 4, :], psum_row[:, u % 4, :]).then_inc(rrow_made.sem, 1)
                rrow_made.wait(dve, stage, i, u)
                for qt in range(2):
                    ins = dve.tensor_scalar(scale_d[:, u % 2, qt, :], ident[:, :], rrow[:, u % 4, qt:qt + 1],
                                            None, ALU.mult)
                ins.then_inc(scale_made.sem, 1)

            def attention(layer):
                stage = f"A{layer}"
                scale = SCALE2 if layer == 2 else SCALE3
                after = ahead[layer]

                def take(ins):
                    ins.then_inc(proj_read_v.sem, 1)

                def low(i, n, src, by):
                    proj_read_a.wait(dve, stage, i, proj_read_a.per[stage] - 2 + n // 2)
                    take(dve.scalar_tensor_tensor(out=parts[:, n + 1, :], in0=src[:, :], scalar=by,
                                                  in1=parts[:, n, :], op0=ALU.mult, op1=ALU.subtract))

                def both(a):
                    return a.rearrange("p (b c) -> p b c", b=2)

                def times(i, n, src, full, by):
                    proj_full.wait(dve, stage, i, full)
                    table = (cos_t, sin_t)[n]
                    take(dve.scalar_tensor_tensor(
                        out=both(rot[:, n, :]), in0=both(src[:, :]), scalar=by,
                        in1=table[:, :].rearrange("p (b c) -> p b c", b=1).broadcast_to([P, 2, SEQ]),
                        op0=ALU.mult, op1=ALU.mult))

                def rotated_parts(i, first, dst, low_rows):
                    proj_read_v.wait(dve, stage, i, first - 1)
                    take(dve.tensor_tensor(rotated, rot[:, 0, :], rot[:, 1, :], ALU.add))
                    proj_read_v.wait(dve, stage, i, first)
                    take(dve.tensor_copy(dst, rotated))
                    proj_read_v.wait(dve, stage, i, first + 1)
                    for a, b in low_rows:
                        take(dve.tensor_tensor(dst[a:b, :], rotated[a:b, :], dst[a:b, :], ALU.subtract))

                def keep_values(i, full):
                    proj_full.wait(dve, stage, i, full)
                    take(dve.tensor_copy(after["v"], misc[:, :]))

                def mask(i, g):
                    stacked.wait(dve, stage, i, 2 * g)
                    for j in range(4):
                        ins = dve.tensor_scalar(q_stack[:, g % 2, j, :], q_raw, head_pick[:, j:j + 1], None, ALU.mult)
                    ins.then_inc(masked.sem, 1)

                def prepare(i, s):
                    if s == (19 if layer == 2 else 17):
                        normalise(stage, i, to_xn, 1, 0)
                    if layer == 2:
                        if s == 24:
                            low(i, 0, misc, scale)
                            low(i, 2, acc, 1.0)
                        if s == 26:
                            keep_values(i, 2)
                        if s == 27:
                            mask(i, 0)
                    else:
                        if s == 23:
                            low(i, 0, misc, scale)
                            times(i, 0, acc, 2, scale)
                        if s == 25:
                            times(i, 1, misc, 3, scale)
                            rotated_parts(i, 3, after["q"], ((64, 128),))
                        if s == 26:
                            low(i, 2, acc, 1.0)
                        if s == 27:
                            times(i, 0, misc, 5, 1.0)
                        if s == 28:
                            times(i, 1, acc, 6, 1.0)
                            rotated_parts(i, 9, after["k"], ((32, 64), (96, 128)))
                        if s == 29:
                            keep_values(i, 7)
                        if s == 31:
                            mask(i, 0)

                def advance(i):
                    proj_read_v.wait(dve, stage, i, proj_read_v.per[stage] - 1)
                    if layer == 3:
                        dve.sem_inc(passed_v, 1)
                        dve.tensor_copy(xnT[:, :], after["xT"]).then_inc(moved.sem, 1)
                        dve.tensor_copy(turned_q, after["q"]).then_inc(moved.sem, 1)
                        dve.tensor_copy(turned_k, after["k"]).then_inc(moved.sem, 1)
                    dve.tensor_copy(v2, after["v"].rearrange("p (t d) -> p t d", t=TILES)).then_inc(moved.sem, 1)

                def keep_turned(i, u):
                    prob_turned.wait(dve, stage, i, u)
                    if u >= 2:
                        av_full.wait(dve, stage, i, u - 2)
                    dve.tensor_copy(probT[:, u % 2, 0:384], pts[u % 2][:, 0:384]).then_inc(probT_made.sem, 1)

                def chunk(i, more):
                    for s in range(UNITS + 2):
                        if s < UNITS:
                            row_max(stage, i, s)
                        if s >= 2:
                            keep_turned(i, s - 2)
                        if s % 8 == 2 and s // 8 < 3:
                            mask(i, s // 8 + 1)
                        if more and s < UNITS:
                            prepare(i + 1, s)
                    exp_made.wait(dve, stage, i, UNITS - 1)
                    dve.reciprocal(rsum, sums).then_inc(o_scaled.sem, 1)
                    o_scaled.wait(dve, stage, i, 0)
                    av_full.wait(dve, stage, i, UNITS - 1)
                    dve.tensor_tensor(o_tok.rearrange("p (h c) -> p h c", c=8), ob[:, :].rearrange("p (h c) -> p h c", c=8),
                                      rsum.rearrange("p t (h o) -> p (t h) o", o=1)
                                      .broadcast_to([P, TILES * HEADS, 8]), ALU.mult).then_inc(o_scaled.sem, 1)
                    if more:
                        if layer == 3:
                            sh_up.wait(dve, stage, i, FB - 1)
                        advance(i + 1)
                    acc_full.wait(dve, stage, i)
                    dst = x[:, bass.ds(i * TILES, TILES), :]
                    dve.tensor_tensor(dst, dst, acc[:, :].rearrange("p (t d) -> p t d", t=TILES), ALU.add)\
                        .then_inc(x_made.sem, 1)

                for s in range(AHEAD, UNITS):
                    prepare(0, s)
                advance(0)
                last_chunk_apart(dve, chunk)

            dve.wait_ge(x_in, 16 * NCH)
            with dve.Fori(0, NCH) as i:
                measure("N0", i)
            dve.wait_ge(rstd_made, 1)
            with dve.Fori(0, NCH) as i:
                normalise("L0", i, to_xn, 1, 0)
                proj_read_a.wait(dve, "L0", i, 1)
                dve.tensor_tensor(qT[:, 0, :], oT[:, 0, :], yT, ALU.add).then_inc(proj_read_v.sem, 1)
                proj_full.wait(dve, "L0", i, 3)
                dve.tensor_tensor(oT[:, 0, :], kT[:, 0, :], ob[:, :], ALU.mult).then_inc(proj_read_v.sem, 1)
                finish("L0", i)
                x_made.wait(dve, "L0", i)
                measure("L0", i)
            dve.sem_inc(done["dve"], 1)
            split(1)
            dve.wait_ge(w1_high, 1)
            dve.tensor_tensor(w1[:, 1, :], region[:, :], w1[:, 0, :], ALU.subtract).then_inc(w1_low, 1)

            router(1)
            vb = [sco[0], sco[1], pt, ob]

            def q_low(i, j):
                q_high.wait(dve, "A1", i, j)
                dve.scalar_tensor_tensor(out=q16[:, j % 2, 1, :], in0=misc[:, :], scalar=SCALE1,
                                         in1=q16[:, j % 2, 0, :], op0=ALU.mult, op1=ALU.subtract)\
                    .then_inc(q_made.sem, 1)

            def k_low(i, j):
                k_high.wait(dve, "A1", i, j)
                dve.tensor_tensor(k16[:, j % 2, 1, :], misc[:, :], k16[:, j % 2, 0, :], ALU.subtract)\
                    .then_inc(k_made.sem, 1)

            def values_low(i, n):
                proj_read_a.wait(dve, "A1", i, n)
                c = slice(512 * (n % 2), 512 * (n % 2) + 512)
                dve.tensor_tensor(v16[:, n // 2, 1, c], vb[n % 4][:, :], v16[:, n // 2, 0, c], ALU.subtract)\
                    .then_inc(proj_read_v.sem, 1)

            def prepare(i, s):
                if s == 29:
                    normalise("A1", i, to_xn, 3, 0)
                if s == 32:
                    xT_made.wait(dve, "A1", i)
                    col = COL["L1_attn_norm_scale"]
                    dve.scalar_tensor_tensor(out=x16[:, 1, :], in0=misc[:, :], scalar=cols[:, col:col + 1],
                                             in1=x16[:, 0, :], op0=ALU.mult, op1=ALU.subtract).then_inc(xT_low.sem, 1)
                if s == 35:
                    q_low(i, 0)
                if s == 36:
                    k_low(i, 0)

            def chunk(i, more):
                for s in range(UNITS + 5):
                    if s >= 8 and s % 4 == 0:
                        j = (s - 8) // 4
                        oT_high.wait(dve, "A1", i, j)
                        dve.tensor_tensor(o16[:, j % 2, 1, :], ob[:, :], o16[:, j % 2, 0, :], ALU.subtract)\
                            .then_inc(oT_made.sem, 1)
                    if s < UNITS:
                        if s % 4 == 1 and s // 4 + 1 < 8:
                            q_low(i, s // 4 + 1)
                        if s % 4 == 3 and s // 4 + 1 < 8:
                            k_low(i, s // 4 + 1)
                        row_max("A1", i, s)
                    if 1 <= s <= UNITS:
                        row_scale("A1", i, s - 1)
                    if 3 <= s < UNITS + 3:
                        u = s - 3
                        probT_high.wait(dve, "A1", i, u)
                        dve.tensor_tensor(p16[u % 4][:, 1, :], pts[u % 2][:, :], p16[u % 4][:, 0, :], ALU.subtract)\
                            .then_inc(probT_made.sem, 1)
                    if more:
                        prepare(i + 1, s)
                if more:
                    for n in range(4):
                        values_low(i + 1, n)
                finish("A1", i)
                if more:
                    for n in range(4, 8):
                        values_low(i + 1, n)

            for s in range(AHEAD, UNITS + 5):
                prepare(0, s)
            for n in range(8):
                values_low(0, n)
            last_chunk_apart(dve, chunk)
            x_made.wait(dve, "A1", NCH - 1)
            dve.sem_inc(done["dve"], 1)
            split(2)
            experts_dve(1)
            combine(1)

            router(2)
            attention(2)
            x_made.wait(dve, "A2", NCH - 1)
            dve.sem_inc(done["dve"], 1)
            split(3)
            experts_dve(2)
            combine(2)

            router(3)
            attention(3)
            x_made.wait(dve, "A3", NCH - 1)
            dve.sem_inc(done["dve"], 1)
            experts_dve(3)
            combine(3)


_INS = ["L0_attn_x", "L0_attn_Wq", "L0_attn_bq", "L0_attn_Wk", "L0_attn_bk", "L0_attn_Wv", "L0_attn_bv", "L0_attn_Wo",
        "L0_attn_bo", "L0_ffn_weight", "L0_ffn_alpha", "L0_ffn_bias", "L1_attn_norm_scale", "L1_attn_wq", "L1_attn_wk",
        "L1_attn_wv", "L1_attn_w_out", "L1_attn_b_out", "L1_ffn_gate_w", "L1_ffn_gate_b", "L1_ffn_w1", "L1_ffn_w3",
        "L1_ffn_w2", "L2_attn_w_qkv", "L2_attn_w_out", "L2_ffn_Wr", "L2_ffn_br", "L2_ffn_ln_g", "L2_ffn_ln_b",
        "L2_ffn_W1", "L2_ffn_b1", "L2_ffn_W2", "L2_ffn_b2", "L3_attn_W_kv_down", "L3_attn_W_k_up", "L3_attn_W_v_up",
        "L3_attn_W_q", "L3_attn_W_q_rope", "L3_attn_W_k_rope", "L3_attn_W_o", "L3_ffn_gate_w", "L3_ffn_gate_b",
        "L3_ffn_w1", "L3_ffn_b1", "L3_ffn_w2", "L3_ffn_b2", "L3_ffn_ws1", "L3_ffn_bs1", "L3_ffn_ws2", "L3_ffn_bs2"]
_OUT = (16, 256, 128)


def constants():
    p = np.arange(P)
    f32 = np.float32
    head = (p % GROUP) // 8
    inv_freq = (f32(1.0) / f32(10000.0) ** (np.arange(0, ROPE, 2, dtype=f32) / f32(ROPE))).astype(f32)
    freqs = np.outer(inv_freq, np.arange(SEQ, dtype=f32)).astype(f32)
    sign = np.where(p % ROPE < ROPE // 2, -1.0, 1.0).astype(f32)
    own = (head[:, None] == np.arange(4)[None, :]).astype(f32)
    return {
        "ident": np.eye(P, dtype=f32),
        "causal": np.where(p[None, :] <= p[:, None], 0.0, -1e30).astype(f32),
        "head_sum": (p[:, None] // 8 == p[None, :] // 8).astype(f32),
        "head_pick": own,
        "expert_pick": np.repeat(np.eye(E, dtype=f32)[:, :, None], P, axis=2),
        "rank_w": np.broadcast_to(np.arange(E, 0, -1, dtype=f32), (P, E)).copy(),
        "before": np.triu(np.ones((P, P), f32), 1),
        "before_e": np.broadcast_to(np.tril(np.ones((E, E), f32), -1), (P, E, E)).copy(),
        "multiples": np.broadcast_to(np.arange(0, TOKENS, SLOTS, dtype=f32), (P, TOKENS // SLOTS)).copy(),
        "tile_no": np.broadcast_to(np.arange(MOST, dtype=f32), (P, MOST)).copy(),
        "token_id": (np.arange(ALL, dtype=f32)[None, :] * P + p[:, None]).astype(f32),
        "blank": np.concatenate([np.zeros((P, 4, P)), TRASH + P * np.arange(4)[None, :, None] + p[:, None, None],
                                 np.zeros((P, 4, 1))], 2).astype(f32),
        "cos_t": np.cos(freqs)[p % (ROPE // 2)].astype(f32),
        "sin_t": (np.sin(freqs)[p % (ROPE // 2)] * sign[:, None]).astype(f32),
    }


def kernel(**inputs):
    import numpy as _np
    import concourse.bacc as _bacc
    from concourse import mybir as _mybir
    from concourse.bass_utils import run_bass_kernel_spmd as _run

    nc = _bacc.Bacc("TRN2", target_bir_lowering=False, num_devices=1)
    arrays, aps = {}, {}
    data = {name: _np.ascontiguousarray(inputs[name]) for name in _INS}
    data.update(constants())
    for name, a in data.items():
        arrays[f"in_{name}_dram"] = a
        aps[name] = nc.dram_tensor(f"in_{name}_dram", a.shape, _mybir.dt.from_np(a.dtype), kind="ExternalInput").ap()
    out = nc.dram_tensor("out_0_dram", _OUT, _mybir.dt.float32, kind="ExternalOutput").ap()
    build_program(nc, aps, out)
    r = _run(nc, [arrays], core_ids=[0])
    return r.results[0]["out_0_dram"]
```
